# Optimizing a Trainium2 kernel written in Bass

```python
import numpy as np
import jax
import jax.numpy as jnp

def _softmax(x, axis=-1):
    return jax.nn.softmax(x, axis=axis)

def _gelu(x):
    return jax.nn.gelu(x, approximate=True)

def _silu(x):
    return jax.nn.silu(x)

def _sigmoid(x):
    return jax.nn.sigmoid(x)

def _layernorm(x, axis=-1, eps=1e-05):
    m = jnp.mean(x, axis=axis, keepdims=True)
    v = jnp.var(x, axis=axis, keepdims=True)
    return (x - m) / jnp.sqrt(v + eps)

def _scatter_add(tgt, idx, src, axis=0):
    return tgt.at[idx].add(src)

def _segment_sum(src, seg, n):
    return jax.ops.segment_sum(src, seg, n)
kernel_name = 'mk_audio_tower_d2_tok_audfeat512_r4_96edc5'

def setup_inputs(seed: int=0):
    np.random.seed(seed)
    _w = jnp.asarray

    def _rec_inputs():
        import jax
        import jax.numpy as jnp
        _rk = jax.random.key(seed)
        x = 7.22013e-05 + 1.00017 * jax.random.normal(jax.random.fold_in(_rk, 1), (32, 375, 64), jnp.float32)
        return x
    x = _rec_inputs()

    def _L0_tok_setup():
        import jax, jax.numpy as jnp
        import numpy as np
        EPS = 1e-07
        C_CURV = 1.0
        LAM_HALF = 1.0 / (1.0 + EPS)
        key = jax.random.key(seed)
        k1, k2 = jax.random.split(key)
        B, L, Cin, K, F = (32, 256, 64, 9, 128)
        x = jax.random.normal(k1, (B, L, Cin), dtype=jnp.float32)
        lim = float(np.sqrt(6.0 / (K * Cin + F)))
        kernel = jax.random.uniform(k2, (K, Cin, F), dtype=jnp.float32, minval=-lim, maxval=lim)
        bias = jnp.zeros((F,), dtype=jnp.float32)
        return {'x': x, 'kernel': kernel, 'bias': bias}
    _L0_tok_all = _L0_tok_setup()
    _L0_tok_in = {k: v for k, v in _L0_tok_all.items() if k in ('kernel', 'bias')}
    del _L0_tok_all

    def _L0_attn_setup():
        import jax, jax.numpy as jnp
        import numpy as np

        def _init_linear(key, out_dim, in_dim):
            kw, kb = jax.random.split(key)
            bound = 1.0 / np.sqrt(in_dim)
            W = jax.random.uniform(kw, (out_dim, in_dim), jnp.float32, -bound, bound)
            b = jax.random.uniform(kb, (out_dim,), jnp.float32, -bound, bound)
            return (W, b)
        key = jax.random.key(seed)
        ks = jax.random.split(key, 5)
        B, N, D = (8, 512, 128)
        H, DK = (512, 128)
        x = jax.random.normal(ks[0], (B, N, D), jnp.float32)
        We1, be1 = _init_linear(ks[1], H, D)
        We2, be2 = _init_linear(ks[2], D, H)
        Wk1, bk1 = _init_linear(ks[3], H, D)
        Wk2, bk2 = _init_linear(ks[4], 2 * DK, H)
        return {'x': x, 'We1': We1, 'be1': be1, 'We2': We2, 'be2': be2, 'Wk1': Wk1, 'bk1': bk1, 'Wk2': Wk2, 'bk2': bk2}
    _L0_attn_all = _L0_attn_setup()
    _L0_attn_in = {k: v for k, v in _L0_attn_all.items() if k in ('We1', 'be1', 'We2', 'be2', 'Wk1', 'bk1', 'Wk2', 'bk2')}
    del _L0_attn_all

    def _L0_ffn_setup():
        import jax, jax.numpy as jnp
        import numpy as np
        MICRO_BATCHES = 2
        TOP_K = 2
        D = 128
        E = 8
        B, S = (8, 2048)
        key = jax.random.key(seed)
        ks = jax.random.split(key, 12)
        s = 0.02
        return {'x': jax.random.normal(ks[0], (B, S, D), dtype=jnp.float32), 'ln_g': jnp.ones((D,), jnp.float32), 'ln_b': jnp.zeros((D,), jnp.float32), 'attn_w': jax.random.normal(ks[1], (D, D), jnp.float32) * s, 'attn_b': jnp.zeros((D,), jnp.float32), 'gate_w': jax.random.normal(ks[2], (E, D), jnp.float32) * s, 'fc1_w': jax.random.normal(ks[3], (E, 4 * D, D), jnp.float32) * s, 'fc1_b': jnp.zeros((E, 4 * D), jnp.float32), 'fc2_w': jax.random.normal(ks[4], (E, D, 4 * D), jnp.float32) * s, 'fc2_b': jnp.zeros((E, D), jnp.float32), 'next_w': jax.random.normal(ks[5], (D, D), jnp.float32) * s, 'next_b': jnp.zeros((D,), jnp.float32)}
    _L0_ffn_all = _L0_ffn_setup()
    _L0_ffn_in = {k: v for k, v in _L0_ffn_all.items() if k in ('ln_g', 'ln_b', 'attn_w', 'attn_b', 'gate_w', 'fc1_w', 'fc1_b', 'fc2_w', 'fc2_b', 'next_w', 'next_b')}
    del _L0_ffn_all

    def _L1_attn_setup():
        import jax, jax.numpy as jnp
        import numpy as np
        N_HEADS = 8
        key = jax.random.key(seed)
        ks = jax.random.split(key, 5)
        b, s, d = (2, 1024, 128)
        return {'x': jax.random.normal(ks[0], (b, s, d), dtype=jnp.float32), 'qkv_w': jax.random.normal(ks[1], (3 * d, d), dtype=jnp.float32) * 0.02, 'qkv_b': jax.random.normal(ks[2], (3 * d,), dtype=jnp.float32) * 0.02, 'out_w': jax.random.normal(ks[3], (d, d), dtype=jnp.float32) * 0.02, 'out_b': jax.random.normal(ks[4], (d,), dtype=jnp.float32) * 0.02}
    _L1_attn_all = _L1_attn_setup()
    _L1_attn_in = {k: v for k, v in _L1_attn_all.items() if k in ('qkv_w', 'qkv_b', 'out_w', 'out_b')}
    del _L1_attn_all

    def _L1_ffn_setup():
        import jax, jax.numpy as jnp
        import numpy as np
        B, S, D, H, E = (4, 512, 128, 256, 8)
        key = jax.random.key(seed)
        ks = jax.random.split(key, 4)
        x = jax.random.normal(ks[0], (B, S, D), jnp.float32)
        Wr = jax.random.normal(ks[1], (E, D), jnp.float32) * 0.02
        br = jnp.zeros((E,), jnp.float32)
        W1 = jax.random.normal(ks[2], (E, D, H), jnp.float32) * 0.02
        b1 = jnp.zeros((E, H), jnp.float32)
        W2 = jax.random.normal(ks[3], (E, H, D), jnp.float32) * 0.02
        b2 = jnp.zeros((E, D), jnp.float32)
        return {'x': x, 'Wr': Wr, 'br': br, 'W1': W1, 'b1': b1, 'W2': W2, 'b2': b2}
    _L1_ffn_all = _L1_ffn_setup()
    _L1_ffn_in = {k: v for k, v in _L1_ffn_all.items() if k in ('Wr', 'br', 'W1', 'b1', 'W2', 'b2')}
    del _L1_ffn_all
    return {'x': x, 'L0_tok_kernel': _L0_tok_in['kernel'], 'L0_tok_bias': _L0_tok_in['bias'], 'L0_attn_We1': _L0_attn_in['We1'], 'L0_attn_be1': _L0_attn_in['be1'], 'L0_attn_We2': _L0_attn_in['We2'], 'L0_attn_be2': _L0_attn_in['be2'], 'L0_attn_Wk1': _L0_attn_in['Wk1'], 'L0_attn_bk1': _L0_attn_in['bk1'], 'L0_attn_Wk2': _L0_attn_in['Wk2'], 'L0_attn_bk2': _L0_attn_in['bk2'], 'L0_ffn_ln_g': _L0_ffn_in['ln_g'], 'L0_ffn_ln_b': _L0_ffn_in['ln_b'], 'L0_ffn_attn_w': _L0_ffn_in['attn_w'], 'L0_ffn_attn_b': _L0_ffn_in['attn_b'], 'L0_ffn_gate_w': _L0_ffn_in['gate_w'], 'L0_ffn_fc1_w': _L0_ffn_in['fc1_w'], 'L0_ffn_fc1_b': _L0_ffn_in['fc1_b'], 'L0_ffn_fc2_w': _L0_ffn_in['fc2_w'], 'L0_ffn_fc2_b': _L0_ffn_in['fc2_b'], 'L0_ffn_next_w': _L0_ffn_in['next_w'], 'L0_ffn_next_b': _L0_ffn_in['next_b'], 'L1_attn_qkv_w': _L1_attn_in['qkv_w'], 'L1_attn_qkv_b': _L1_attn_in['qkv_b'], 'L1_attn_out_w': _L1_attn_in['out_w'], 'L1_attn_out_b': _L1_attn_in['out_b'], 'L1_ffn_Wr': _L1_ffn_in['Wr'], 'L1_ffn_br': _L1_ffn_in['br'], 'L1_ffn_W1': _L1_ffn_in['W1'], 'L1_ffn_b1': _L1_ffn_in['b1'], 'L1_ffn_W2': _L1_ffn_in['W2'], 'L1_ffn_b2': _L1_ffn_in['b2']}

def reference(x, L0_tok_kernel, L0_tok_bias, L0_attn_We1, L0_attn_be1, L0_attn_We2, L0_attn_be2, L0_attn_Wk1, L0_attn_bk1, L0_attn_Wk2, L0_attn_bk2, L0_ffn_ln_g, L0_ffn_ln_b, L0_ffn_attn_w, L0_ffn_attn_b, L0_ffn_gate_w, L0_ffn_fc1_w, L0_ffn_fc1_b, L0_ffn_fc2_w, L0_ffn_fc2_b, L0_ffn_next_w, L0_ffn_next_b, L1_attn_qkv_w, L1_attn_qkv_b, L1_attn_out_w, L1_attn_out_b, L1_ffn_Wr, L1_ffn_br, L1_ffn_W1, L1_ffn_b1, L1_ffn_W2, L1_ffn_b2):
    import jax
    import jax.numpy as jnp

    def _L0_tok_ref(x, kernel, bias):
        import jax, jax.numpy as jnp
        import numpy as np
        EPS = 1e-07
        C_CURV = 1.0
        LAM_HALF = 1.0 / (1.0 + EPS)
        B, L, Cin = x.shape
        K, _, F = kernel.shape
        Lout = L - K + 1
        sq = jnp.sum(x * x, axis=-1)
        cs = jnp.concatenate([jnp.zeros((B, 1), x.dtype), jnp.cumsum(sq, axis=1)], axis=1)
        wsq = cs[:, K:] - cs[:, :Lout]
        wnorm = jnp.sqrt(jnp.maximum(wsq, 0.0))
        scale = jnp.where(wnorm < 1.0, 1.0, 1.0 / (wnorm + EPS))[..., None]
        conv = jax.lax.conv_general_dilated(x, kernel, window_strides=(1,), padding='VALID', dimension_numbers=('NWC', 'WIO', 'NWC'))
        v = conv * scale
        v_norm = jnp.maximum(jnp.abs(v), EPS)
        y = jnp.tanh(v_norm * LAM_HALF) * (v / v_norm)
        return jax.nn.relu(y + bias)

    def _L0_attn_ref(x, We1, be1, We2, be2, Wk1, bk1, Wk2, bk2):
        import jax, jax.numpy as jnp
        import numpy as np

        def _init_linear(key, out_dim, in_dim):
            kw, kb = jax.random.split(key)
            bound = 1.0 / np.sqrt(in_dim)
            W = jax.random.uniform(kw, (out_dim, in_dim), jnp.float32, -bound, bound)
            b = jax.random.uniform(kb, (out_dim,), jnp.float32, -bound, bound)
            return (W, b)
        embs = jnp.einsum('bnh,dh->bnd', jax.nn.relu(jnp.einsum('bnd,hd->bnh', x, We1) + be1), We2) + be2
        kq = jnp.einsum('bnh,kh->bnk', jax.nn.relu(jnp.einsum('bnd,hd->bnh', x, Wk1) + bk1), Wk2) + bk2
        dk = kq.shape[-1] // 2
        K, Q = (kq[..., :dk], kq[..., dk:])
        A = jax.nn.softmax(jnp.einsum('bnk,bmk->bnm', Q, K), axis=-1)
        return jnp.einsum('bnm,bmd->bnd', A, embs)

    def _L0_ffn_ref(x, ln_g, ln_b, attn_w, attn_b, gate_w, fc1_w, fc1_b, fc2_w, fc2_b, next_w, next_b):
        import jax, jax.numpy as jnp
        import numpy as np
        MICRO_BATCHES = 2
        TOP_K = 2
        D = 128
        E = 8
        B, S = (8, 2048)
        b, s, d = x.shape
        xf = x.reshape(b * s, d)
        mu = jnp.mean(xf, axis=-1, keepdims=True)
        var = jnp.var(xf, axis=-1, keepdims=True)
        normed = (xf - mu) / jnp.sqrt(var + 1e-05) * ln_g + ln_b
        x_attn = normed @ attn_w.T + attn_b + xf
        logits = x_attn @ gate_w.T
        _scores, _indices = jax.lax.top_k(logits, TOP_K)
        e = fc1_w.shape[0]
        t = b * s // (MICRO_BATCHES * e)
        tok = x_attn.reshape(MICRO_BATCHES, e, t, d)
        h = jnp.einsum('meti,ehi->meth', tok, fc1_w) + fc1_b[None, :, None, :]
        h = jax.nn.gelu(h, approximate=False)
        y = jnp.einsum('meth,edh->metd', h, fc2_w) + fc2_b[None, :, None, :]
        yf = y.reshape(b * s, d)
        out = jax.nn.gelu(yf @ next_w.T + next_b, approximate=False)
        return out.reshape(b, s, d)

    def _L1_attn_ref(x, qkv_w, qkv_b, out_w, out_b):
        import jax, jax.numpy as jnp
        import numpy as np
        N_HEADS = 8
        b, s, d = x.shape
        h = N_HEADS
        c = d // h
        factor = 1.0 / jnp.sqrt(jnp.asarray(c, dtype=x.dtype))
        qkv = x @ qkv_w.T + qkv_b
        qkv = qkv.reshape(b, s, h, 3, c)
        q, k, v = (qkv[..., 0, :], qkv[..., 1, :], qkv[..., 2, :])
        scores = jnp.einsum('bshc,bthc->bhst', q, k) * factor
        attn = jax.nn.softmax(scores, axis=-1)
        ctx = jnp.einsum('bhst,bthc->bshc', attn, v).reshape(b, s, d)
        return ctx @ out_w.T + out_b

    def _L1_ffn_ref(x, Wr, br, W1, b1, W2, b2):
        import jax, jax.numpy as jnp
        import numpy as np
        B, S, D, H, E = (4, 512, 128, 256, 8)
        b, s, d = x.shape
        n = b * s
        e = Wr.shape[0]
        xf = x.reshape(n, d)
        logits = xf @ Wr.T + br
        probs = jax.nn.softmax(logits, axis=-1)
        top2_prob, top2_idx = jax.lax.top_k(probs, 2)
        comb = jnp.zeros((n, e), x.dtype).at[jnp.arange(n)[:, None], top2_idx].add(top2_prob)
        h = jax.nn.gelu(jnp.einsum('nd,edh->enh', xf, W1) + b1[:, None, :], approximate=False)
        o = jnp.einsum('enh,ehd->end', h, W2) + b2[:, None, :]
        y = jnp.einsum('ne,end->nd', comb, o)
        return y.reshape(b, s, d)
    h = _L0_tok_ref(x, L0_tok_kernel, L0_tok_bias)
    h = h + _L0_attn_ref(_layernorm(h, axis=-1), L0_attn_We1, L0_attn_be1, L0_attn_We2, L0_attn_be2, L0_attn_Wk1, L0_attn_bk1, L0_attn_Wk2, L0_attn_bk2)
    h = h + _L0_ffn_ref(_layernorm(h, axis=-1), L0_ffn_ln_g, L0_ffn_ln_b, L0_ffn_attn_w, L0_ffn_attn_b, L0_ffn_gate_w, L0_ffn_fc1_w, L0_ffn_fc1_b, L0_ffn_fc2_w, L0_ffn_fc2_b, L0_ffn_next_w, L0_ffn_next_b)
    h = h + _L1_attn_ref(_layernorm(h, axis=-1), L1_attn_qkv_w, L1_attn_qkv_b, L1_attn_out_w, L1_attn_out_b)
    h = h + _L1_ffn_ref(_layernorm(h, axis=-1), L1_ffn_Wr, L1_ffn_br, L1_ffn_W1, L1_ffn_b1, L1_ffn_W2, L1_ffn_b2)
    return h

_drawn_inputs = setup_inputs


def setup_inputs(seed=0):
    import zlib

    import numpy as np

    out = dict(_drawn_inputs(seed))
    spreads = {'L0_tok_bias': (0.0, 0.1),
     'L0_ffn_ln_g': (1.0, 0.6),
     'L0_ffn_ln_b': (0.0, 0.8),
     'L0_ffn_attn_b': (0.0, 2.0),
     'L0_ffn_fc1_b': (0.0, 0.608),
     'L0_ffn_fc2_b': (0.0, 0.1),
     'L0_ffn_next_b': (0.0, 0.1),
     'L1_ffn_br': (0.0, 0.8),
     'L1_ffn_b1': (0.0, 0.427),
     'L1_ffn_b2': (0.0, 0.1)}
    factors = {'L0_attn_Wk1': 3.535,
     'L0_attn_bk1': 8.0,
     'L0_attn_Wk2': 3.327,
     'L0_attn_bk2': 8.0,
     'L0_ffn_attn_w': 8.0,
     'L1_attn_qkv_b': 2.891}
    for name, (base, spread) in spreads.items():
        noise = np.random.default_rng([zlib.crc32(name.encode()), seed]).standard_normal(out[name].shape)
        drawn = base * np.exp(spread * noise) if base else spread * noise
        out[name] = jnp.asarray(drawn.astype(out[name].dtype))
    for name, factor in factors.items():
        out[name] = (out[name] * factor).astype(out[name].dtype)
    return out
```

```python
from contextlib import ExitStack

import numpy as np

import concourse.bass as bass
from concourse import mybir

F32 = mybir.dt.float32
F32R = mybir.dt.float32r
I32 = mybir.dt.int32
ALU = mybir.AluOpType
ACT = mybir.ActivationFunctionType
AX = mybir.AxisListType

NB, L_IN, CIN = 32, 375, 64
TAPS = 9
L = L_IN - TAPS + 1
D = 128
CH, TP = 3, 124
NT = CH * TP
TLAST = L - 2 * TP
XW = NT + TAPS + 1
XPAD = XW + 2
NPAIR = (TAPS + 1) // 2
NH, HD = 8, 16
E0, H0 = 8, 512
E1, H1 = 8, 256
EPS_LN = 1e-5
EPS_TOK = 1e-7
LAM_HALF = 1.0 / (1.0 + 1e-7)
FACTOR = HD ** -0.5

WEIGHTS = [("conv", NPAIR * D), ("k2", 4 * 2 * D), ("e2", 4 * D), ("attn", D), ("next", D), ("v", D),
           ("out", D), ("router", D), ("b2", D), ("w2", E1 * 2 * D), ("ident", D), ("ones", D)]
SPLIT = [("k1", 512), ("e1", 512), ("qk", 8 * D), ("w1", E1 * H1)]
COLS = [("bk1", 4), ("be1", 4), ("bk2", 2), ("ln_g", 1), ("ln_b", 1), ("attn_b", 1), ("qkb", 8), ("b1", 16),
        ("qneg", 1), ("kneg", 1)]
ROWS = [("tok_b", D), ("be2", D), ("next_b", D), ("vb", D), ("out_b", D), ("br", E1), ("before", E1 * E1)]
FFW = H0 + H0 + 4 + 1


def offsets(parts):
    at, n = {}, 0
    for name, width in parts:
        at[name] = (n, n + width)
        n += width
    return at, n


W_AT, W_N = offsets(WEIGHTS)
S_AT, S_N = offsets(SPLIT)
C_AT, C_N = offsets(COLS)
R_AT, R_N = offsets(ROWS)

WEAVE = "ABABABABABABABABABABB"


class Signal:

    def __init__(self, sem, per):
        self.sem, self.per = sem, per

    def at(self, b, count):
        return b * self.per + count

    def through(self, b):
        return b * self.per + self.per

    def before(self, b):
        return b * self.per


def later(b):
    return not (isinstance(b, int) and b == 0)


def weave(a, b):
    streams = {"A": a, "B": b}
    for which in WEAVE:
        if streams[which] is not None:
            next(streams[which], None)


def tower_kernel(nc, x, weights, split_w, cols, rows, ffw, out):
    with ExitStack() as ctx:
        def sb(name, shape, dt=F32):
            return ctx.enter_context(nc.sbuf_tensor(name, shape, dt))

        def signal(name, per):
            return Signal(ctx.enter_context(nc.semaphore(name)), per)

        W = sb("W", [128, W_N])
        WH = sb("WH", [128, S_N], F32R)
        WL = sb("WL", [128, S_N], F32R)
        C = sb("C", [128, C_N])
        ROW = sb("ROW", [128, R_N])
        GATE = sb("GATE", [128, 16])
        MAGIC = sb("MAGIC", [128, 3], I32)

        def w(name, i=0, width=D):
            lo = W_AT[name][0] + i * width
            return W[:, lo:lo + width]

        def ws(name, i):
            lo = S_AT[name][0] + i * D
            return WH[:, lo:lo + D], WL[:, lo:lo + D]

        def col(name, i=0):
            return C[:, C_AT[name][0] + i:C_AT[name][0] + i + 1]

        def row(name):
            return ROW[0:TP, R_AT[name][0]:R_AT[name][1]]

        def row3(name):
            return row(name).unsqueeze(1).to_broadcast([TP, CH, R_AT[name][1] - R_AT[name][0]])

        ident = w("ident")
        identT = ident[0:TP, 0:TP]

        XX = sb("XX", [128, XW])
        SQ = sb("SQ", [128, XW])
        S4 = sb("S4", [128, XW])
        S8 = sb("S8", [128, XW])
        FW = sb("FW", [128, FFW])
        F1H = sb("F1H", [128, H0], F32R)
        F1L = sb("F1L", [128, H0], F32R)
        smA = sb("smA", [TP, 16, CH])
        stA = sb("stA", [TP, CH, 6])
        mvA = sb("mvA", [TP, CH, 2])
        TOK = sb("TOK", [TP, CH, D])
        HA = sb("HA", [TP, CH, D])
        NA = sb("NA", [TP, CH, D])
        NA2 = sb("NA2", [TP, CH, D])
        XHa = sb("XHa", [128, NT], F32R)
        XLa = sb("XLa", [128, NT], F32R)
        K1 = sb("K1", [128, 4, NT])
        E1t = sb("E1t", [128, 4, NT])
        KQH = sb("KQH", [128, 2, NT], F32R)
        KQL = sb("KQL", [128, 2, NT], F32R)
        EMB = sb("EMB", [TP, CH, D])
        EX = sb("EX", [TP, CH, NT])
        EXT = E1t[0:TP, 0:CH, :]
        XF = sb("XF", [128, NT])
        NTt = sb("NTt", [128, NT])
        XA = sb("XA", [128, NT])
        G0 = K1
        Y0 = sb("Y0", [128, NT])
        NX = sb("NX", [TP, CH, D])
        NG = sb("NG", [TP, CH, D])
        HN = sb("HN", [TP, CH, D])

        smB = sb("smB", [TP, 16, CH])
        stB = sb("stB", [TP, CH, 6])
        mvB = sb("mvB", [TP, CH, 2])
        NBt = sb("NBt", [TP, CH, D])
        XFb = sb("XFb", [128, NT])
        XHb = sb("XHb", [128, NT], F32R)
        XLb = sb("XLb", [128, NT], F32R)
        QKF = sb("QKF", [128, 2, NT])
        QKR = sb("QKR", [128, 2, NT], F32R)
        Q = sb("Q", [128, 4, NT], F32R)
        Q2 = sb("Q2", [128, 4, NT], F32R)
        KZ = sb("KZ", [128, NH, NT], F32R)
        V = sb("V", [TP, CH, NH, 32])
        MX = sb("MX", [TP, NH, CH])
        M = sb("M", [TP, CH, NH, 64])
        ET = sb("ET", [128, NH, CH, NT])
        WS = ET[:, :, :, :].rearrange("p h c t -> p (h c t)")[:, 0:S_N]
        CT = sb("CT", [128, 2, NT])
        RD = sb("RD", [TP, CH, NH])
        CN = sb("CN", [TP, CH, D])
        spare = ET[:, :, :, :].rearrange("p h c t -> p (h c t)")
        G1 = spare[:, 0:4 * NT].rearrange("p (j t) -> p j t", j=4)
        CNT = spare[:, 4 * NT:5 * NT]
        CBT = spare[:, 5 * NT:6 * NT]
        HB = sb("HB", [TP, CH, D])
        LG = sb("LG", [TP, CH, E1])
        PRB = sb("PRB", [TP, CH, E1])
        BEAT = sb("BEAT", [TP, CH, E1, E1])
        TIE = sb("TIE", [TP, CH, E1, E1])
        CNTB = sb("CNTB", [TP, CH, E1])
        CB = sb("CB", [TP, CH, D])

        PA = ctx.enter_context(nc.psum_tensor("PA", [128, 4, 512], F32))
        PB = ctx.enter_context(nc.psum_tensor("PB", [128, 4, 512], F32))

        def tm(bank, P):
            return P[0:TP, bank, 0:CH * D].rearrange("p (c d) -> p c d", c=CH)

        def chunk(tile, c, n=TP):
            return tile[:, c * TP:c * TP + n]

        loaded = signal("loaded", 80)
        weights_split = signal("weights_split", 1)
        zeros_set = signal("zeros_set", 1)
        x_loaded = signal("x_loaded", 32)
        ffw_loaded = signal("ffw_loaded", 16)
        window_sums = signal("window_sums", 1)
        poolA = signal("poolA", 4)
        wsq_done = signal("wsq_done", 1)
        conv_done = signal("conv_done", 1)
        tok_scale = signal("tok_scale", 1)
        tanh_done = signal("tanh_done", 1)
        dveA = signal("dveA", 74)
        n1_ready = signal("n1_ready", 1)
        n1T_done = signal("n1T_done", 1)
        xa_hi = signal("xa_hi", 1)
        xa_lo = signal("xa_lo", 1)
        k1_mm = signal("k1_mm", 4)
        e1_mm = signal("e1_mm", 4)
        k1_out = signal("k1_out", 4)
        e1_out = signal("e1_out", 4)
        kq_mm = signal("kq_mm", 2)
        kq_hi = signal("kq_hi", 2)
        kq_lo = signal("kq_lo", 2)
        emb_mm = signal("emb_mm", 1)
        emb_out = signal("emb_out", 1)
        s0_mm = signal("s0_mm", 1)
        max0 = signal("max0", 1)
        exp0 = signal("exp0", 3)
        exT_mm = signal("exT_mm", 3)
        exT_out = signal("exT_out", 3)
        av0_mm = signal("av0_mm", 1)
        n2_ready = signal("n2_ready", 1)
        n2T_done = signal("n2T_done", 2)
        xf_out = signal("xf_out", 1)
        nt_out = signal("nt_out", 1)
        at_mm = signal("at_mm", 1)
        xa_out = signal("xa_out", 2)
        f1_split = signal("f1_split", 1)
        fc1_mm = signal("fc1_mm", 4)
        gelu0 = signal("gelu0", 4)
        fc2_mm = signal("fc2_mm", 1)
        y0_out = signal("y0_out", 1)
        next_mm = signal("next_mm", 1)
        next_in = signal("next_in", 1)
        gelu_n = signal("gelu_n", 1)
        hn_ready = signal("hn_ready", 1)
        dveB = signal("dveB", 48)
        n3_ready = signal("n3_ready", 2)
        n3T_mm = signal("n3T_mm", 2)
        xb_hi = signal("xb_hi", 2)
        xb_lo = signal("xb_lo", 2)
        qk_mm = signal("qk_mm", 8)
        qk_full = signal("qk_full", 8)
        qk_round = signal("qk_round", 8)
        qk_out = signal("qk_out", 4)
        v_mm = signal("v_mm", 1)
        v_out = signal("v_out", 1)
        s1_mm = signal("s1_mm", 12)
        s1_max = signal("s1_max", 12)
        m_ready = signal("m_ready", 1)
        mT_mm = signal("mT_mm", 4)
        q2_out = signal("q2_out", 4)
        st_mm = signal("st_mm", 16)
        exp1 = signal("exp1", 16)
        av1_mm = signal("av1_mm", 2)
        ct_out = signal("ct_out", 2)
        ctT_mm = signal("ctT_mm", 2)
        cn_ready = signal("cn_ready", 1)
        cnT_mm = signal("cnT_mm", 1)
        cnT_out = signal("cnT_out", 1)
        out_mm = signal("out_mm", 1)
        hb_ready = signal("hb_ready", 1)
        rt_mm = signal("rt_mm", 1)
        rt_in = signal("rt_in", 1)
        rt_exp = signal("rt_exp", 1)
        cb_ready = signal("cb_ready", 1)
        cbT_mm = signal("cbT_mm", 1)
        cbT_out = signal("cbT_out", 1)
        b2_mm = signal("b2_mm", 1)
        w1_mm = signal("w1_mm", 16)
        gelu1 = signal("gelu1", 16)
        w2_mm = signal("w2_mm", 8)
        w2_out = signal("w2_out", 9)
        stored = signal("stored", 32)

        class Chain:

            def __init__(self, eng, sig, b):
                self.eng, self.sig, self.b, self.n = eng, sig, b, 0

            def __call__(self, ins):
                self.n += 1
                ins.then_inc(self.sig.sem, 1)
                self.eng.wait_ge(self.sig.sem, self.b * self.sig.per + self.n)

            def end(self):
                assert self.n == self.sig.per, (self.n, self.sig.per)

        def run_streams(eng, stream_a, stream_b):
            weave(stream_a(eng, 0), None)
            with eng.Fori(1, NB) as b:
                weave(stream_a(eng, b), stream_b(eng, b - 1))
            weave(None, stream_b(eng, NB - 1))

        block = ctx.enter_context(nc.Block())

        @block.sync
        def _(sp):
            sp.dma_start(W[:, :], weights).then_inc(loaded.sem, 16)
            sp.dma_start(WS, split_w).then_inc(loaded.sem, 16)
            sp.dma_start(C[:, :], cols).then_inc(loaded.sem, 16)
            sp.dma_start(ROW[:, :], rows).then_inc(loaded.sem, 16)

            def load_x(b):
                if later(b):
                    sp.wait_ge(conv_done.sem, conv_done.before(b))
                    sp.wait_ge(window_sums.sem, window_sums.before(b))
                sp.dma_start(XX[0:CIN, :], x[b, :, 0:XW]).then_inc(x_loaded.sem, 16)
                sp.dma_start(XX[CIN:128, :], x[b, :, 1:XW + 1]).then_inc(x_loaded.sem, 16)

            def load_ffw(b):
                if later(b):
                    sp.wait_ge(y0_out.sem, y0_out.before(b))
                    sp.wait_ge(f1_split.sem, f1_split.before(b))
                sp.dma_start(FW[:, :], ffw[(b // 2) % E0]).then_inc(ffw_loaded.sem, 16)

            def store(b):
                sp.wait_ge(w2_out.sem, w2_out.through(b))
                sp.dma_start(out[b, 0:2 * TP, :].rearrange("(c p) d -> p c d", c=2),
                             HB[:, 0:2, :]).then_inc(stored.sem, 16)
                sp.dma_start(out[b, 2 * TP:L, :], HB[0:TLAST, 2, :]).then_inc(stored.sem, 16)

            load_x(0)
            load_ffw(0)
            with sp.Fori(1, NB) as b:
                load_x(b)
                load_ffw(b)
                store(b - 1)
            store(NB - 1)
            sp.wait_ge(stored.sem, NB * stored.per)

        @block.gpsimd
        def _(g):
            def gate(g, i):
                g.tensor_tensor(GATE[:, i:i + 1], GATE[:, 15:16], GATE[:, 15:16], ALU.add)

            def pool_a(g, b):
                link = Chain(g, poolA, b)
                g.wait_ge(x_loaded.sem, x_loaded.through(b))
                if later(b):
                    g.wait_ge(wsq_done.sem, wsq_done.before(b))
                link(g.tensor_tensor(SQ[:, :], XX[:, :], XX[:, :], ALU.mult))
                link(g.tensor_tensor(S4[:, 0:NT + 4], SQ[:, 0:NT + 4], SQ[:, 2:NT + 6], ALU.add))
                link(g.tensor_tensor(S8[:, 0:NT], S4[:, 0:NT], S4[:, 4:NT + 4], ALU.add))
                g.tensor_tensor(S8[0:CIN, 0:NT], S8[0:CIN, 0:NT], SQ[0:CIN, 8:NT + 8],
                                ALU.add).then_inc(window_sums.sem, 1)
                g.wait_ge(ffw_loaded.sem, ffw_loaded.through(b))
                if later(b):
                    g.wait_ge(fc1_mm.sem, fc1_mm.before(b))
                gate(g, 8)
                link(g.tensor_scalar(F1H[:, :], FW[:, 0:H0], 1.0, None, ALU.mult))
                g.tensor_tensor(F1L[:, :], FW[:, 0:H0], F1H[:, :], ALU.subtract).then_inc(f1_split.sem, 1)
                yield

            def pool_b(g, b):
                for p in range(4):
                    for i in range(2):
                        g.wait_ge(qk_full.sem, qk_full.at(b, 2 * p + i + 1))
                        if p > 0:
                            g.wait_ge(qk_out.sem, qk_out.at(b, p))
                        else:
                            if later(b):
                                g.wait_ge(qk_out.sem, qk_out.before(b))
                        gate(g, 2 * p + i)
                        g.tensor_scalar(QKR[:, i, :], QKF[:, i, :], 1.0, None,
                                        ALU.mult).then_inc(qk_round.sem, 1)
                yield

            g.memset(KZ[:, :, :].bitcast(F32), 0.0)
            g.memset(V[:, :, :, HD:32], 0.0)
            g.memset(M[:, :, :, :], 0.0)
            g.memset(CB[:, :, :], 0.0)
            g.memset(GATE[:, :], 0.0)
            g.memset(MAGIC[:, :], 0x5F3759DF).then_inc(zeros_set.sem, 1)
            g.wait_ge(zeros_set.sem, 1)
            g.memset(V[:, :, :, HD:HD + 1], 1.0).then_inc(zeros_set.sem, 1)
            run_streams(g, pool_a, pool_b)

        @block.tensor
        def _(pe):
            def mm3(pe, o, wt, xt, first=True, last=True):
                pe.matmul(o, wt[0], xt[0], start=first, stop=False)
                pe.matmul(o, wt[0], xt[1], start=False, stop=False)
                return pe.matmul(o, wt[1], xt[0], start=False, stop=last)

            def pe_a(pe, b):
                if isinstance(b, int):
                    pe.wait_ge(loaded.sem, 64)
                    pe.wait_ge(weights_split.sem, 2)
                pe.wait_ge(window_sums.sem, window_sums.through(b))
                if later(b):
                    pe.wait_ge(next_in.sem, next_in.before(b))
                    pe.wait_ge(gelu0.sem, gelu0.before(b))
                for c in range(CH):
                    mm = pe.matmul(tm(0, PA)[:, c, :], chunk(S8, c), w("ones"), start=True, stop=True)
                mm.then_inc(wsq_done.sem, 1)
                pe.wait_ge(x_loaded.sem, x_loaded.through(b))
                for c in range(CH):
                    for j in range(NPAIR):
                        mm = pe.matmul(tm(1, PA)[:, c, :], XX[:, c * TP + 2 * j:c * TP + 2 * j + TP], w("conv", j),
                                       start=(j == 0), stop=(j == NPAIR - 1))
                mm.then_inc(conv_done.sem, 1)
                yield
                pe.wait_ge(n1_ready.sem, n1_ready.through(b))
                if later(b):
                    pe.wait_ge(xa_out.sem, xa_out.before(b))
                for c in range(CH):
                    mm = pe.transpose(chunk(PA[:, 2, :], c), NA[:, c, :], identT)
                mm.then_inc(n1T_done.sem, 1)
                yield
                pe.wait_ge(xa_hi.sem, xa_hi.through(b))
                pe.wait_ge(xa_lo.sem, xa_lo.through(b))
                pe.wait_ge(tanh_done.sem, tanh_done.through(b))
                if later(b):
                    pe.wait_ge(y0_out.sem, y0_out.before(b))
                for j in range(4):
                    if j >= 2:
                        pe.wait_ge(k1_out.sem, k1_out.at(b, j - 1))
                    mm3(pe, PA[:, j % 2, 0:NT], ws("k1", j), (XHa[:, :], XLa[:, :])).then_inc(k1_mm.sem, 1)
                    if j >= 2:
                        pe.wait_ge(e1_out.sem, e1_out.at(b, j - 1))
                    mm3(pe, PA[:, 3 - j % 2, 0:NT], ws("e1", j), (XHa[:, :], XLa[:, :])).then_inc(e1_mm.sem, 1)
                yield
                pe.wait_ge(k1_out.sem, k1_out.through(b))
                for i in range(2):
                    for j in range(4):
                        mm = pe.matmul(PA[:, i, 0:NT], w("k2", 2 * j + i), K1[:, j, :], start=(j == 0), stop=(j == 3))
                    mm.then_inc(kq_mm.sem, 1)
                pe.wait_ge(e1_out.sem, e1_out.through(b))
                for c in range(CH):
                    for j in range(4):
                        mm = pe.matmul(tm(3, PA)[:, c, :], chunk(E1t[:, j, :], c), w("e2", j),
                                       start=(j == 0), stop=(j == 3))
                mm.then_inc(emb_mm.sem, 1)
                yield
                pe.wait_ge(kq_hi.sem, kq_hi.through(b))
                pe.wait_ge(kq_lo.sem, kq_lo.through(b))
                for c in range(CH):
                    mm = mm3(pe, PA[0:TP, c, 0:NT], (chunk(KQH[:, 1, :], c), chunk(KQL[:, 1, :], c)),
                             (KQH[:, 0, :], KQL[:, 0, :]))
                mm.then_inc(s0_mm.sem, 1)
                yield
                pe.wait_ge(exp0.sem, exp0.through(b))
                for k in range(CH):
                    n = TP if k < CH - 1 else TLAST
                    for c in range(CH):
                        mm = pe.transpose(chunk(PA[0:n, k, :], c), EX[:, c, k * TP:k * TP + n], identT)
                    mm.then_inc(exT_mm.sem, 1)
                pe.wait_ge(exT_out.sem, exT_out.through(b))
                pe.wait_ge(emb_out.sem, emb_out.through(b))
                for c in range(CH):
                    for k in range(CH):
                        n = TP if k < CH - 1 else TLAST
                        mm = pe.matmul(tm(3, PA)[:, c, :], chunk(EXT[0:n, k, :], c), EMB[0:n, k, :],
                                       start=(k == 0), stop=(k == CH - 1))
                mm.then_inc(av0_mm.sem, 1)
                yield
                pe.wait_ge(n2_ready.sem, n2_ready.through(b))
                for i, t in enumerate((NA, NA2)):
                    for c in range(CH):
                        mm = pe.transpose(chunk(PA[:, i, :], c), t[:, c, :], identT)
                    mm.then_inc(n2T_done.sem, 1)
                pe.wait_ge(nt_out.sem, nt_out.through(b))
                pe.matmul(PA[:, 2, 0:NT], w("attn"), NTt[:, :], start=True, stop=True).then_inc(at_mm.sem, 1)
                yield
                pe.wait_ge(xa_out.sem, xa_out.through(b))
                pe.wait_ge(f1_split.sem, f1_split.through(b))
                for j in range(4):
                    mm3(pe, PA[:, (3 + j) % 4, 0:NT], (F1H[:, j * D:(j + 1) * D], F1L[:, j * D:(j + 1) * D]),
                        (XHa[:, :], XLa[:, :])).then_inc(fc1_mm.sem, 1)
                yield
                for j in range(4):
                    pe.wait_ge(gelu0.sem, gelu0.at(b, j + 1))
                    mm = pe.matmul(PA[:, 3, 0:NT], FW[:, H0 + j * D:H0 + (j + 1) * D], G0[:, j, :],
                                   start=(j == 0), stop=(j == 3))
                mm.then_inc(fc2_mm.sem, 1)
                yield
                pe.wait_ge(y0_out.sem, y0_out.through(b))
                for c in range(CH):
                    mm = pe.matmul(tm(0, PA)[:, c, :], chunk(Y0, c), w("next"), start=True, stop=True)
                mm.then_inc(next_mm.sem, 1)
                yield

            def pe_b(pe, b):
                pe.wait_ge(n3_ready.sem, n3_ready.at(b, 1))
                if later(b):
                    pe.wait_ge(gelu1.sem, gelu1.before(b))
                for c in range(CH):
                    mm = pe.transpose(chunk(PB[:, 0, :], c), NBt[:, c, :], identT)
                mm.then_inc(n3T_mm.sem, 1)
                yield
                pe.wait_ge(xb_hi.sem, xb_hi.at(b, 1))
                pe.wait_ge(xb_lo.sem, xb_lo.at(b, 1))
                if later(b):
                    pe.wait_ge(w2_out.sem, w2_out.before(b))
                for c in range(CH):
                    mm = pe.matmul(tm(0, PB)[:, c, :], chunk(XFb, c), w("v"), start=True, stop=True)
                mm.then_inc(v_mm.sem, 1)
                for i in range(8):
                    if i >= 3:
                        pe.wait_ge(qk_full.sem, qk_full.at(b, i - 2))
                    mm3(pe, PB[:, 1 + i % 3, 0:NT], ws("qk", i), (XHb[:, :], XLb[:, :])).then_inc(qk_mm.sem, 1)
                yield
                pe.wait_ge(v_out.sem, v_out.through(b))
                pe.wait_ge(qk_full.sem, qk_full.through(b))
                for half in range(2):
                    for s in range(6 * half, 6 * half + 6):
                        if s >= 2:
                            pe.wait_ge(s1_max.sem, s1_max.at(b, s - 1))
                        for u in (2 * s, 2 * s + 1):
                            h, c = divmod(u, CH)
                            if c == 0 and h % 2 == 0:
                                pe.wait_ge(qk_out.sem, qk_out.at(b, h // 2 + 1))
                            mm = pe.matmul(PB[0:TP, 2 * (s % 2) + u % 2, 0:NT], chunk(Q[:, h // 2, :], c), KZ[:, h, :],
                                           start=True, stop=True)
                        mm.then_inc(s1_mm.sem, 1)
                    yield
                pe.wait_ge(m_ready.sem, m_ready.through(b))
                for p in range(4):
                    for c in range(CH):
                        mm = pe.transpose(chunk(PB[:, p, :], c), M[:, c, 2 * p:2 * p + 2, :].rearrange("p h d -> p (h d)"),
                                          identT)
                    mm.then_inc(mT_mm.sem, 1)
                for g in range(2):
                    for h in range(4 * g, 4 * g + 4):
                        for k in range(CH):
                            if k != 1:
                                if h == 0:
                                    pe.wait_ge(q2_out.sem, q2_out.at(b, 4 if k else 2))
                                else:
                                    pe.wait_ge(exp1.sem, exp1.at(b, 2 * h - 1 if k == 0 else 2 * h))
                            if h == 0 and k == 0:
                                pe.wait_ge(q2_out.sem, q2_out.through(b))
                            n = TP if k < CH - 1 else TLAST
                            mm = pe.matmul(PB[0:n, k, 0:NT], chunk(KZ[:, h, :], k, n), Q2[:, h // 2, :],
                                           start=True, stop=True)
                            if k > 0:
                                mm.then_inc(st_mm.sem, 1)
                    yield
                    pe.wait_ge(exp1.sem, exp1.at(b, 8 * g + 8))
                    if g == 1:
                        pe.wait_ge(ct_out.sem, ct_out.at(b, 1))
                    for k in range(CH):
                        n = TP if k < CH - 1 else TLAST
                        for j in range(4):
                            mm = pe.matmul(PB[32 * j:32 * j + 32, 3, 0:NT], V[0:n, k, 4 * g + j, :],
                                           ET[0:n, 4 * g + j, k, :], start=(k == 0), stop=(k == CH - 1),
                                           skip_group_check=True)
                    mm.then_inc(av1_mm.sem, 1)
                for g in range(2):
                    pe.wait_ge(ct_out.sem, ct_out.at(b, g + 1))
                    for c in range(CH):
                        mm = pe.transpose(tm(g, PB)[:, c, :], chunk(CT[:, g, :], c), ident)
                    mm.then_inc(ctT_mm.sem, 1)
                yield
                pe.wait_ge(cn_ready.sem, cn_ready.through(b))
                for c in range(CH):
                    mm = pe.transpose(chunk(PB[:, 2, :], c), CN[:, c, :], identT)
                mm.then_inc(cnT_mm.sem, 1)
                pe.wait_ge(cnT_out.sem, cnT_out.through(b))
                for c in range(CH):
                    mm = pe.matmul(tm(3, PB)[:, c, :], chunk(CNT, c), w("out"), start=True, stop=True)
                mm.then_inc(out_mm.sem, 1)
                yield
                pe.wait_ge(n3_ready.sem, n3_ready.at(b, 2))
                for c in range(CH):
                    mm = pe.transpose(chunk(PB[:, 0, :], c), NBt[:, c, :], identT)
                mm.then_inc(n3T_mm.sem, 1)
                pe.wait_ge(xb_hi.sem, xb_hi.at(b, 2))
                for c in range(CH):
                    mm = pe.matmul(tm(1, PB)[:, c, :], chunk(XFb, c), w("router"), start=True, stop=True)
                mm.then_inc(rt_mm.sem, 1)
                pe.wait_ge(xb_lo.sem, xb_lo.at(b, 2))

                def w1(t):
                    if t == 1:
                        pe.wait_ge(rt_in.sem, rt_in.through(b))
                    if t >= 2:
                        pe.wait_ge(gelu1.sem, gelu1.at(b, t - 1))
                    mm3(pe, PB[:, t % 2, 0:NT], ws("w1", t), (XHb[:, :], XLb[:, :])).then_inc(w1_mm.sem, 1)

                def w2(e):
                    pe.wait_ge(gelu1.sem, gelu1.at(b, 2 * e + 2))
                    pe.wait_ge(w2_out.sem, w2_out.at(b, e))
                    for c in range(CH):
                        for j in range(2):
                            mm = pe.matmul(tm(2 + e % 2, PB)[:, c, :], chunk(G1[:, (2 * e + j) % 4, :], c),
                                           w("w2", 2 * e + j), start=(j == 0), stop=(j == 1))
                    mm.then_inc(w2_mm.sem, 1)

                w1(0)
                w1(1)
                yield
                pe.wait_ge(cb_ready.sem, cb_ready.through(b))
                for c in range(CH):
                    mm = pe.transpose(chunk(PB[:, 2, :], c), CB[:, c, :], identT)
                mm.then_inc(cbT_mm.sem, 1)
                pe.wait_ge(cbT_out.sem, cbT_out.through(b))
                for c in range(CH):
                    mm = pe.matmul(tm(3, PB)[:, c, :], chunk(CBT, c), w("b2"), start=True, stop=True)
                mm.then_inc(b2_mm.sem, 1)
                for e in range(E1):
                    if e + 1 < E1:
                        w1(2 * e + 2)
                        w1(2 * e + 3)
                    w2(e)
                    if e == 3:
                        yield
                yield

            run_streams(pe, pe_a, pe_b)

        @block.scalar
        def _(s):
            def act_a(s, b):
                if isinstance(b, int):
                    s.wait_ge(loaded.sem, 64)
                s.wait_ge(conv_done.sem, conv_done.through(b))
                s.wait_ge(tok_scale.sem, tok_scale.through(b))
                if later(b):
                    s.wait_ge(n1_ready.sem, n1_ready.before(b))
                for c in range(CH):
                    a = s.activation(TOK[:, c, :], tm(1, PA)[:, c, :], ACT.Tanh, scale=smA[:, 4, c:c + 1])
                a.then_inc(tanh_done.sem, 1)
                yield
                s.wait_ge(n1T_done.sem, n1T_done.through(b))
                s.activation(XHa[:, :], PA[:, 2, 0:NT], ACT.Copy).then_inc(xa_hi.sem, 1)
                yield
                for j in range(4):
                    s.wait_ge(k1_mm.sem, k1_mm.at(b, j + 1))
                    s.activation(K1[:, j, :], PA[:, j % 2, 0:NT], ACT.Relu, bias=col("bk1", j)).then_inc(k1_out.sem, 1)
                yield
                for i in range(2):
                    s.wait_ge(kq_mm.sem, kq_mm.at(b, i + 1))
                    s.activation(KQH[:, i, :], PA[:, i, 0:NT], ACT.Identity, bias=col("bk2", i)).then_inc(kq_hi.sem, 1)
                yield
                s.wait_ge(max0.sem, max0.through(b))
                for c in range(CH):
                    s.activation(EX[:, c, 0:L], PA[0:TP, c, 0:L], ACT.Exp, bias=smA[:, 5, c:c + 1],
                                 accum_out=smA[:, 6 + c, 0:1]).then_inc(exp0.sem, 1)
                yield
                for k in (0, 2):
                    n = TP if k < CH - 1 else TLAST
                    s.wait_ge(exT_mm.sem, exT_mm.at(b, k + 1))
                    a = s.activation(EXT[0:n, k, :], PA[0:n, k, 0:NT], ACT.Copy)
                    a.then_inc(exT_out.sem, 1)
                yield
                s.wait_ge(n2T_done.sem, n2T_done.at(b, 1))
                s.activation(XF[:, :], PA[:, 0, 0:NT], ACT.Copy).then_inc(xf_out.sem, 1)
                s.wait_ge(n2T_done.sem, n2T_done.at(b, 2))
                s.activation(NTt[:, :], PA[:, 1, 0:NT], ACT.Identity, bias=col("ln_b"), scale=col("ln_g"))\
                    .then_inc(nt_out.sem, 1)
                yield
                yield
                for j in range(4):
                    s.wait_ge(fc1_mm.sem, fc1_mm.at(b, j + 1))
                    s.activation(G0[:, j, :], PA[:, (3 + j) % 4, 0:NT], ACT.Gelu,
                                 bias=FW[:, 2 * H0 + j:2 * H0 + j + 1]).then_inc(gelu0.sem, 1)
                yield
                s.wait_ge(next_in.sem, next_in.through(b))
                s.activation(NG[:, :, :], NX[:, :, :], ACT.Gelu).then_inc(gelu_n.sem, 1)
                yield

            def act_b(s, b):
                def split_input(i):
                    s.wait_ge(n3T_mm.sem, n3T_mm.at(b, i))
                    s.activation(XFb[:, :], PB[:, 0, 0:NT], ACT.Copy)
                    s.activation(XHb[:, :], PB[:, 0, 0:NT], ACT.Copy).then_inc(xb_hi.sem, 1)

                split_input(1)
                yield
                for i in range(8):
                    s.wait_ge(qk_mm.sem, qk_mm.at(b, i + 1))
                    if i >= 2:
                        s.wait_ge(qk_out.sem, qk_out.at(b, i // 2))
                    else:
                        if later(b):
                            s.wait_ge(qk_out.sem, qk_out.before(b))
                    s.activation(QKF[:, i % 2, :], PB[:, 1 + i % 3, 0:NT], ACT.Identity,
                                 bias=col("qkb", i)).then_inc(qk_full.sem, 1)
                yield
                yield
                yield
                for g in range(2):
                    for h in range(4 * g, 4 * g + 4):
                        s.wait_ge(st_mm.sem, st_mm.at(b, 2 * h + 1))
                        if h == 0:
                            if later(b):
                                s.wait_ge(av1_mm.sem, av1_mm.before(b))
                        s.activation(ET[0:TP, h, 0:2, :], PB[0:TP, 0:2, 0:NT], ACT.Exp, scale=FACTOR)\
                            .then_inc(exp1.sem, 1)
                        s.wait_ge(st_mm.sem, st_mm.at(b, 2 * h + 2))
                        s.activation(ET[0:TLAST, h, 2, :], PB[0:TLAST, 2, 0:NT], ACT.Exp, scale=FACTOR)\
                            .then_inc(exp1.sem, 1)
                    yield
                    s.wait_ge(av1_mm.sem, av1_mm.at(b, g + 1))
                    s.activation(CT[:, g, :], PB[:, 3, 0:NT], ACT.Copy).then_inc(ct_out.sem, 1)
                yield
                s.wait_ge(cnT_mm.sem, cnT_mm.through(b))
                s.activation(CNT, PB[:, 2, 0:NT], ACT.Copy).then_inc(cnT_out.sem, 1)
                yield
                split_input(2)
                s.wait_ge(rt_in.sem, rt_in.through(b))
                s.activation(PRB[:, :, :], LG[:, :, :], ACT.Exp).then_inc(rt_exp.sem, 1)
                yield

                def gelu(t):
                    s.wait_ge(w1_mm.sem, w1_mm.at(b, t + 1))
                    if t >= 4:
                        s.wait_ge(w2_mm.sem, w2_mm.at(b, t // 2 - 1))
                    s.activation(G1[:, t % 4, :], PB[:, t % 2, 0:NT], ACT.Gelu, bias=col("b1", t))\
                        .then_inc(gelu1.sem, 1)

                gelu(0)
                gelu(1)
                for e in range(E1 - 1):
                    gelu(2 * e + 2)
                    gelu(2 * e + 3)
                    if e == 3:
                        yield
                yield

            run_streams(s, act_a, act_b)

        @block.vector
        def _(v):
            def rsqrt(y, x, small, at, link):
                half, t = small[:, at, :], small[:, at + 1, :]
                link(v.tensor_scalar(t.bitcast(I32), x.bitcast(I32), 1, None, ALU.logical_shift_right))
                link(v.tensor_tensor(y.bitcast(I32), MAGIC[0:TP, :], t.bitcast(I32), ALU.subtract))
                link(v.tensor_scalar(half, x, -0.5, None, ALU.mult))
                for _ in range(3):
                    link(v.tensor_tensor(t, y, y, ALU.mult))
                    link(v.tensor_tensor(t, t, half, ALU.mult))
                    link(v.scalar_tensor_tensor(out=y, in0=t, scalar=1.5, in1=y, op0=ALU.add, op1=ALU.mult))

            def norm_stats(h, st, mv, small, link):
                for c in range(CH):
                    last = v.bn_stats(st[:, c, :], h[:, c, :])
                link(last)
                mean_e, m2_e, mean_o, m2_o = st[:, :, 1], st[:, :, 2], st[:, :, 4], st[:, :, 5]
                v.tensor_tensor(small[:, 1, :], mean_e, mean_o, ALU.add)
                v.tensor_tensor(small[:, 3, :], m2_e, m2_o, ALU.add)
                link(v.tensor_tensor(small[:, 2, :], mean_e, mean_o, ALU.subtract))
                v.tensor_scalar(mv[:, :, 0], small[:, 1, :], 0.5, None, ALU.mult)
                link(v.tensor_tensor(small[:, 2, :], small[:, 2, :], small[:, 2, :], ALU.mult))
                link(v.scalar_tensor_tensor(out=small[:, 3, :], in0=small[:, 2, :], scalar=0.25 * D,
                                              in1=small[:, 3, :], op0=ALU.mult, op1=ALU.add))
                link(v.tensor_scalar(mv[:, :, 1], small[:, 3, :], 1.0 / D, None, ALU.mult))
                link(v.tensor_scalar(small[:, 1, :], mv[:, :, 1], EPS_LN, None, ALU.add))
                rsqrt(small[:, 0, :], small[:, 1, :], small, 2, link)

            def dve_a(v, b):
                link = Chain(v, dveA, b)
                v.wait_ge(wsq_done.sem, wsq_done.through(b))
                if later(b):
                    v.wait_ge(tanh_done.sem, tanh_done.before(b))
                link(v.tensor_scalar(smA[:, 1, :], tm(0, PA)[:, :, 0], 1e-30, None, ALU.max))
                rsqrt(smA[:, 0, :], smA[:, 1, :], smA, 2, link)
                link(v.tensor_tensor(smA[:, 0, :], smA[:, 0, :], smA[:, 1, :], ALU.mult))
                link(v.tensor_scalar(smA[:, 0, :], smA[:, 0, :], EPS_TOK, 1.0, ALU.add, ALU.max))
                link(v.reciprocal(smA[:, 1, :], smA[:, 0, :]))
                v.tensor_scalar(smA[:, 4, :], smA[:, 1, :], LAM_HALF, None, ALU.mult).then_inc(tok_scale.sem, 1)
                v.wait_ge(tanh_done.sem, tanh_done.through(b))
                link(v.tensor_tensor(TOK[:, :, :], TOK[:, :, :], row3("tok_b"), ALU.add))
                link(v.tensor_scalar(HA[:, :, :], TOK[:, :, :], 0.0, None, ALU.max))
                norm_stats(HA, stA, mvA, smA, link)
                for c in range(CH):
                    last = v.tensor_scalar(NA[:, c, :], HA[:, c, :], mvA[:, c, 0:1], smA[:, 0, c:c + 1],
                                           ALU.subtract, ALU.mult)
                last.then_inc(n1_ready.sem, 1)
                yield
                v.wait_ge(n1T_done.sem, n1T_done.through(b))
                v.wait_ge(xa_hi.sem, xa_hi.through(b))
                v.tensor_tensor(XLa[:, :], PA[:, 2, 0:NT], XHa[:, :], ALU.subtract).then_inc(xa_lo.sem, 1)
                yield
                for j in range(4):
                    v.wait_ge(e1_mm.sem, e1_mm.at(b, j + 1))
                    v.tensor_scalar(E1t[:, j, :], PA[:, 3 - j % 2, 0:NT], col("be1", j), 0.0,
                                    ALU.add, ALU.max).then_inc(e1_out.sem, 1)
                yield
                for i in range(2):
                    v.wait_ge(kq_hi.sem, kq_hi.at(b, i + 1))
                    v.scalar_tensor_tensor(out=KQL[:, i, :], in0=PA[:, i, 0:NT], scalar=col("bk2", i),
                                           in1=KQH[:, i, :], op0=ALU.add, op1=ALU.subtract).then_inc(kq_lo.sem, 1)
                v.wait_ge(emb_mm.sem, emb_mm.through(b))
                v.tensor_tensor(EMB[:, :, :], tm(3, PA), row3("be2"), ALU.add).then_inc(emb_out.sem, 1)
                yield
                v.wait_ge(s0_mm.sem, s0_mm.through(b))
                link(v.tensor_reduce(smA[:, 1, :], PA[0:TP, 0:CH, 0:L], AX.X, ALU.max))
                v.tensor_scalar(smA[:, 5, :], smA[:, 1, :], -1.0, None, ALU.mult).then_inc(max0.sem, 1)
                yield
                v.wait_ge(exT_mm.sem, exT_mm.at(b, 2))
                v.tensor_copy(EXT[:, 1, :], PA[0:TP, 1, 0:NT]).then_inc(exT_out.sem, 1)
                v.wait_ge(exp0.sem, exp0.through(b))
                link(v.reciprocal(smA[:, 9, :], smA[:, 6:9, 0:1].rearrange("p c o -> p (c o)")))
                v.wait_ge(av0_mm.sem, av0_mm.through(b))
                for c in range(CH):
                    last = v.scalar_tensor_tensor(out=HA[:, c, :], in0=tm(3, PA)[:, c, :], scalar=smA[:, 9, c:c + 1],
                                                  in1=HA[:, c, :], op0=ALU.mult, op1=ALU.add)
                link(last)
                norm_stats(HA, stA, mvA, smA, link)
                link(v.tensor_tensor(smA[:, 1, :], smA[:, 0, :], smA[:, 0, :], ALU.mult))
                link(v.tensor_tensor(smA[:, 1, :], smA[:, 1, :], mvA[:, :, 1], ALU.mult))
                link(v.tensor_scalar(smA[:, 1, :], smA[:, 1, :], EPS_LN, None, ALU.add))
                rsqrt(smA[:, 10, :], smA[:, 1, :], smA, 2, link)
                for c in range(CH):
                    last = v.tensor_scalar(NA[:, c, :], HA[:, c, :], mvA[:, c, 0:1], smA[:, 0, c:c + 1],
                                           ALU.subtract, ALU.mult)
                link(last)
                for c in range(CH):
                    last = v.tensor_scalar(NA2[:, c, :], NA[:, c, :], smA[:, 10, c:c + 1], None, ALU.mult)
                last.then_inc(n2_ready.sem, 1)
                yield
                v.wait_ge(at_mm.sem, at_mm.through(b))
                v.wait_ge(xf_out.sem, xf_out.through(b))
                link(v.scalar_tensor_tensor(out=XA[:, :], in0=PA[:, 2, 0:NT], scalar=col("attn_b"), in1=XF[:, :],
                                            op0=ALU.add, op1=ALU.add))
                v.tensor_copy(XHa[:, :], XA[:, :]).then_inc(xa_out.sem, 1)
                v.wait_ge(xa_out.sem, xa_out.at(b, 1))
                v.tensor_tensor(XLa[:, :], XA[:, :], XHa[:, :], ALU.subtract).then_inc(xa_out.sem, 1)
                yield
                yield
                v.wait_ge(fc2_mm.sem, fc2_mm.through(b))
                v.tensor_scalar(Y0[:, :], PA[:, 3, 0:NT], FW[:, 2 * H0 + 4:2 * H0 + 5], None, ALU.add)\
                    .then_inc(y0_out.sem, 1)
                yield
                v.wait_ge(next_mm.sem, next_mm.through(b))
                v.tensor_tensor(NX[:, :, :], tm(0, PA), row3("next_b"), ALU.add).then_inc(next_in.sem, 1)
                v.wait_ge(gelu_n.sem, gelu_n.through(b))
                if later(b):
                    v.wait_ge(hb_ready.sem, hb_ready.before(b))
                v.tensor_tensor(HN[:, :, :], HA[:, :, :], NG[:, :, :], ALU.add).then_inc(hn_ready.sem, 1)
                link.end()
                yield

            def dve_b(v, b):
                link = Chain(v, dveB, b)

                def normalise(h):
                    norm_stats(h, stB, mvB, smB, link)
                    for c in range(CH):
                        last = v.tensor_scalar(NBt[:, c, :], h[:, c, :], mvB[:, c, 0:1], smB[:, 0, c:c + 1],
                                               ALU.subtract, ALU.mult)
                    last.then_inc(n3_ready.sem, 1)

                def input_lo(i):
                    v.wait_ge(xb_hi.sem, xb_hi.at(b, i))
                    v.tensor_tensor(XLb[:, :], PB[:, 0, 0:NT], XHb[:, :], ALU.subtract).then_inc(xb_lo.sem, 1)

                v.wait_ge(hn_ready.sem, hn_ready.through(b))
                normalise(HN)
                yield
                input_lo(1)
                v.wait_ge(v_mm.sem, v_mm.through(b))
                if later(b):
                    v.wait_ge(av1_mm.sem, av1_mm.before(b))
                v.tensor_tensor(V[:, :, :, 0:HD], tm(0, PB).rearrange("p c (h d) -> p c h d", h=NH),
                                row3("vb").rearrange("p c (h d) -> p c h d", h=NH), ALU.add).then_inc(v_out.sem, 1)
                for p in range(4):
                    v.wait_ge(qk_round.sem, qk_round.at(b, 2 * p + 2))
                    v.scalar_tensor_tensor(out=Q[:, p, :], in0=QKR[:, 0, :], scalar=col("qneg"), in1=QKF[:, 0, :],
                                           op0=ALU.mult, op1=ALU.add)
                    for i in range(2):
                        r = slice(64 * i, 64 * i + 64)
                        last = v.scalar_tensor_tensor(out=KZ[r, 2 * p + i, :], in0=QKR[r, 1, :], scalar=col("kneg")[r, :],
                                                      in1=QKF[r, 1, :], op0=ALU.mult, op1=ALU.add)
                    last.then_inc(qk_out.sem, 1)
                yield
                for s in range(12):
                    v.wait_ge(s1_mm.sem, s1_mm.at(b, s + 1))
                    o = MX[:, :, :].rearrange("p h c -> p (h c)")[:, 2 * s:2 * s + 2]
                    v.tensor_reduce(o, PB[0:TP, 2 * (s % 2):2 * (s % 2) + 2, 0:L], AX.X, ALU.max).then_inc(s1_max.sem, 1)
                    if s == 5:
                        yield
                v.wait_ge(s1_max.sem, s1_max.through(b))
                v.tensor_scalar(M[:, :, :, 0], MX[:, :, :].rearrange("p h c -> p c h"), -1.0, None, ALU.mult)\
                    .then_inc(m_ready.sem, 1)
                yield
                for p in range(4):
                    v.wait_ge(mT_mm.sem, mT_mm.at(b, p + 1))
                    v.tensor_tensor(Q2[:, p, :], PB[:, p, 0:NT], Q[:, p, :], ALU.add).then_inc(q2_out.sem, 1)
                yield
                yield
                v.wait_ge(ctT_mm.sem, ctT_mm.at(b, 2))
                for g in range(2):
                    ct = tm(g, PB).rearrange("p c (h d) -> p c h d", h=4)
                    link(v.reciprocal(RD[:, :, 4 * g:4 * g + 4], ct[:, :, :, HD]))
                    last = v.tensor_tensor(
                        CN[:, :, 64 * g:64 * g + 64].rearrange("p c (h d) -> p c h d", h=4), ct[:, :, :, 0:HD],
                        RD[:, :, 4 * g:4 * g + 4].unsqueeze(3).to_broadcast([TP, CH, 4, HD]), ALU.mult)
                last.then_inc(cn_ready.sem, 1)
                yield
                if later(b):
                    v.wait_ge(stored.sem, stored.before(b))
                link(v.tensor_tensor(HB[:, :, :], HN[:, :, :], row3("out_b"), ALU.add))
                v.wait_ge(out_mm.sem, out_mm.through(b))
                v.tensor_tensor(HB[:, :, :], tm(3, PB), HB[:, :, :], ALU.add).then_inc(hb_ready.sem, 1)
                v.wait_ge(hb_ready.sem, hb_ready.through(b))
                normalise(HB)
                yield
                input_lo(2)
                v.wait_ge(rt_mm.sem, rt_mm.through(b))
                link(v.tensor_tensor(LG[:, :, :], tm(1, PB)[:, :, 0:E1], row3("br"), ALU.add))
                link(v.tensor_reduce(smB[:, 5, :], LG[:, :, :], AX.X, ALU.max))
                v.tensor_tensor(LG[:, :, :], LG[:, :, :], smB[:, 5, :].unsqueeze(2).to_broadcast([TP, CH, E1]),
                                ALU.subtract).then_inc(rt_in.sem, 1)
                v.wait_ge(rt_exp.sem, rt_exp.through(b))
                link(v.tensor_reduce(smB[:, 6, :], PRB[:, :, :], AX.X, ALU.add))
                link(v.reciprocal(smB[:, 7, :], smB[:, 6, :]))
                link(v.tensor_tensor(PRB[:, :, :], PRB[:, :, :],
                                     smB[:, 7, :].unsqueeze(2).to_broadcast([TP, CH, E1]), ALU.mult))
                mine = PRB[:, :, :].unsqueeze(3).to_broadcast([TP, CH, E1, E1])
                theirs = PRB[:, :, :].unsqueeze(2).to_broadcast([TP, CH, E1, E1])
                before = row("before").rearrange("p (e j) -> p e j", e=E1).unsqueeze(1).to_broadcast([TP, CH, E1, E1])
                v.tensor_tensor(BEAT[:, :, :, :], theirs, mine, ALU.is_gt)
                link(v.tensor_tensor(TIE[:, :, :, :], theirs, mine, ALU.is_equal))
                link(v.tensor_tensor(TIE[:, :, :, :], TIE[:, :, :, :], before, ALU.mult))
                link(v.tensor_tensor(BEAT[:, :, :, :], BEAT[:, :, :, :], TIE[:, :, :, :], ALU.add))
                link(v.tensor_reduce(CNTB[:, :, :], BEAT[:, :, :, :], AX.X, ALU.add))
                if later(b):
                    v.wait_ge(w2_out.sem, w2_out.before(b))
                v.scalar_tensor_tensor(out=CB[:, :, 0:E1], in0=CNTB[:, :, :], scalar=1.5, in1=PRB[:, :, :],
                                       op0=ALU.is_lt, op1=ALU.mult).then_inc(cb_ready.sem, 1)
                yield
                v.wait_ge(cbT_mm.sem, cbT_mm.through(b))
                v.tensor_copy(CBT, PB[:, 2, 0:NT]).then_inc(cbT_out.sem, 1)
                v.wait_ge(b2_mm.sem, b2_mm.through(b))
                v.tensor_tensor(HB[:, :, :], tm(3, PB), HB[:, :, :], ALU.add).then_inc(w2_out.sem, 1)
                for e in range(E1):
                    v.wait_ge(w2_mm.sem, w2_mm.at(b, e + 1))
                    v.wait_ge(w2_out.sem, w2_out.at(b, e + 1))
                    for c in range(CH):
                        last = v.scalar_tensor_tensor(out=HB[:, c, :], in0=tm(2 + e % 2, PB)[:, c, :],
                                                      scalar=CB[:, c, e:e + 1], in1=HB[:, c, :],
                                                      op0=ALU.mult, op1=ALU.add)
                    last.then_inc(w2_out.sem, 1)
                    if e == 3:
                        yield
                link.end()
                yield

            v.wait_ge(loaded.sem, 64)
            v.wait_ge(zeros_set.sem, 2)
            v.tensor_copy(WH[:, :], WS).then_inc(weights_split.sem, 1)
            v.wait_ge(weights_split.sem, 1)
            v.tensor_tensor(WL[:, :], WS, WH[:, :], ALU.subtract).then_inc(weights_split.sem, 1)
            run_streams(v, dve_a, dve_b)


_INS = ["x", "weights", "split_w", "cols", "rows", "ffw"]


def lay_out(i):
    f = np.float32
    a = {k: np.asarray(v) for k, v in i.items()}

    def blocks(m):
        n = m.shape[0] // 128
        return m.reshape(n, 128, -1).transpose(1, 0, 2).reshape(128, -1)

    def wide(m):
        o = np.zeros((m.shape[0], 128), f)
        o[:, :m.shape[1]] = m
        return o

    x = np.zeros((NB, CIN, XPAD), f)
    x[:, :, :L_IN] = a["x"].transpose(0, 2, 1)
    conv = np.zeros((TAPS + 1, CIN, D), f)
    conv[:TAPS] = a["L0_tok_kernel"]
    b2 = np.zeros((128, D), f)
    b2[:E1] = a["L1_ffn_b2"]
    qkv = a["L1_attn_qkv_w"].reshape(NH, 3, HD, D)
    qkv_b = a["L1_attn_qkv_b"].reshape(NH, 3, HD)
    parts = {
        "conv": blocks(conv.reshape(-1, D)),
        "k2": blocks(a["L0_attn_Wk2"].T), "e2": blocks(a["L0_attn_We2"].T),
        "attn": a["L0_ffn_attn_w"].T, "next": a["L0_ffn_next_w"].T,
        "v": qkv[:, 2].reshape(NH * HD, D).T, "out": a["L1_attn_out_w"].T,
        "router": wide(a["L1_ffn_Wr"].T), "b2": b2,
        "w2": blocks(a["L1_ffn_W2"].reshape(E1 * H1, D)),
        "ident": np.eye(128, dtype=f), "ones": np.ones((128, 128), f),
    }
    qk = np.zeros((D, 4, 2, 2, 4, HD), f)
    qkb = np.zeros((4, 2, 2, 4, HD), f)
    for h in range(NH):
        for s in range(2):
            for blk in range(1, 4):
                qk[:, h // 2, s, h % 2, blk] = qkv[h, s].T
                qkb[h // 2, s, h % 2, blk] = qkv_b[h, s]
    qkb[:, 1, :, 0, 0] = 1.0
    neg = np.zeros((2, 2, 4, HD), f)
    neg[0, :, 3], neg[1, :, 2] = -1.0, -1.0
    split = {"k1": a["L0_attn_Wk1"].T, "e1": a["L0_attn_We1"].T, "qk": qk.reshape(D, -1),
             "w1": a["L1_ffn_W1"].transpose(1, 0, 2).reshape(D, -1)}
    cols = {"bk1": a["L0_attn_bk1"].reshape(4, 128).T, "be1": a["L0_attn_be1"].reshape(4, 128).T,
            "bk2": a["L0_attn_bk2"].reshape(2, 128).T, "ln_g": a["L0_ffn_ln_g"][:, None],
            "ln_b": a["L0_ffn_ln_b"][:, None], "attn_b": a["L0_ffn_attn_b"][:, None],
            "qkb": qkb.reshape(8, 128).T, "b1": a["L1_ffn_b1"].reshape(16, 128).T,
            "qneg": neg[0].reshape(128, 1), "kneg": neg[1].reshape(128, 1)}
    before = np.tril(np.ones((E1, E1), f), -1)
    rows = {"tok_b": a["L0_tok_bias"], "be2": a["L0_attn_be2"], "next_b": a["L0_ffn_next_b"],
            "vb": qkv_b[:, 2].reshape(-1), "out_b": a["L1_attn_out_b"], "br": a["L1_ffn_br"],
            "before": before.reshape(-1)}
    ffw = np.zeros((E0, 128, FFW), f)
    ffw[:, :, 0:H0] = a["L0_ffn_fc1_w"].transpose(0, 2, 1)
    ffw[:, :, H0:2 * H0] = a["L0_ffn_fc2_w"].transpose(0, 2, 1).reshape(E0, 4, 128, D).transpose(0, 2, 1, 3)\
        .reshape(E0, 128, 4 * D)
    ffw[:, :, 2 * H0:2 * H0 + 4] = a["L0_ffn_fc1_b"].reshape(E0, 4, 128).transpose(0, 2, 1)
    ffw[:, :, 2 * H0 + 4] = a["L0_ffn_fc2_b"]
    row = np.concatenate([rows[n] for n, _ in ROWS])
    return {
        "x": x, "ffw": ffw,
        "weights": np.concatenate([parts[n] for n, _ in WEIGHTS], 1),
        "split_w": np.concatenate([split[n] for n, _ in SPLIT], 1),
        "cols": np.concatenate([cols[n] for n, _ in COLS], 1),
        "rows": np.ascontiguousarray(np.broadcast_to(row, (128, R_N))),
    }


def kernel(**inputs):
    import concourse.bacc as bacc
    from concourse.bass_utils import run_bass_kernel_spmd

    nc = bacc.Bacc("TRN2", target_bir_lowering=False, num_devices=1)
    arrays, args = {}, []
    for name, value in lay_out(inputs).items():
        value = np.ascontiguousarray(value)
        arrays[f"in_{name}"] = value
    for name in _INS:
        value = arrays[f"in_{name}"]
        args.append(nc.dram_tensor(f"in_{name}", value.shape, mybir.dt.from_np(value.dtype), kind="ExternalInput").ap())
    out = nc.dram_tensor("out_0", (NB, L, D), F32, kind="ExternalOutput").ap()
    tower_kernel(nc, *args, out)
    r = run_bass_kernel_spmd(nc, [arrays], core_ids=[0])
    return r.results[0]["out_0"]
```

```python
from contextlib import ExitStack

import numpy as np

import concourse.bass as bass
from concourse import mybir

F32 = mybir.dt.float32
F32R = mybir.dt.float32r
I32 = mybir.dt.int32
ALU = mybir.AluOpType
ACT = mybir.ActivationFunctionType
AX = mybir.AxisListType

NB, L_IN, CIN = 32, 375, 64
TAPS = 9
L = L_IN - TAPS + 1
D = 128
CH, TP = 3, 124
NT = CH * TP
TLAST = L - 2 * TP
XW = NT + TAPS + 1
XPAD = XW + 2
NPAIR = (TAPS + 1) // 2
NH, HD = 8, 16
E0, H0 = 8, 512
E1, H1 = 8, 256
EPS_LN = 1e-5
EPS_TOK = 1e-7
W2_BANK = (2, 3, 3, 3, 2, 3, 2, 3)
LAM_HALF = 1.0 / (1.0 + 1e-7)
FACTOR = HD ** -0.5

WEIGHTS = [("conv", NPAIR * D), ("k2", 4 * 2 * D), ("e2", 4 * D), ("attn", D), ("next", D), ("v", D),
           ("out", D), ("router", D), ("b2", D), ("w2", E1 * 2 * D), ("ident", D), ("ones", D)]
SPLIT = [("k1", 512), ("e1", 512), ("qk", 8 * D), ("w1", E1 * H1)]
COLS = [("bk1", 4), ("be1", 4), ("bk2", 2), ("ln_g", 1), ("ln_b", 1), ("attn_b", 1), ("qkb", 8), ("b1", 16),
        ("qneg", 1), ("kneg", 1)]
ROWS = [("tok_b", D), ("be2", D), ("next_b", D), ("vb", D), ("out_b", D), ("br", E1), ("before", E1 * E1)]
FFW = H0 + H0 + 4 + 1


def offsets(parts):
    at, n = {}, 0
    for name, width in parts:
        at[name] = (n, n + width)
        n += width
    return at, n


W_AT, W_N = offsets(WEIGHTS)
S_AT, S_N = offsets(SPLIT)
C_AT, C_N = offsets(COLS)
R_AT, R_N = offsets(ROWS)

SCHEDULE = """
c.turn2 c.router a.window c.top2 c.first c.e0 c.e1 a.split_fc1 a.conv a.tanh c.combT c.e2 a.norm1 c.bias c.e3
b.norm1 c.e4 a.turn1 c.e5 c.e6 b.turn1 c.e7 a.hid0 b.qk0 a.hid1 b.qk1 a.hid2 a.hid3 b.qk2 b.qk3 b.values
a.queries a.keys a.emb a.scores b.s0 b.s1 b.s2 b.s3 a.exp b.s4 b.s5 a.probsT b.s6 b.s7 a.attend a.norm2 b.s8
b.s9 b.s10 b.s11 a.turn2 b.maxT a.attn b.st0 b.st1 a.fc1_0 a.fc1_1 a.fc1_2 a.fc1_3 b.st2 a.fc2 b.st3 b.st4
b.st5 b.av0 b.st6 b.st7 b.av1 b.ctx a.last b.ctxT b.proj a.gelu a.result
""".split()


class Signal:

    def __init__(self, sem, per):
        self.sem, self.per = sem, per

    def at(self, b, count):
        return b * self.per + count

    def through(self, b):
        return b * self.per + self.per

    def before(self, b):
        return b * self.per


def later(b):
    return not (isinstance(b, int) and b == 0)


def weave(a=None, b=None, c=None):
    streams = {"a": a, "b": b, "c": c}
    ahead = {k: next(v, None) if v is not None else None for k, v in streams.items()}
    for step in SCHEDULE:
        while ahead[step[0]] == step:
            ahead[step[0]] = next(streams[step[0]], None)
    assert set(ahead.values()) == {None}, ahead


def nothing(b):
    yield from ()


def tower_kernel(nc, x, weights, split_w, cols, rows, ffw, out):
    with ExitStack() as ctx:
        def sb(name, shape, dt=F32):
            return ctx.enter_context(nc.sbuf_tensor(name, shape, dt))

        def signal(name, per):
            return Signal(ctx.enter_context(nc.semaphore(name)), per)

        W = sb("W", [128, W_N])
        WH = sb("WH", [128, S_N], F32R)
        WL = sb("WL", [128, S_N], F32R)
        C = sb("C", [128, C_N])
        ROW = sb("ROW", [128, R_N])
        GATE = sb("GATE", [128, 16])
        MAGIC = sb("MAGIC", [128, 3], I32)

        def w(name, i=0, width=D):
            lo = W_AT[name][0] + i * width
            return W[:, lo:lo + width]

        def ws(name, i):
            lo = S_AT[name][0] + i * D
            return WH[:, lo:lo + D], WL[:, lo:lo + D]

        def col(name, i=0):
            return C[:, C_AT[name][0] + i:C_AT[name][0] + i + 1]

        def row(name):
            return ROW[0:TP, R_AT[name][0]:R_AT[name][1]]

        def row3(name):
            return row(name).unsqueeze(1).to_broadcast([TP, CH, R_AT[name][1] - R_AT[name][0]])

        ident = w("ident")
        identT = ident[0:TP, 0:TP]

        XX = sb("XX", [128, XW])
        SQ = sb("SQ", [128, XW])
        S4 = sb("S4", [128, XW])
        S8 = sb("S8", [128, XW])
        FW = sb("FW", [128, FFW])
        F1H = sb("F1H", [128, H0], F32R)
        F1L = sb("F1L", [128, H0], F32R)
        smA = sb("smA", [TP, 16, CH])
        stA = sb("stA", [TP, CH, 6])
        mvA = sb("mvA", [TP, CH, 2])
        TOK = sb("TOK", [TP, CH, D])
        HA = sb("HA", [TP, CH, D])
        NA = sb("NA", [TP, CH, D])
        NA2 = TOK
        XHa = sb("XHa", [128, NT], F32R)
        XLa = sb("XLa", [128, NT], F32R)
        K1 = sb("K1", [128, 4, NT])
        E1t = sb("E1t", [128, 4, NT])
        KQH = sb("KQH", [128, 2, NT], F32R)
        KQL = sb("KQL", [128, 2, NT], F32R)
        EMB = sb("EMB", [TP, CH, D])
        EX = sb("EX", [TP, CH, NT])
        EXT = E1t[0:TP, 0:CH, :]
        XF = sb("XF", [128, NT])
        NTt = sb("NTt", [128, NT])
        XA = sb("XA", [128, NT])
        G0 = K1
        Y0 = XF
        NX = sb("NX", [TP, CH, D])
        NG = NX
        HN = sb("HN", [TP, CH, D])

        smB = sb("smB", [TP, 16, CH])
        stB = sb("stB", [TP, CH, 6])
        mvB = sb("mvB", [TP, CH, 2])
        NBt = sb("NBt", [TP, CH, D])
        XFb = sb("XFb", [128, NT])
        XHb = sb("XHb", [128, NT], F32R)
        XLb = sb("XLb", [128, NT], F32R)
        QKF = sb("QKF", [128, 4, NT])
        QKR = sb("QKR", [128, 4, NT], F32R)
        Q = sb("Q", [128, 4, NT], F32R)
        Q2 = sb("Q2", [128, 4, NT], F32R)
        KZ = sb("KZ", [128, NH, NT], F32R)
        V = sb("V", [TP, CH, NH, 32])
        MX = sb("MX", [TP, NH, CH])
        M = sb("M", [TP, CH, NH, 64])
        ET = sb("ET", [128, NH, CH, NT])
        WS = ET[:, :, :, :].rearrange("p h c t -> p (h c t)")[:, 0:S_N]
        CT = sb("CT", [128, 2, NT])
        RD = sb("RD", [TP, CH, NH])
        CN = sb("CN", [TP, CH, D])
        spare = ET[:, :, :, :].rearrange("p h c t -> p (h c t)")
        G1 = spare[:, 0:4 * NT].rearrange("p (j t) -> p j t", j=4)
        CNT = spare[:, 4 * NT:5 * NT]
        CBT = spare[:, 5 * NT:6 * NT]
        HM = sb("HM", [TP, CH, D])
        HB = sb("HB", [TP, CH, D])
        LG = sb("LG", [TP, CH, E1])
        PRB = sb("PRB", [TP, CH, E1])
        BEAT = sb("BEAT", [TP, CH, E1, E1])
        TIE = sb("TIE", [TP, CH, E1, E1])
        CNTB = sb("CNTB", [TP, CH, E1])
        CB = sb("CB", [TP, CH, D])

        PA = ctx.enter_context(nc.psum_tensor("PA", [128, 4, 512], F32))
        PB = ctx.enter_context(nc.psum_tensor("PB", [128, 4, 512], F32))

        def tm(bank, P):
            return P[0:TP, bank, 0:CH * D].rearrange("p (c d) -> p c d", c=CH)

        def chunk(tile, c, n=TP):
            return tile[:, c * TP:c * TP + n]

        loaded = signal("loaded", 80)
        weights_split = signal("weights_split", 1)
        zeros_set = signal("zeros_set", 1)
        x_loaded = signal("x_loaded", 32)
        ffw_loaded = signal("ffw_loaded", 16)
        window_sums = signal("window_sums", 1)
        poolA = signal("poolA", 4)
        wsq_done = signal("wsq_done", 1)
        conv_done = signal("conv_done", 1)
        tok_scale = signal("tok_scale", 1)
        tanh_done = signal("tanh_done", 1)
        dveA = signal("dveA", 63)
        n1_ready = signal("n1_ready", 1)
        n1T_done = signal("n1T_done", 1)
        xa_hi = signal("xa_hi", 1)
        xa_lo = signal("xa_lo", 1)
        k1_mm = signal("k1_mm", 4)
        e1_mm = signal("e1_mm", 4)
        k1_out = signal("k1_out", 4)
        e1_out = signal("e1_out", 4)
        kq_mm = signal("kq_mm", 2)
        kq_hi = signal("kq_hi", 2)
        kq_lo = signal("kq_lo", 2)
        emb_mm = signal("emb_mm", 1)
        emb_out = signal("emb_out", 1)
        s0_mm = signal("s0_mm", 3)
        max0 = signal("max0", 1)
        exp0 = signal("exp0", 3)
        exT_mm = signal("exT_mm", 3)
        exT_out = signal("exT_out", 3)
        av0_mm = signal("av0_mm", 1)
        n2_ready = signal("n2_ready", 2)
        n2T_done = signal("n2T_done", 2)
        xf_out = signal("xf_out", 1)
        nt_out = signal("nt_out", 1)
        at_mm = signal("at_mm", 1)
        xa_out = signal("xa_out", 2)
        f1_split = signal("f1_split", 1)
        fc1_mm = signal("fc1_mm", 4)
        gelu0 = signal("gelu0", 4)
        fc2_mm = signal("fc2_mm", 1)
        y0_out = signal("y0_out", 1)
        next_mm = signal("next_mm", 1)
        next_in = signal("next_in", 1)
        gelu_n = signal("gelu_n", 1)
        hn_ready = signal("hn_ready", 1)
        dveB = signal("dveB", 29)
        dveC = signal("dveC", 10)
        n3_ready = signal("n3_ready", 2)
        n3T_mm = signal("n3T_mm", 2)
        xb_hi = signal("xb_hi", 2)
        xb_lo = signal("xb_lo", 2)
        xb_full = signal("xb_full", 2)
        qk_mm = signal("qk_mm", 8)
        qk_full = signal("qk_full", 8)
        qk_round = signal("qk_round", 8)
        q_signed = signal("q_signed", 4)
        q_out = signal("q_out", 4)
        k_out = signal("k_out", 4)
        v_mm = signal("v_mm", 1)
        v_out = signal("v_out", 1)
        s1_mm = signal("s1_mm", 12)
        s1_max = signal("s1_max", 12)
        m_ready = signal("m_ready", 1)
        mT_mm = signal("mT_mm", 4)
        q2_out = signal("q2_out", 4)
        st_mm = signal("st_mm", 24)
        exp1 = signal("exp1", 24)
        av1_mm = signal("av1_mm", 2)
        ct_out = signal("ct_out", 2)
        ctT_mm = signal("ctT_mm", 2)
        cn_ready = signal("cn_ready", 1)
        cnT_mm = signal("cnT_mm", 1)
        cnT_out = signal("cnT_out", 1)
        out_mm = signal("out_mm", 1)
        hm_ready = signal("hm_ready", 1)
        hb_ready = signal("hb_ready", 1)
        rt_mm = signal("rt_mm", 1)
        rt_in = signal("rt_in", 1)
        rt_exp = signal("rt_exp", 1)
        cbT_mm = signal("cbT_mm", 1)
        cbT_out = signal("cbT_out", 1)
        b2_mm = signal("b2_mm", 1)
        w1_mm = signal("w1_mm", 16)
        gelu1 = signal("gelu1", 16)
        w2_mm = signal("w2_mm", 8)
        w2_out = signal("w2_out", 9)
        stored = signal("stored", 32)

        class Chain:

            def __init__(self, eng, sig, b):
                self.eng, self.sig, self.b, self.n = eng, sig, b, 0

            def __call__(self, ins):
                self.n += 1
                ins.then_inc(self.sig.sem, 1)
                self.eng.wait_ge(self.sig.sem, self.b * self.sig.per + self.n)

            def end(self):
                assert self.n == self.sig.per, (self.n, self.sig.per)

        def run_streams(eng, stream_a, stream_b, stream_c):
            weave(stream_a(0))
            weave(stream_a(1), stream_b(0))
            with eng.Fori(2, NB) as b:
                weave(stream_a(b), stream_b(b - 1), stream_c(b - 2))
            weave(None, stream_b(NB - 1), stream_c(NB - 2))
            weave(None, None, stream_c(NB - 1))

        block = ctx.enter_context(nc.Block())

        @block.sync
        def _(sp):
            sp.dma_start(W[:, :], weights).then_inc(loaded.sem, 16)
            sp.dma_start(WS, split_w).then_inc(loaded.sem, 16)
            sp.dma_start(C[:, :], cols).then_inc(loaded.sem, 16)
            sp.dma_start(ROW[:, :], rows).then_inc(loaded.sem, 16)

            def load_x(b):
                if later(b):
                    sp.wait_ge(conv_done.sem, conv_done.before(b))
                    sp.wait_ge(window_sums.sem, window_sums.before(b))
                sp.dma_start(XX[0:CIN, :], x[b, :, 0:XW]).then_inc(x_loaded.sem, 16)
                sp.dma_start(XX[CIN:128, :], x[b, :, 1:XW + 1]).then_inc(x_loaded.sem, 16)

            def load_ffw(b):
                if later(b):
                    sp.wait_ge(y0_out.sem, y0_out.before(b))
                    sp.wait_ge(f1_split.sem, f1_split.before(b))
                sp.dma_start(FW[:, :], ffw[(b // 2) % E0]).then_inc(ffw_loaded.sem, 16)

            def store(b):
                sp.wait_ge(w2_out.sem, w2_out.through(b))
                sp.dma_start(out[b, 0:2 * TP, :].rearrange("(c p) d -> p c d", c=2),
                             HB[:, 0:2, :]).then_inc(stored.sem, 16)
                sp.dma_start(out[b, 2 * TP:L, :], HB[0:TLAST, 2, :]).then_inc(stored.sem, 16)

            load_x(0)
            load_ffw(0)
            load_x(1)
            load_ffw(1)
            load_x(2)
            load_ffw(2)
            with sp.Fori(2, NB - 1) as b:
                load_x(b + 1)
                store(b - 2)
                load_ffw(b + 1)
            store(NB - 3)
            store(NB - 2)
            store(NB - 1)
            sp.wait_ge(stored.sem, NB * stored.per)

        @block.gpsimd
        def _(g):
            def gate(i):
                g.tensor_tensor(GATE[:, i:i + 1], GATE[:, 15:16], GATE[:, 15:16], ALU.add)

            def pool_a(b):
                link = Chain(g, poolA, b)
                yield "a.window"
                g.wait_ge(x_loaded.sem, x_loaded.through(b))
                if later(b):
                    g.wait_ge(wsq_done.sem, wsq_done.before(b))
                link(g.tensor_tensor(SQ[:, :], XX[:, :], XX[:, :], ALU.mult))
                link(g.tensor_tensor(S4[:, 0:NT + 4], SQ[:, 0:NT + 4], SQ[:, 2:NT + 6], ALU.add))
                link(g.tensor_tensor(S8[:, 0:NT], S4[:, 0:NT], S4[:, 4:NT + 4], ALU.add))
                g.tensor_tensor(S8[0:CIN, 0:NT], S8[0:CIN, 0:NT], SQ[0:CIN, 8:NT + 8],
                                ALU.add).then_inc(window_sums.sem, 1)
                yield "a.split_fc1"
                g.wait_ge(ffw_loaded.sem, ffw_loaded.through(b))
                if later(b):
                    g.wait_ge(fc1_mm.sem, fc1_mm.before(b))
                gate(8)
                link(g.tensor_scalar(F1H[:, :], FW[:, 0:H0], 1.0, 0.0, ALU.mult, ALU.add))
                g.tensor_tensor(F1L[:, :], FW[:, 0:H0], F1H[:, :], ALU.subtract).then_inc(f1_split.sem, 1)
                link.end()

            def pool_b(b):
                for p in range(4):
                    yield f"b.qk{p}"
                    full, rounded = QKF[:, 2 * (p % 2):2 * (p % 2) + 2, :], QKR[:, 2 * (p % 2):2 * (p % 2) + 2, :]
                    g.wait_ge(qk_full.sem, qk_full.at(b, 2 * p + 2))
                    if p >= 2:
                        g.wait_ge(k_out.sem, k_out.at(b, p - 1))
                    elif later(b):
                        g.wait_ge(k_out.sem, k_out.before(b))
                    gate(2 * p)
                    g.tensor_scalar(rounded[:, 1, :], full[:, 1, :], 1.0, 0.0, ALU.mult,
                                    ALU.add).then_inc(qk_round.sem, 1)
                    g.tensor_scalar(rounded[:, 0, :], full[:, 0, :], 1.0, 0.0, ALU.mult,
                                    ALU.add).then_inc(qk_round.sem, 1)
                    g.wait_ge(qk_round.sem, qk_round.at(b, 2 * p + 2))
                    if later(b):
                        g.wait_ge(q2_out.sem, q2_out.before(b))
                    gate(2 * p + 1)
                    g.tensor_scalar(rounded[:, 0, :], rounded[:, 0, :], col("qneg"), 0.0, ALU.mult,
                                    ALU.add).then_inc(q_signed.sem, 1)
                    g.wait_ge(q_signed.sem, q_signed.at(b, p + 1))
                    g.tensor_tensor(Q[:, p, :], rounded[:, 0, :], full[:, 0, :], ALU.add).then_inc(q_out.sem, 1)

            g.memset(KZ[:, :, :].bitcast(F32), 0.0)
            g.memset(V[:, :, :, HD:32], 0.0)
            g.memset(M[:, :, :, :], 0.0)
            g.memset(CB[:, :, :], 0.0)
            g.memset(GATE[:, :], 0.0)
            g.memset(MAGIC[:, :], 0x5F3759DF).then_inc(zeros_set.sem, 1)
            g.wait_ge(zeros_set.sem, 1)
            g.memset(V[:, :, :, HD:HD + 1], 1.0).then_inc(zeros_set.sem, 1)
            g.wait_ge(loaded.sem, 64)
            run_streams(g, pool_a, pool_b, nothing)

        @block.tensor
        def _(pe):
            def mm3(o, wt, xt):
                pe.matmul(o, wt[0], xt[0], start=True, stop=False)
                pe.matmul(o, wt[0], xt[1], start=False, stop=False)
                return pe.matmul(o, wt[1], xt[0], start=False, stop=True)

            def keys(k):
                return TP if k < CH - 1 else TLAST

            def pe_a(b):
                yield "a.window"
                pe.wait_ge(window_sums.sem, window_sums.through(b))
                if later(b):
                    pe.wait_ge(next_in.sem, next_in.before(b))
                for c in range(CH):
                    mm = pe.matmul(tm(0, PA)[:, c, :], chunk(S8, c), w("ones"), start=True, stop=True)
                mm.then_inc(wsq_done.sem, 1)
                yield "a.conv"
                pe.wait_ge(x_loaded.sem, x_loaded.through(b))
                if later(b):
                    pe.wait_ge(gelu0.sem, gelu0.before(b))
                for c in range(CH):
                    for j in range(NPAIR):
                        mm = pe.matmul(tm(1, PA)[:, c, :], XX[:, c * TP + 2 * j:c * TP + 2 * j + TP], w("conv", j),
                                       start=(j == 0), stop=(j == NPAIR - 1))
                mm.then_inc(conv_done.sem, 1)
                yield "a.turn1"
                pe.wait_ge(n1_ready.sem, n1_ready.through(b))
                if later(b):
                    pe.wait_ge(xa_out.sem, xa_out.before(b))
                for c in range(CH):
                    mm = pe.transpose(chunk(PA[:, 2, :], c), NA[:, c, :], identT)
                mm.then_inc(n1T_done.sem, 1)
                for j in range(4):
                    yield f"a.hid{j}"
                    if j == 0:
                        pe.wait_ge(xa_hi.sem, xa_hi.through(b))
                        pe.wait_ge(xa_lo.sem, xa_lo.through(b))
                        pe.wait_ge(tanh_done.sem, tanh_done.through(b))
                        if later(b):
                            pe.wait_ge(y0_out.sem, y0_out.before(b))
                    if j >= 2:
                        pe.wait_ge(k1_out.sem, k1_out.at(b, j - 1))
                    mm3(PA[:, j % 2, 0:NT], ws("k1", j), (XHa[:, :], XLa[:, :])).then_inc(k1_mm.sem, 1)
                    if j >= 2:
                        pe.wait_ge(e1_out.sem, e1_out.at(b, j - 1))
                    mm3(PA[:, 3 - j % 2, 0:NT], ws("e1", j), (XHa[:, :], XLa[:, :])).then_inc(e1_mm.sem, 1)
                for i, name in ((1, "a.queries"), (0, "a.keys")):
                    yield name
                    pe.wait_ge(k1_out.sem, k1_out.through(b))
                    for j in range(4):
                        mm = pe.matmul(PA[:, i, 0:NT], w("k2", 2 * j + i), K1[:, j, :], start=(j == 0), stop=(j == 3))
                    mm.then_inc(kq_mm.sem, 1)
                yield "a.emb"
                pe.wait_ge(e1_out.sem, e1_out.through(b))
                for c in range(CH):
                    for j in range(4):
                        mm = pe.matmul(tm(3, PA)[:, c, :], chunk(E1t[:, j, :], c), w("e2", j),
                                       start=(j == 0), stop=(j == 3))
                mm.then_inc(emb_mm.sem, 1)
                yield "a.scores"
                pe.wait_ge(kq_hi.sem, kq_hi.through(b))
                pe.wait_ge(kq_lo.sem, kq_lo.through(b))
                for c in range(CH):
                    mm = mm3(PA[0:TP, c, 0:NT], (chunk(KQH[:, 1, :], c), chunk(KQL[:, 1, :], c)),
                             (KQH[:, 0, :], KQL[:, 0, :]))
                    mm.then_inc(s0_mm.sem, 1)
                yield "a.probsT"
                pe.wait_ge(exp0.sem, exp0.through(b))
                for k in range(CH):
                    for c in range(CH):
                        mm = pe.transpose(chunk(PA[0:keys(k), k, :], c), EX[:, c, k * TP:k * TP + keys(k)], identT)
                    mm.then_inc(exT_mm.sem, 1)
                yield "a.attend"
                pe.wait_ge(exT_out.sem, exT_out.through(b))
                pe.wait_ge(emb_out.sem, emb_out.through(b))
                for c in range(CH):
                    for k in range(CH):
                        mm = pe.matmul(tm(3, PA)[:, c, :], chunk(EXT[0:keys(k), k, :], c), EMB[0:keys(k), k, :],
                                       start=(k == 0), stop=(k == CH - 1))
                mm.then_inc(av0_mm.sem, 1)
                yield "a.turn2"
                for i, t in enumerate((NA, NA2)):
                    pe.wait_ge(n2_ready.sem, n2_ready.at(b, i + 1))
                    for c in range(CH):
                        mm = pe.transpose(chunk(PA[:, i, :], c), t[:, c, :], identT)
                    mm.then_inc(n2T_done.sem, 1)
                yield "a.attn"
                pe.wait_ge(nt_out.sem, nt_out.through(b))
                pe.matmul(PA[:, 2, 0:NT], w("attn"), NTt[:, :], start=True, stop=True).then_inc(at_mm.sem, 1)
                for j in range(4):
                    yield f"a.fc1_{j}"
                    if j == 0:
                        pe.wait_ge(xa_out.sem, xa_out.through(b))
                        pe.wait_ge(f1_split.sem, f1_split.through(b))
                    mm3(PA[:, (3 + j) % 4, 0:NT], (F1H[:, j * D:(j + 1) * D], F1L[:, j * D:(j + 1) * D]),
                        (XHa[:, :], XLa[:, :])).then_inc(fc1_mm.sem, 1)
                yield "a.fc2"
                for j in range(4):
                    pe.wait_ge(gelu0.sem, gelu0.at(b, j + 1))
                    mm = pe.matmul(PA[:, 3, 0:NT], FW[:, H0 + j * D:H0 + (j + 1) * D], G0[:, j, :],
                                   start=(j == 0), stop=(j == 3))
                mm.then_inc(fc2_mm.sem, 1)
                yield "a.last"
                pe.wait_ge(y0_out.sem, y0_out.through(b))
                for c in range(CH):
                    mm = pe.matmul(tm(0, PA)[:, c, :], chunk(Y0, c), w("next"), start=True, stop=True)
                mm.then_inc(next_mm.sem, 1)

            def pe_b(b):
                yield "b.turn1"
                pe.wait_ge(n3_ready.sem, n3_ready.at(b, 1))
                if later(b):
                    pe.wait_ge(gelu1.sem, gelu1.before(b))
                for c in range(CH):
                    mm = pe.transpose(chunk(PB[:, 0, :], c), NBt[:, c, :], identT)
                mm.then_inc(n3T_mm.sem, 1)
                for p in range(4):
                    yield f"b.qk{p}"
                    if p == 0:
                        pe.wait_ge(xb_hi.sem, xb_hi.at(b, 1))
                        pe.wait_ge(xb_lo.sem, xb_lo.at(b, 1))
                        if later(b):
                            pe.wait_ge(w2_out.sem, w2_out.before(b))
                    for i in (2 * p, 2 * p + 1):
                        if i >= 3:
                            pe.wait_ge(qk_full.sem, qk_full.at(b, i - 2))
                        mm3(PB[:, 1 + i % 3, 0:NT], ws("qk", i), (XHb[:, :], XLb[:, :])).then_inc(qk_mm.sem, 1)
                yield "b.values"
                for c in range(CH):
                    mm = pe.matmul(tm(0, PB)[:, c, :], chunk(XFb, c), w("v"), start=True, stop=True)
                mm.then_inc(v_mm.sem, 1)
                for s in range(12):
                    yield f"b.s{s}"
                    if s == 0:
                        pe.wait_ge(v_out.sem, v_out.through(b))
                        pe.wait_ge(qk_full.sem, qk_full.through(b))
                    if s >= 2:
                        pe.wait_ge(s1_max.sem, s1_max.at(b, s - 1))
                    for u in (2 * s, 2 * s + 1):
                        h, c = divmod(u, CH)
                        if c == 0 and h % 2 == 0:
                            pe.wait_ge(q_out.sem, q_out.at(b, h // 2 + 1))
                            pe.wait_ge(k_out.sem, k_out.at(b, h // 2 + 1))
                        mm = pe.matmul(PB[0:TP, 2 * (s % 2) + u % 2, 0:NT], chunk(Q[:, h // 2, :], c), KZ[:, h, :],
                                       start=True, stop=True)
                    mm.then_inc(s1_mm.sem, 1)
                yield "b.maxT"
                pe.wait_ge(m_ready.sem, m_ready.through(b))
                for p in range(4):
                    for c in range(CH):
                        mm = pe.transpose(chunk(PB[:, p, :], c),
                                          M[:, c, 2 * p:2 * p + 2, :].rearrange("p h d -> p (h d)"), identT)
                    mm.then_inc(mT_mm.sem, 1)

                def scores_t(h):
                    for k in range(CH):
                        if h == 0:
                            pe.wait_ge(q2_out.sem, q2_out.at(b, k + 1))
                        else:
                            pe.wait_ge(exp1.sem, exp1.at(b, CH * (h - 1) + k + 1))
                        pe.matmul(PB[0:keys(k), k, 0:NT], chunk(KZ[:, h, :], k, keys(k)), Q2[:, h // 2, :],
                                  start=True, stop=True).then_inc(st_mm.sem, 1)

                def attend(q):
                    pe.wait_ge(exp1.sem, exp1.at(b, 4 * CH * (q + 1)))
                    if q == 0:
                        pe.wait_ge(q2_out.sem, q2_out.through(b))
                    else:
                        pe.wait_ge(ct_out.sem, ct_out.at(b, 1))
                    for k in range(CH):
                        for j in range(4):
                            mm = pe.matmul(PB[32 * j:32 * j + 32, 3, 0:NT], V[0:keys(k), k, 4 * q + j, :],
                                           ET[0:keys(k), 4 * q + j, k, :], start=(k == 0), stop=(k == CH - 1),
                                           skip_group_check=True)
                    mm.then_inc(av1_mm.sem, 1)

                for h in range(NH):
                    yield f"b.st{h}"
                    scores_t(h)
                    if h == 5:
                        yield "b.av0"
                        attend(0)
                yield "b.av1"
                attend(1)
                yield "b.ctx"
                for q in range(2):
                    pe.wait_ge(ct_out.sem, ct_out.at(b, q + 1))
                    for c in range(CH):
                        mm = pe.transpose(tm(q, PB)[:, c, :], chunk(CT[:, q, :], c), ident)
                    mm.then_inc(ctT_mm.sem, 1)
                yield "b.ctxT"
                pe.wait_ge(cn_ready.sem, cn_ready.through(b))
                for c in range(CH):
                    mm = pe.transpose(chunk(PB[:, 2, :], c), CN[:, c, :], identT)
                mm.then_inc(cnT_mm.sem, 1)
                yield "b.proj"
                pe.wait_ge(cnT_out.sem, cnT_out.through(b))
                for c in range(CH):
                    mm = pe.matmul(tm(3, PB)[:, c, :], chunk(CNT, c), w("out"), start=True, stop=True)
                mm.then_inc(out_mm.sem, 1)
            def pe_c(b):
                yield "c.turn2"
                pe.wait_ge(n3_ready.sem, n3_ready.at(b, 2))
                for c in range(CH):
                    mm = pe.transpose(chunk(PB[:, 0, :], c), NBt[:, c, :], identT)
                mm.then_inc(n3T_mm.sem, 1)
                yield "c.router"
                pe.wait_ge(xb_hi.sem, xb_hi.at(b, 2))
                for c in range(CH):
                    mm = pe.matmul(tm(1, PB)[:, c, :], chunk(XFb, c), w("router"), start=True, stop=True)
                mm.then_inc(rt_mm.sem, 1)

                def w1(t):
                    if t == 1:
                        pe.wait_ge(rt_in.sem, rt_in.through(b))
                    if t >= 2:
                        pe.wait_ge(gelu1.sem, gelu1.at(b, t - 1))
                    mm3(PB[:, t % 2, 0:NT], ws("w1", t), (XHb[:, :], XLb[:, :])).then_inc(w1_mm.sem, 1)

                def w2(e):
                    pe.wait_ge(gelu1.sem, gelu1.at(b, 2 * e + 2))
                    if e >= 2:
                        pe.wait_ge(w2_out.sem, w2_out.at(b, e))
                    for c in range(CH):
                        for j in range(2):
                            mm = pe.matmul(tm(W2_BANK[e], PB)[:, c, :], chunk(G1[:, (2 * e + j) % 4, :], c),
                                           w("w2", 2 * e + j), start=(j == 0), stop=(j == 1))
                    mm.then_inc(w2_mm.sem, 1)

                yield "c.first"
                pe.wait_ge(xb_lo.sem, xb_lo.at(b, 2))
                w1(0)
                w1(1)
                for e in range(E1):
                    yield f"c.e{e}"
                    if e + 1 < E1:
                        w1(2 * e + 2)
                        w1(2 * e + 3)
                    w2(e)
                    if e == 1:
                        yield "c.combT"
                        pe.wait_ge(w2_out.sem, w2_out.at(b, 1))
                        for c in range(CH):
                            mm = pe.transpose(chunk(PB[:, 2, :], c), CB[:, c, :], identT)
                        mm.then_inc(cbT_mm.sem, 1)
                    if e == 2:
                        yield "c.bias"
                        pe.wait_ge(cbT_out.sem, cbT_out.through(b))
                        for c in range(CH):
                            mm = pe.matmul(tm(2, PB)[:, c, :], chunk(CBT, c), w("b2"), start=True, stop=True)
                        mm.then_inc(b2_mm.sem, 1)

            pe.wait_ge(loaded.sem, 64)
            pe.wait_ge(weights_split.sem, 2)
            run_streams(pe, pe_a, pe_b, pe_c)

        @block.scalar
        def _(s):
            def act_a(b):
                yield "a.tanh"
                s.wait_ge(conv_done.sem, conv_done.through(b))
                s.wait_ge(tok_scale.sem, tok_scale.through(b))
                if later(b):
                    s.wait_ge(n1_ready.sem, n1_ready.before(b))
                for c in range(CH):
                    a = s.activation(TOK[:, c, :], tm(1, PA)[:, c, :], ACT.Tanh, scale=smA[:, 4, c:c + 1])
                a.then_inc(tanh_done.sem, 1)
                yield "a.turn1"
                s.wait_ge(n1T_done.sem, n1T_done.through(b))
                s.activation(XHa[:, :], PA[:, 2, 0:NT], ACT.Copy).then_inc(xa_hi.sem, 1)
                for j in range(4):
                    yield f"a.hid{j}"
                    s.wait_ge(k1_mm.sem, k1_mm.at(b, j + 1))
                    s.activation(K1[:, j, :], PA[:, j % 2, 0:NT], ACT.Relu, bias=col("bk1", j)).then_inc(k1_out.sem, 1)
                for n, (i, name) in enumerate(((1, "a.queries"), (0, "a.keys"))):
                    yield name
                    s.wait_ge(kq_mm.sem, kq_mm.at(b, n + 1))
                    s.activation(KQH[:, i, :], PA[:, i, 0:NT], ACT.Identity, bias=col("bk2", i)).then_inc(kq_hi.sem, 1)
                yield "a.exp"
                s.wait_ge(max0.sem, max0.through(b))
                for c in range(CH):
                    s.activation(EX[:, c, 0:L], PA[0:TP, c, 0:L], ACT.Exp, bias=smA[:, 5, c:c + 1],
                                 accum_out=smA[:, 6 + c, 0:1]).then_inc(exp0.sem, 1)
                yield "a.probsT"
                s.wait_ge(exT_mm.sem, exT_mm.at(b, 1))
                s.activation(EXT[:, 0, :], PA[0:TP, 0, 0:NT], ACT.Copy).then_inc(exT_out.sem, 1)
                s.wait_ge(exT_mm.sem, exT_mm.at(b, 3))
                s.activation(EXT[0:TLAST, 2, :], PA[0:TLAST, 2, 0:NT], ACT.Copy).then_inc(exT_out.sem, 1)
                yield "a.turn2"
                s.wait_ge(n2T_done.sem, n2T_done.at(b, 1))
                s.activation(XF[:, :], PA[:, 0, 0:NT], ACT.Copy).then_inc(xf_out.sem, 1)
                s.wait_ge(n2T_done.sem, n2T_done.at(b, 2))
                s.activation(NTt[:, :], PA[:, 1, 0:NT], ACT.Identity, bias=col("ln_b"), scale=col("ln_g"))\
                    .then_inc(nt_out.sem, 1)
                for j in range(4):
                    yield f"a.fc1_{j}"
                    s.wait_ge(fc1_mm.sem, fc1_mm.at(b, j + 1))
                    s.activation(G0[:, j, :], PA[:, (3 + j) % 4, 0:NT], ACT.Gelu,
                                 bias=FW[:, 2 * H0 + j:2 * H0 + j + 1]).then_inc(gelu0.sem, 1)
                yield "a.gelu"
                s.wait_ge(next_in.sem, next_in.through(b))
                s.activation(NG[:, :, :], NX[:, :, :], ACT.Gelu).then_inc(gelu_n.sem, 1)

            def act_b(b):
                yield "b.turn1"
                s.wait_ge(n3T_mm.sem, n3T_mm.at(b, 1))
                s.activation(XHb[:, :], PB[:, 0, 0:NT], ACT.Copy).then_inc(xb_hi.sem, 1)
                s.activation(XFb[:, :], PB[:, 0, 0:NT], ACT.Copy).then_inc(xb_full.sem, 1)
                for p in range(4):
                    yield f"b.qk{p}"
                    if p >= 2:
                        s.wait_ge(q_out.sem, q_out.at(b, p - 1))
                        s.wait_ge(k_out.sem, k_out.at(b, p - 1))
                    elif later(b):
                        s.wait_ge(q_out.sem, q_out.before(b))
                        s.wait_ge(k_out.sem, k_out.before(b))
                    for i in (2 * p, 2 * p + 1):
                        s.wait_ge(qk_mm.sem, qk_mm.at(b, i + 1))
                        s.activation(QKF[:, i % 4, :], PB[:, 1 + i % 3, 0:NT], ACT.Identity,
                                     bias=col("qkb", i)).then_inc(qk_full.sem, 1)

                def exps(h):
                    if h == 0 and later(b):
                        s.wait_ge(w2_mm.sem, w2_mm.before(b))
                    for k in range(CH):
                        n = TP if k < CH - 1 else TLAST
                        s.wait_ge(st_mm.sem, st_mm.at(b, CH * h + k + 1))
                        s.activation(ET[0:n, h, k, :], PB[0:n, k, 0:NT], ACT.Exp, scale=FACTOR).then_inc(exp1.sem, 1)

                def context(q):
                    s.wait_ge(av1_mm.sem, av1_mm.at(b, q + 1))
                    s.activation(CT[:, q, :], PB[:, 3, 0:NT], ACT.Copy).then_inc(ct_out.sem, 1)

                for h in range(NH):
                    yield f"b.st{h}"
                    exps(h)
                    if h == 5:
                        yield "b.av0"
                        context(0)
                yield "b.av1"
                context(1)
                yield "b.ctxT"
                s.wait_ge(cnT_mm.sem, cnT_mm.through(b))
                s.activation(CNT, PB[:, 2, 0:NT], ACT.Copy).then_inc(cnT_out.sem, 1)
            def act_c(b):
                yield "c.turn2"
                s.wait_ge(n3T_mm.sem, n3T_mm.at(b, 2))
                s.activation(XFb[:, :], PB[:, 0, 0:NT], ACT.Copy).then_inc(xb_full.sem, 1)
                s.activation(XHb[:, :], PB[:, 0, 0:NT], ACT.Copy).then_inc(xb_hi.sem, 1)
                yield "c.router"
                s.wait_ge(rt_in.sem, rt_in.through(b))
                s.activation(PRB[:, :, :], LG[:, :, :], ACT.Exp).then_inc(rt_exp.sem, 1)

                def gelu(t):
                    s.wait_ge(w1_mm.sem, w1_mm.at(b, t + 1))
                    if t >= 4:
                        s.wait_ge(w2_mm.sem, w2_mm.at(b, t // 2 - 1))
                    s.activation(G1[:, t % 4, :], PB[:, t % 2, 0:NT], ACT.Gelu, bias=col("b1", t))\
                        .then_inc(gelu1.sem, 1)

                yield "c.first"
                gelu(0)
                gelu(1)
                for e in range(E1 - 1):
                    yield f"c.e{e}"
                    gelu(2 * e + 2)
                    gelu(2 * e + 3)

            s.wait_ge(loaded.sem, 64)
            run_streams(s, act_a, act_b, act_c)

        @block.vector
        def _(v):
            def rsqrt(y, x, small, at, link):
                half, t = small[:, at, :], small[:, at + 1, :]
                v.tensor_scalar(half, x, -0.5, None, ALU.mult)
                link(v.tensor_scalar(t.bitcast(I32), x.bitcast(I32), 1, None, ALU.logical_shift_right))
                link(v.tensor_tensor(y.bitcast(I32), MAGIC[0:TP, :], t.bitcast(I32), ALU.subtract))
                for _ in range(3):
                    link(v.tensor_tensor(t, y, y, ALU.mult))
                    link(v.tensor_tensor(t, t, half, ALU.mult))
                    link(v.scalar_tensor_tensor(out=y, in0=t, scalar=1.5, in1=y, op0=ALU.add, op1=ALU.mult))

            def norm_stats(h, st, mv, small, link):
                for c in range(CH):
                    last = v.bn_stats(st[:, c, :], h[:, c, :])
                link(last)
                v.tensor_tensor(small[:, 15, 0:1], small[:, 15, 2:3], small[:, 15, 2:3], ALU.add)
                for c in range(CH):
                    last = v.bn_aggr(mv[:, c, :], st[:, c, :])
                link(last)
                link(v.tensor_scalar(small[:, 1, :], mv[:, :, 1], EPS_LN, None, ALU.add))
                rsqrt(small[:, 0, :], small[:, 1, :], small, 2, link)

            def dve_a(b):
                link = Chain(v, dveA, b)
                yield "a.window"
                v.wait_ge(wsq_done.sem, wsq_done.through(b))
                if later(b):
                    v.wait_ge(tanh_done.sem, tanh_done.before(b))
                link(v.tensor_scalar(smA[:, 1, :], tm(0, PA)[:, :, 0], 1e-30, None, ALU.max))
                rsqrt(smA[:, 0, :], smA[:, 1, :], smA, 2, link)
                link(v.tensor_tensor(smA[:, 0, :], smA[:, 0, :], smA[:, 1, :], ALU.mult))
                link(v.tensor_scalar(smA[:, 0, :], smA[:, 0, :], EPS_TOK, 1.0, ALU.add, ALU.max))
                link(v.reciprocal(smA[:, 1, :], smA[:, 0, :]))
                v.tensor_scalar(smA[:, 4, :], smA[:, 1, :], LAM_HALF, None, ALU.mult).then_inc(tok_scale.sem, 1)
                yield "a.norm1"
                v.wait_ge(tanh_done.sem, tanh_done.through(b))
                link(v.tensor_tensor(TOK[:, :, :], TOK[:, :, :], row3("tok_b"), ALU.add))
                link(v.tensor_scalar(HA[:, :, :], TOK[:, :, :], 0.0, None, ALU.max))
                norm_stats(HA, stA, mvA, smA, link)
                for c in range(CH):
                    last = v.tensor_scalar(NA[:, c, :], HA[:, c, :], mvA[:, c, 0:1], smA[:, 0, c:c + 1],
                                           ALU.subtract, ALU.mult)
                last.then_inc(n1_ready.sem, 1)
                yield "a.turn1"
                v.wait_ge(n1T_done.sem, n1T_done.through(b))
                v.wait_ge(xa_hi.sem, xa_hi.through(b))
                v.tensor_tensor(XLa[:, :], PA[:, 2, 0:NT], XHa[:, :], ALU.subtract).then_inc(xa_lo.sem, 1)
                for j in range(4):
                    yield f"a.hid{j}"
                    v.wait_ge(e1_mm.sem, e1_mm.at(b, j + 1))
                    v.tensor_scalar(E1t[:, j, :], PA[:, 3 - j % 2, 0:NT], col("be1", j), 0.0,
                                    ALU.add, ALU.max).then_inc(e1_out.sem, 1)
                for n, (i, name) in enumerate(((1, "a.queries"), (0, "a.keys"))):
                    yield name
                    v.wait_ge(kq_hi.sem, kq_hi.at(b, n + 1))
                    v.scalar_tensor_tensor(out=KQL[:, i, :], in0=PA[:, i, 0:NT], scalar=col("bk2", i),
                                           in1=KQH[:, i, :], op0=ALU.add, op1=ALU.subtract).then_inc(kq_lo.sem, 1)
                yield "a.emb"
                v.wait_ge(emb_mm.sem, emb_mm.through(b))
                v.tensor_tensor(EMB[:, :, :], tm(3, PA), row3("be2"), ALU.add).then_inc(emb_out.sem, 1)
                yield "a.scores"
                for c in range(CH):
                    v.wait_ge(s0_mm.sem, s0_mm.at(b, c + 1))
                    last = v.tensor_reduce(smA[:, 1, c:c + 1], PA[0:TP, c, 0:L], AX.X, ALU.max)
                link(last)
                v.tensor_scalar(smA[:, 5, :], smA[:, 1, :], -1.0, None, ALU.mult).then_inc(max0.sem, 1)
                yield "a.probsT"
                v.wait_ge(exT_mm.sem, exT_mm.at(b, 2))
                v.tensor_copy(EXT[:, 1, :], PA[0:TP, 1, 0:NT]).then_inc(exT_out.sem, 1)
                v.wait_ge(exp0.sem, exp0.through(b))
                link(v.reciprocal(smA[:, 9, :], smA[:, 6:9, 0:1].rearrange("p c o -> p (c o)")))
                yield "a.attend"
                v.wait_ge(av0_mm.sem, av0_mm.through(b))
                for c in range(CH):
                    last = v.scalar_tensor_tensor(out=HA[:, c, :], in0=tm(3, PA)[:, c, :], scalar=smA[:, 9, c:c + 1],
                                                  in1=HA[:, c, :], op0=ALU.mult, op1=ALU.add)
                link(last)
                norm_stats(HA, stA, mvA, smA, link)
                for c in range(CH):
                    last = v.tensor_scalar(NA[:, c, :], HA[:, c, :], mvA[:, c, 0:1], smA[:, 0, c:c + 1],
                                           ALU.subtract, ALU.mult)
                last.then_inc(n2_ready.sem, 1)
                yield "a.norm2"
                link(v.tensor_tensor(smA[:, 1, :], smA[:, 0, :], smA[:, 0, :], ALU.mult))
                link(v.tensor_tensor(smA[:, 1, :], smA[:, 1, :], mvA[:, :, 1], ALU.mult))
                link(v.tensor_scalar(smA[:, 1, :], smA[:, 1, :], EPS_LN, None, ALU.add))
                rsqrt(smA[:, 10, :], smA[:, 1, :], smA, 2, link)
                v.wait_ge(n2_ready.sem, n2_ready.at(b, 1))
                for c in range(CH):
                    last = v.tensor_scalar(NA2[:, c, :], NA[:, c, :], smA[:, 10, c:c + 1], None, ALU.mult)
                last.then_inc(n2_ready.sem, 1)
                yield "a.attn"
                v.wait_ge(at_mm.sem, at_mm.through(b))
                v.wait_ge(xf_out.sem, xf_out.through(b))
                link(v.scalar_tensor_tensor(out=XA[:, :], in0=PA[:, 2, 0:NT], scalar=col("attn_b"), in1=XF[:, :],
                                            op0=ALU.add, op1=ALU.add))
                v.tensor_copy(XHa[:, :], XA[:, :]).then_inc(xa_out.sem, 1)
                v.wait_ge(xa_out.sem, xa_out.at(b, 1))
                v.tensor_tensor(XLa[:, :], XA[:, :], XHa[:, :], ALU.subtract).then_inc(xa_out.sem, 1)
                yield "a.fc2"
                v.wait_ge(fc2_mm.sem, fc2_mm.through(b))
                v.tensor_scalar(Y0[:, :], PA[:, 3, 0:NT], FW[:, 2 * H0 + 4:2 * H0 + 5], None, ALU.add)\
                    .then_inc(y0_out.sem, 1)
                yield "a.last"
                v.wait_ge(next_mm.sem, next_mm.through(b))
                v.tensor_tensor(NX[:, :, :], tm(0, PA), row3("next_b"), ALU.add).then_inc(next_in.sem, 1)
                yield "a.result"
                v.wait_ge(gelu_n.sem, gelu_n.through(b))
                if later(b):
                    v.wait_ge(hm_ready.sem, hm_ready.before(b))
                v.tensor_tensor(HN[:, :, :], HA[:, :, :], NG[:, :, :], ALU.add).then_inc(hn_ready.sem, 1)
                link.end()

            def dve_b(b):
                link = Chain(v, dveB, b)

                def normalise(h):
                    norm_stats(h, stB, mvB, smB, link)
                    for c in range(CH):
                        last = v.tensor_scalar(NBt[:, c, :], h[:, c, :], mvB[:, c, 0:1], smB[:, 0, c:c + 1],
                                               ALU.subtract, ALU.mult)
                    last.then_inc(n3_ready.sem, 1)

                yield "b.norm1"
                v.wait_ge(hn_ready.sem, hn_ready.through(b))
                if later(b):
                    v.wait_ge(n3T_mm.sem, n3T_mm.before(b))
                normalise(HN)
                v.tensor_tensor(HM[:, :, :], HN[:, :, :], row3("out_b"), ALU.add).then_inc(hm_ready.sem, 1)
                yield "b.turn1"
                v.wait_ge(xb_full.sem, xb_full.at(b, 1))
                v.wait_ge(xb_hi.sem, xb_hi.at(b, 1))
                v.tensor_tensor(XLb[:, :], PB[:, 0, 0:NT], XHb[:, :], ALU.subtract).then_inc(xb_lo.sem, 1)
                for p in range(4):
                    yield f"b.qk{p}"
                    v.wait_ge(qk_round.sem, qk_round.at(b, 2 * p + 1))
                    for i in range(2):
                        r = slice(64 * i, 64 * i + 64)
                        last = v.scalar_tensor_tensor(out=KZ[r, 2 * p + i, :], in0=QKR[r, 2 * (p % 2) + 1, :],
                                                      scalar=col("kneg")[r, :], in1=QKF[r, 2 * (p % 2) + 1, :],
                                                      op0=ALU.mult, op1=ALU.add)
                    last.then_inc(k_out.sem, 1)
                yield "b.values"
                v.wait_ge(v_mm.sem, v_mm.through(b))
                v.tensor_tensor(V[:, :, :, 0:HD], tm(0, PB).rearrange("p c (h d) -> p c h d", h=NH),
                                row3("vb").rearrange("p c (h d) -> p c h d", h=NH), ALU.add).then_inc(v_out.sem, 1)
                for step in range(12):
                    yield f"b.s{step}"
                    v.wait_ge(s1_mm.sem, s1_mm.at(b, step + 1))
                    o = MX[:, :, :].rearrange("p h c -> p (h c)")[:, 2 * step:2 * step + 2]
                    v.tensor_reduce(o, PB[0:TP, 2 * (step % 2):2 * (step % 2) + 2, 0:L], AX.X, ALU.max)\
                        .then_inc(s1_max.sem, 1)
                yield "b.maxT"
                v.wait_ge(s1_max.sem, s1_max.through(b))
                v.tensor_scalar(M[:, :, :, 0], MX[:, :, :].rearrange("p h c -> p c h"), -1.0, None, ALU.mult)\
                    .then_inc(m_ready.sem, 1)
                for p in range(4):
                    v.wait_ge(mT_mm.sem, mT_mm.at(b, p + 1))
                    v.tensor_tensor(Q2[:, p, :], PB[:, p, 0:NT], Q[:, p, :], ALU.add).then_inc(q2_out.sem, 1)
                yield "b.ctx"
                v.wait_ge(ctT_mm.sem, ctT_mm.through(b))
                ct = [tm(q, PB).rearrange("p c (h d) -> p c h d", h=4) for q in range(2)]
                for q in range(2):
                    last = v.reciprocal(RD[:, :, 4 * q:4 * q + 4], ct[q][:, :, :, HD])
                link(last)
                for q in range(2):
                    last = v.tensor_tensor(
                        CN[:, :, 64 * q:64 * q + 64].rearrange("p c (h d) -> p c h d", h=4), ct[q][:, :, :, 0:HD],
                        RD[:, :, 4 * q:4 * q + 4].unsqueeze(3).to_broadcast([TP, CH, 4, HD]), ALU.mult)
                last.then_inc(cn_ready.sem, 1)
                yield "b.proj"
                v.wait_ge(out_mm.sem, out_mm.through(b))
                v.wait_ge(hm_ready.sem, hm_ready.through(b))
                if later(b):
                    v.wait_ge(stored.sem, stored.before(b))
                v.tensor_tensor(HB[:, :, :], tm(3, PB), HM[:, :, :], ALU.add).then_inc(hb_ready.sem, 1)
                v.wait_ge(hb_ready.sem, hb_ready.through(b))
                normalise(HB)
                link.end()

            def dve_c(b):
                link = Chain(v, dveC, b)
                yield "c.router"
                v.wait_ge(rt_mm.sem, rt_mm.through(b))
                link(v.tensor_tensor(LG[:, :, :], tm(1, PB)[:, :, 0:E1], row3("br"), ALU.add))
                link(v.tensor_reduce(smB[:, 5, :], LG[:, :, :], AX.X, ALU.max))
                v.tensor_tensor(LG[:, :, :], LG[:, :, :], smB[:, 5, :].unsqueeze(2).to_broadcast([TP, CH, E1]),
                                ALU.subtract).then_inc(rt_in.sem, 1)
                v.wait_ge(xb_full.sem, xb_full.at(b, 2))
                v.wait_ge(xb_hi.sem, xb_hi.at(b, 2))
                v.tensor_tensor(XLb[:, :], PB[:, 0, 0:NT], XHb[:, :], ALU.subtract).then_inc(xb_lo.sem, 1)
                yield "c.top2"
                v.wait_ge(rt_exp.sem, rt_exp.through(b))
                link(v.tensor_reduce(smB[:, 6, :], PRB[:, :, :], AX.X, ALU.add))
                link(v.reciprocal(smB[:, 7, :], smB[:, 6, :]))
                link(v.tensor_tensor(PRB[:, :, :], PRB[:, :, :],
                                     smB[:, 7, :].unsqueeze(2).to_broadcast([TP, CH, E1]), ALU.mult))
                mine = PRB[:, :, :].unsqueeze(3).to_broadcast([TP, CH, E1, E1])
                theirs = PRB[:, :, :].unsqueeze(2).to_broadcast([TP, CH, E1, E1])
                before = row("before").rearrange("p (e j) -> p e j", e=E1).unsqueeze(1)\
                    .to_broadcast([TP, CH, E1, E1])
                v.tensor_tensor(BEAT[:, :, :, :], theirs, mine, ALU.is_gt)
                link(v.tensor_tensor(TIE[:, :, :, :], theirs, mine, ALU.is_equal))
                link(v.tensor_tensor(TIE[:, :, :, :], TIE[:, :, :, :], before, ALU.mult))
                link(v.tensor_tensor(BEAT[:, :, :, :], BEAT[:, :, :, :], TIE[:, :, :, :], ALU.add))
                link(v.tensor_reduce(CNTB[:, :, :], BEAT[:, :, :, :], AX.X, ALU.add))
                link(v.scalar_tensor_tensor(out=CB[:, :, 0:E1], in0=CNTB[:, :, :], scalar=1.5, in1=PRB[:, :, :],
                                            op0=ALU.is_lt, op1=ALU.mult))
                for e in range(E1):
                    yield f"c.e{e}"
                    v.wait_ge(w2_mm.sem, w2_mm.at(b, e + 1))
                    if e > 0:
                        v.wait_ge(w2_out.sem, w2_out.at(b, e if e < 3 else e + 1))
                    for c in range(CH):
                        last = v.scalar_tensor_tensor(out=HB[:, c, :], in0=tm(W2_BANK[e], PB)[:, c, :],
                                                      scalar=CB[:, c, e:e + 1], in1=HB[:, c, :],
                                                      op0=ALU.mult, op1=ALU.add)
                    last.then_inc(w2_out.sem, 1)
                    if e == 1:
                        yield "c.combT"
                        v.wait_ge(cbT_mm.sem, cbT_mm.through(b))
                        v.tensor_copy(CBT, PB[:, 2, 0:NT]).then_inc(cbT_out.sem, 1)
                    if e == 2:
                        yield "c.bias"
                        v.wait_ge(b2_mm.sem, b2_mm.through(b))
                        v.wait_ge(w2_out.sem, w2_out.at(b, 3))
                        v.tensor_tensor(HB[:, :, :], tm(2, PB), HB[:, :, :], ALU.add).then_inc(w2_out.sem, 1)
                link.end()

            v.wait_ge(loaded.sem, 64)
            v.wait_ge(zeros_set.sem, 2)
            v.memset(smA[:, 15, :], 0.0)
            v.memset(smB[:, 15, :], 0.0)
            v.tensor_copy(WH[:, :], WS).then_inc(weights_split.sem, 1)
            v.wait_ge(weights_split.sem, 1)
            v.tensor_tensor(WL[:, :], WS, WH[:, :], ALU.subtract).then_inc(weights_split.sem, 1)
            run_streams(v, dve_a, dve_b, dve_c)


_INS = ["x", "weights", "split_w", "cols", "rows", "ffw"]


def lay_out(i):
    f = np.float32
    a = {k: np.asarray(v) for k, v in i.items()}

    def blocks(m):
        n = m.shape[0] // 128
        return m.reshape(n, 128, -1).transpose(1, 0, 2).reshape(128, -1)

    def wide(m):
        o = np.zeros((m.shape[0], 128), f)
        o[:, :m.shape[1]] = m
        return o

    x = np.zeros((NB, CIN, XPAD), f)
    x[:, :, :L_IN] = a["x"].transpose(0, 2, 1)
    conv = np.zeros((TAPS + 1, CIN, D), f)
    conv[:TAPS] = a["L0_tok_kernel"]
    b2 = np.zeros((128, D), f)
    b2[:E1] = a["L1_ffn_b2"]
    qkv = a["L1_attn_qkv_w"].reshape(NH, 3, HD, D)
    qkv_b = a["L1_attn_qkv_b"].reshape(NH, 3, HD)
    parts = {
        "conv": blocks(conv.reshape(-1, D)),
        "k2": blocks(a["L0_attn_Wk2"].T), "e2": blocks(a["L0_attn_We2"].T),
        "attn": a["L0_ffn_attn_w"].T, "next": a["L0_ffn_next_w"].T,
        "v": qkv[:, 2].reshape(NH * HD, D).T, "out": a["L1_attn_out_w"].T,
        "router": wide(a["L1_ffn_Wr"].T), "b2": b2,
        "w2": blocks(a["L1_ffn_W2"].reshape(E1 * H1, D)),
        "ident": np.eye(128, dtype=f), "ones": np.ones((128, 128), f),
    }
    qk = np.zeros((D, 4, 2, 2, 4, HD), f)
    qkb = np.zeros((4, 2, 2, 4, HD), f)
    for h in range(NH):
        for s in range(2):
            for blk in range(1, 4):
                qk[:, h // 2, s, h % 2, blk] = qkv[h, s].T
                qkb[h // 2, s, h % 2, blk] = qkv_b[h, s]
    qkb[:, 1, :, 0, 0] = 1.0
    neg = np.zeros((2, 2, 4, HD), f)
    neg[0, :, 3], neg[1, :, 2] = -1.0, -1.0
    split = {"k1": a["L0_attn_Wk1"].T, "e1": a["L0_attn_We1"].T, "qk": qk.reshape(D, -1),
             "w1": a["L1_ffn_W1"].transpose(1, 0, 2).reshape(D, -1)}
    cols = {"bk1": a["L0_attn_bk1"].reshape(4, 128).T, "be1": a["L0_attn_be1"].reshape(4, 128).T,
            "bk2": a["L0_attn_bk2"].reshape(2, 128).T, "ln_g": a["L0_ffn_ln_g"][:, None],
            "ln_b": a["L0_ffn_ln_b"][:, None], "attn_b": a["L0_ffn_attn_b"][:, None],
            "qkb": qkb.reshape(8, 128).T, "b1": a["L1_ffn_b1"].reshape(16, 128).T,
            "qneg": neg[0].reshape(128, 1), "kneg": neg[1].reshape(128, 1)}
    before = np.tril(np.ones((E1, E1), f), -1)
    rows = {"tok_b": a["L0_tok_bias"], "be2": a["L0_attn_be2"], "next_b": a["L0_ffn_next_b"],
            "vb": qkv_b[:, 2].reshape(-1), "out_b": a["L1_attn_out_b"], "br": a["L1_ffn_br"],
            "before": before.reshape(-1)}
    ffw = np.zeros((E0, 128, FFW), f)
    ffw[:, :, 0:H0] = a["L0_ffn_fc1_w"].transpose(0, 2, 1)
    ffw[:, :, H0:2 * H0] = a["L0_ffn_fc2_w"].transpose(0, 2, 1).reshape(E0, 4, 128, D).transpose(0, 2, 1, 3)\
        .reshape(E0, 128, 4 * D)
    ffw[:, :, 2 * H0:2 * H0 + 4] = a["L0_ffn_fc1_b"].reshape(E0, 4, 128).transpose(0, 2, 1)
    ffw[:, :, 2 * H0 + 4] = a["L0_ffn_fc2_b"]
    row = np.concatenate([rows[n] for n, _ in ROWS])
    return {
        "x": x, "ffw": ffw,
        "weights": np.concatenate([parts[n] for n, _ in WEIGHTS], 1),
        "split_w": np.concatenate([split[n] for n, _ in SPLIT], 1),
        "cols": np.concatenate([cols[n] for n, _ in COLS], 1),
        "rows": np.ascontiguousarray(np.broadcast_to(row, (128, R_N))),
    }


def kernel(**inputs):
    import concourse.bacc as bacc
    from concourse.bass_utils import run_bass_kernel_spmd

    nc = bacc.Bacc("TRN2", target_bir_lowering=False, num_devices=1)
    arrays, args = {}, []
    for name, value in lay_out(inputs).items():
        value = np.ascontiguousarray(value)
        arrays[f"in_{name}"] = value
    for name in _INS:
        value = arrays[f"in_{name}"]
        args.append(nc.dram_tensor(f"in_{name}", value.shape, mybir.dt.from_np(value.dtype), kind="ExternalInput").ap())
    out = nc.dram_tensor("out_0", (NB, L, D), F32, kind="ExternalOutput").ap()
    tower_kernel(nc, *args, out)
    r = run_bass_kernel_spmd(nc, [arrays], core_ids=[0])
    return r.results[0]["out_0"]
```

```python
from contextlib import ExitStack

import numpy as np

import concourse.bass as bass
from concourse import mybir

F32 = mybir.dt.float32
F32R = mybir.dt.float32r
I32 = mybir.dt.int32
ALU = mybir.AluOpType
ACT = mybir.ActivationFunctionType
AX = mybir.AxisListType

NB, L_IN, CIN = 32, 375, 64
TAPS = 9
L = L_IN - TAPS + 1
D = 128
CH, TP = 3, 124
NT = CH * TP
TLAST = L - 2 * TP
XW = NT + TAPS + 1
XPAD = XW + 2
NPAIR = (TAPS + 1) // 2
NH, HD = 8, 16
E0, H0 = 8, 512
E1, H1 = 8, 256
EPS_LN = 1e-5
EPS_TOK = 1e-7
ET_HEADS = 6
AV_BANK = (2, 0)
LAM_HALF = 1.0 / (1.0 + 1e-7)
FACTOR = HD ** -0.5

WEIGHTS = [("conv", NPAIR * D), ("ident", D), ("ones", D), ("k2", 4 * 2 * D), ("e2", 4 * D), ("attn", D),
           ("next", D), ("v", D), ("out", D), ("router", D), ("b2", D), ("w2", E1 * 2 * D)]
SPLIT = [("k1", 512), ("e1", 512), ("qk", 8 * D), ("w1", E1 * H1)]
COLS = [("bk1", 4), ("be1", 4), ("bk2", 2), ("ln_g", 1), ("ln_b", 1), ("attn_b", 1), ("qkb", 8), ("b1", 16),
        ("qneg", 1), ("kneg", 1)]
ROWS = [("tok_b", D), ("be2", D), ("next_b", D), ("vb", D), ("out_b", D), ("br", E1), ("before", E1 * E1)]
FFW = H0 + H0 + 4 + 1


def offsets(parts):
    at, n = {}, 0
    for name, width in parts:
        at[name] = (n, n + width)
        n += width
    return at, n


W_AT, W_N = offsets(WEIGHTS)
S_AT, S_N = offsets(SPLIT)
C_AT, C_N = offsets(COLS)
R_AT, R_N = offsets(ROWS)

ORDER = {
    "gpsimd": """
        a.window a.split_fc1 b.qk0 b.qk1 b.qk2 b.qk3
    """.split(),
    "tensor": """
        a.window c.turn2 c.router a.conv a.conv/1 c.first a.conv/2 b.turn1 b.qk0 b.qk0/k b.qk1 c.combT b.qk1/k
        b.qk2 b.qk2/k b.qk3 c.bias c.p0 b.qk3/k c.e0 c.e0/1 c.e0/2 c.q0 b.values c.p1 c.e1 c.e1/1 a.turn1 c.e1/2
        c.q1 b.s0 b.s0/1 a.hid0 a.hid0/e a.hid1 a.hid1/e a.hid2 b.s1 a.hid2/e b.s1/1 c.p2 b.s2 b.s2/1 a.hid3
        b.s3 c.e2 b.s3/1 a.hid3/e b.s4 b.s4/1 c.e2/1 b.s5 a.queries b.s5/1 b.s6 a.queries/1 b.s6/1 b.s7
        a.queries/2 b.s7/1 b.s8 a.queries/3 b.s8/1 c.e2/2 b.s9 b.s9/1 a.keys b.s10 c.q2 b.s10/1 a.keys/1 b.s11
        b.s11/1 a.keys/2 c.p3 a.keys/3 b.maxT a.emb b.st0 b.st0/1 b.st0/2 a.emb/1 b.st1 b.st1/1 b.st1/2 a.emb/2
        b.st2 b.st2/1 b.st2/2 a.scores b.st3 b.st3/1 c.e3 b.st3/2 c.e3/1 b.st4 c.e3/2 b.st4/1 c.q3 a.probsT
        b.st4/2 b.st5 b.st5/1 c.p4 a.attend a.attend/1 a.attend/2 b.st5/2 b.av0 b.av0/1 c.e4 b.av0/2 b.st6
        c.e4/1 b.st6/1 b.st6/2 c.e4/2 b.st7 b.st7/1 b.st7/2 c.q4 c.p5 b.av1 b.av1/1 a.turn2 b.av1/2 c.e5 a.attn
        b.ctx c.e5/1 c.e5/2 c.q5 a.fc1_0 a.fc1_1 b.ctxT a.fc1_2 a.fc1_3 b.proj c.p6 a.fc2 a.fc2/1 a.fc2/2
        a.fc2/3 c.e6 c.e6/1 c.e6/2 c.q6 a.last c.e7 c.e7/1 c.e7/2
    """.split(),
    "scalar": """
        c.turn2 c.top2 c.first b.turn1 a.tanh b.qk0 b.qk0/k b.qk1 b.qk1/k b.qk2 c.p0 b.qk2/k b.qk3 c.q0 c.p1
        b.qk3/k a.turn1 c.q1 a.hid0 a.hid0/e a.hid1 a.hid1/e a.hid2 a.hid2/e a.hid3 a.hid3/e c.p2 c.q2 a.queries
        a.keys c.p3 b.st0 b.st0/1 b.st0/2 b.st1 b.st1/1 b.st1/2 b.st2 b.st2/1 b.st2/2 b.st3 b.st3/1 a.exp
        b.st3/2 b.st4 b.st4/1 a.probsT a.probsT/2 b.st4/2 b.st5 b.st5/1 c.q3 c.p4 b.st5/2 b.av0 b.st6 b.st6/1
        b.st6/2 b.st7 b.st7/1 b.st7/2 c.q4 c.p5 a.turn2 a.turn2/1 b.av1 a.fc1_0 b.ctxT c.q5 a.fc1_1 a.fc1_2
        a.fc1_3 c.p6 c.q6 a.gelu
    """.split(),
    "vector": """
        a.window a.root b.norm1 a.root.0 b.rstd1 c.router b.rstd1.0 c.x_low b.rstd1.1 a.root.1 b.rstd1.2
        a.root.2 b.scale1 a.clamp b.bias c.top2 b.turn1 c.rank a.norm1 c.combT b.qk0 a.rstd1 c.bias a.rstd1.0
        b.qk1 a.rstd1.1 c.e0 a.rstd1.2 a.scale1 b.qk2 a.turn1 c.e1 b.qk3 b.values b.s0 b.s0/1 b.s1 b.s1/1 b.s2
        b.s2/1 b.s3 b.s3/1 b.s4 b.s4/1 b.s5 b.s5/1 b.s6 b.s6/1 b.s7 b.s7/1 b.s8 b.s8/1 b.s9 b.s9/1 b.s10 c.e2
        b.s10/1 b.s11 b.s11/1 b.maxT b.maxT/0 b.maxT/1 b.maxT/2 b.maxT/3 a.queries a.keys a.emb a.scores
        a.scores/1 a.scores/2 c.e3 a.probsT a.recip a.attend a.moments2 a.rstd2 a.rstd2.0 a.rstd2.1 c.e4
        a.rstd2.2 a.scale2 a.scale3 a.attn b.ctx c.e5 b.proj b.norm2 b.rstd2 b.rstd2.0 a.fc2 b.rstd2.1 b.rstd2.2
        c.e6 a.last b.scale2 a.result c.e7
    """.split(),
}


class Signal:

    def __init__(self, sem, per):
        self.sem, self.per = sem, per

    def at(self, b, count):
        return b * self.per + count

    def through(self, b):
        return b * self.per + self.per

    def before(self, b):
        return b * self.per


def later(b):
    return not (isinstance(b, int) and b == 0)


def weave(order, a=None, b=None, c=None):
    streams = {"a": a, "b": b, "c": c}
    ahead = {k: next(v, None) if v is not None else None for k, v in streams.items()}
    for step in order:
        while ahead[step[0]] == step:
            ahead[step[0]] = next(streams[step[0]], None)
    assert set(ahead.values()) == {None}, ahead


def nothing(b):
    yield from ()


def tower_kernel(nc, x, weights, split_w, cols, rows, ffw, out):
    with ExitStack() as ctx:
        def sb(name, shape, dt=F32):
            return ctx.enter_context(nc.sbuf_tensor(name, shape, dt))

        def signal(name, per):
            return Signal(ctx.enter_context(nc.semaphore(name)), per)

        W = sb("W", [128, W_N])
        WH = sb("WH", [128, S_N], F32R)
        WL = sb("WL", [128, S_N], F32R)
        C = sb("C", [128, C_N])
        ROW = sb("ROW", [128, R_N])
        GATE = sb("GATE", [128, 16])
        MAGIC = sb("MAGIC", [128, 6], I32)

        def w(name, i=0, width=D):
            lo = W_AT[name][0] + i * width
            return W[:, lo:lo + width]

        def ws(name, i):
            lo = S_AT[name][0] + i * D
            return WH[:, lo:lo + D], WL[:, lo:lo + D]

        def col(name, i=0):
            return C[:, C_AT[name][0] + i:C_AT[name][0] + i + 1]

        def row(name):
            return ROW[0:TP, R_AT[name][0]:R_AT[name][1]]

        def row3(name):
            return row(name).unsqueeze(1).to_broadcast([TP, CH, R_AT[name][1] - R_AT[name][0]])

        ident = w("ident")
        identT = ident[0:TP, 0:TP]

        XX = sb("XX", [128, XW])
        FW = sb("FW", [128, FFW])
        F1H = sb("F1H", [128, H0], F32R)
        F1L = sb("F1L", [128, H0], F32R)
        smA = sb("smA", [TP, 20, CH])
        stA = sb("stA", [TP, CH, 6])
        mvA = sb("mvA", [TP, CH, 2])
        TOK = sb("TOK", [TP, CH, D])
        HA = sb("HA", [TP, CH, D])
        NA = sb("NA", [TP, CH, D])
        NA2 = TOK
        XHa = sb("XHa", [128, NT], F32R)
        XLa = sb("XLa", [128, NT], F32R)
        K1 = sb("K1", [128, 4, NT])
        E1t = sb("E1t", [128, 4, NT])
        KQH = sb("KQH", [128, 2, NT], F32R)
        KQL = sb("KQL", [128, 2, NT], F32R)
        EMB = sb("EMB", [TP, CH, D])
        EX = sb("EX", [TP, CH, NT])
        EXT = E1t[0:TP, 0:CH, :]
        window = E1t[:, :, :].rearrange("p j t -> p (j t)")
        SQ, S4, S8 = (window[:, i * XW:(i + 1) * XW] for i in range(3))
        XF = sb("XF", [128, NT])
        NTt = sb("NTt", [128, NT])
        XA = sb("XA", [128, NT])
        G0 = K1
        Y0 = XF
        NX = sb("NX", [TP, CH, D])
        NG = NX
        HN = sb("HN", [TP, CH, D])

        smB = sb("smB", [TP, 16, CH])
        stB = sb("stB", [TP, CH, 6])
        mvB = sb("mvB", [TP, CH, 2])
        NBt = sb("NBt", [TP, CH, D])
        XFb = sb("XFb", [128, NT])
        XHb = sb("XHb", [128, NT], F32R)
        XLb = sb("XLb", [128, NT], F32R)
        QKF = sb("QKF", [128, 4, NT])
        QKR = sb("QKR", [128, 4, NT], F32R)
        Q = sb("Q", [128, 4, NT], F32R)
        Q2 = sb("Q2", [128, 4, NT], F32R)
        KZ = sb("KZ", [128, NH, NT], F32R)
        V = sb("V", [TP, CH, NH, 32])
        MX = sb("MX", [TP, NH, CH])
        M = sb("M", [TP, CH, NH, 64])
        ET = sb("ET", [128, ET_HEADS, CH, NT])
        WS = ET[:, :, :, :].rearrange("p h c t -> p (h c t)")[:, 0:S_N]
        CT = sb("CT", [128, 2, NT])
        RD = sb("RD", [TP, CH, NH])
        CN = sb("CN", [TP, CH, D])
        CNT = CT[:, 0, :]
        HM = sb("HM", [TP, CH, D])
        HB = sb("HB", [TP, CH, D])

        HC = sb("HC", [TP, CH, D])
        XFc = sb("XFc", [128, NT])
        XHc = sb("XHc", [128, NT], F32R)
        XLc = sb("XLc", [128, NT], F32R)
        G1 = sb("G1", [128, 4, NT])
        CBT = XFc[:, :]
        LG = sb("LG", [TP, CH, E1])
        PRB = sb("PRB", [TP, CH, E1])
        BEAT = sb("BEAT", [TP, CH, E1, E1])
        TIE = sb("TIE", [TP, CH, E1, E1])
        CNTB = sb("CNTB", [TP, CH, E1])
        CB = sb("CB", [TP, CH, D])

        PA = ctx.enter_context(nc.psum_tensor("PA", [128, 3, 512], F32))
        PB = ctx.enter_context(nc.psum_tensor("PB", [128, 3, 512], F32))
        PC = ctx.enter_context(nc.psum_tensor("PC", [128, 2, 512], F32))

        def tm(bank, P):
            return P[0:TP, bank, 0:CH * D].rearrange("p (c d) -> p c d", c=CH)

        def chunk(tile, c, n=TP):
            return tile[:, c * TP:c * TP + n]

        first_loaded = signal("first_loaded", 48)
        split_loaded = signal("split_loaded", 16)
        loaded = signal("loaded", 16)
        weights_split = signal("weights_split", 1)
        zeros_set = signal("zeros_set", 1)
        x_loaded = signal("x_loaded", 32)
        ffw_loaded = signal("ffw_loaded", 16)
        window_sums = signal("window_sums", 1)
        poolA = signal("poolA", 4)
        wsq_done = signal("wsq_done", 1)
        conv_done = signal("conv_done", 1)
        tok_scale = signal("tok_scale", 1)
        tanh_done = signal("tanh_done", 1)
        dveA = signal("dveA", 50)
        n1_ready = signal("n1_ready", 1)
        n1T_done = signal("n1T_done", 1)
        xa_hi = signal("xa_hi", 1)
        xa_lo = signal("xa_lo", 1)
        k1_mm = signal("k1_mm", 4)
        e1_mm = signal("e1_mm", 4)
        k1_out = signal("k1_out", 4)
        e1_out = signal("e1_out", 4)
        kq_mm = signal("kq_mm", 2)
        kq_hi = signal("kq_hi", 2)
        kq_lo = signal("kq_lo", 2)
        emb_mm = signal("emb_mm", 1)
        emb_out = signal("emb_out", 1)
        s0_mm = signal("s0_mm", 3)
        max0 = signal("max0", 1)
        exp0 = signal("exp0", 3)
        exT_mm = signal("exT_mm", 3)
        exT_out = signal("exT_out", 3)
        av0_mm = signal("av0_mm", 1)
        n2_ready = signal("n2_ready", 2)
        n2T_done = signal("n2T_done", 2)
        xf_out = signal("xf_out", 1)
        nt_out = signal("nt_out", 1)
        at_mm = signal("at_mm", 1)
        xa_out = signal("xa_out", 2)
        f1_split = signal("f1_split", 1)
        fc1_mm = signal("fc1_mm", 4)
        gelu0 = signal("gelu0", 4)
        fc2_mm = signal("fc2_mm", 1)
        y0_out = signal("y0_out", 1)
        next_mm = signal("next_mm", 1)
        next_in = signal("next_in", 1)
        gelu_n = signal("gelu_n", 1)
        hn_ready = signal("hn_ready", 1)
        dveB = signal("dveB", 29)
        dveC = signal("dveC", 9)
        n3_ready = signal("n3_ready", 2)
        n3T_mm = signal("n3T_mm", 2)
        xb_hi = signal("xb_hi", 1)
        xb_lo = signal("xb_lo", 1)
        xb_full = signal("xb_full", 1)
        xc_hi = signal("xc_hi", 1)
        xc_lo = signal("xc_lo", 1)
        xc_full = signal("xc_full", 1)
        cb_ready = signal("cb_ready", 1)
        qk_mm = signal("qk_mm", 8)
        qk_full = signal("qk_full", 8)
        qk_round = signal("qk_round", 8)
        q_signed = signal("q_signed", 4)
        q_out = signal("q_out", 4)
        k_out = signal("k_out", 4)
        v_mm = signal("v_mm", 1)
        v_out = signal("v_out", 1)
        s1_mm = signal("s1_mm", 24)
        s1_max = signal("s1_max", 24)
        m_ready = signal("m_ready", 1)
        mT_mm = signal("mT_mm", 4)
        q2_out = signal("q2_out", 4)
        st_mm = signal("st_mm", 24)
        exp1 = signal("exp1", 24)
        av1_mm = signal("av1_mm", 2)
        ct_out = signal("ct_out", 2)
        ctT_mm = signal("ctT_mm", 2)
        cn_ready = signal("cn_ready", 1)
        cnT_mm = signal("cnT_mm", 1)
        cnT_out = signal("cnT_out", 1)
        out_mm = signal("out_mm", 1)
        hm_ready = signal("hm_ready", 1)
        hb_ready = signal("hb_ready", 1)
        rt_mm = signal("rt_mm", 1)
        rt_in = signal("rt_in", 1)
        rt_exp = signal("rt_exp", 1)
        cbT_mm = signal("cbT_mm", 1)
        cbT_out = signal("cbT_out", 1)
        b2_mm = signal("b2_mm", 1)
        w1_mm = signal("w1_mm", 16)
        gelu1 = signal("gelu1", 16)
        w2_mm = signal("w2_mm", 8)
        w2_out = signal("w2_out", 9)
        stored = signal("stored", 32)

        class Chain:

            def __init__(self, eng, sig, b):
                self.eng, self.sig, self.b, self.n = eng, sig, b, 0

            def mark(self, ins):
                self.n += 1
                ins.then_inc(self.sig.sem, 1)

            def wait(self):
                self.eng.wait_ge(self.sig.sem, self.b * self.sig.per + self.n)

            def __call__(self, ins):
                self.mark(ins)
                self.wait()

            def end(self):
                assert self.n == self.sig.per, (self.n, self.sig.per)

        def run_streams(eng, order, stream_a, stream_b, stream_c):
            weave(order, stream_a(0))
            weave(order, stream_a(1), stream_b(0))
            with eng.Fori(2, NB) as b:
                weave(order, stream_a(b), stream_b(b - 1), stream_c(b - 2))
            weave(order, None, stream_b(NB - 1), stream_c(NB - 2))
            weave(order, None, None, stream_c(NB - 1))

        block = ctx.enter_context(nc.Block())

        @block.sync
        def _(sp):
            def load_x(b):
                if later(b):
                    sp.wait_ge(conv_done.sem, conv_done.before(b))
                    sp.wait_ge(window_sums.sem, window_sums.before(b))
                sp.dma_start(XX[0:CIN, :], x[b, :, 0:XW]).then_inc(x_loaded.sem, 16)
                sp.dma_start(XX[CIN:128, :], x[b, :, 1:XW + 1]).then_inc(x_loaded.sem, 16)

            def load_ffw(b):
                if later(b):
                    sp.wait_ge(y0_out.sem, y0_out.before(b))
                    sp.wait_ge(f1_split.sem, f1_split.before(b))
                sp.dma_start(FW[:, :], ffw[(b // 2) % E0]).then_inc(ffw_loaded.sem, 16)

            def store(b):
                sp.wait_ge(w2_out.sem, w2_out.through(b))
                sp.dma_start(out[b, 0:2 * TP, :].rearrange("(c p) d -> p c d", c=2),
                             HC[:, 0:2, :]).then_inc(stored.sem, 16)
                sp.dma_start(out[b, 2 * TP:L, :], HC[0:TLAST, 2, :]).then_inc(stored.sem, 16)

            first = W_AT["ones"][1]
            load_x(0)
            sp.dma_start(W[:, 0:first], weights[:, 0:first]).then_inc(first_loaded.sem, 16)
            sp.dma_start(C[:, :], cols).then_inc(first_loaded.sem, 16)
            sp.dma_start(ROW[:, :], rows).then_inc(first_loaded.sem, 16)
            sp.dma_start(WS, split_w).then_inc(split_loaded.sem, 16)
            sp.dma_start(W[:, first:], weights[:, first:]).then_inc(loaded.sem, 16)
            load_ffw(0)
            load_x(1)
            load_ffw(1)
            load_x(2)
            load_ffw(2)
            with sp.Fori(2, NB - 1) as b:
                load_x(b + 1)
                store(b - 2)
                load_ffw(b + 1)
            store(NB - 3)
            store(NB - 2)
            store(NB - 1)
            sp.wait_ge(stored.sem, NB * stored.per)

        @block.gpsimd
        def _(g):
            def gate(i):
                g.tensor_tensor(GATE[:, i:i + 1], GATE[:, 15:16], GATE[:, 15:16], ALU.add)

            def pool_a(b):
                link = Chain(g, poolA, b)
                yield "a.window"
                g.wait_ge(x_loaded.sem, x_loaded.through(b))
                if later(b):
                    g.wait_ge(av0_mm.sem, av0_mm.before(b))
                link(g.tensor_tensor(SQ[:, :], XX[:, :], XX[:, :], ALU.mult))
                link(g.tensor_tensor(S4[:, 0:NT + 4], SQ[:, 0:NT + 4], SQ[:, 2:NT + 6], ALU.add))
                link(g.tensor_tensor(S8[:, 0:NT], S4[:, 0:NT], S4[:, 4:NT + 4], ALU.add))
                g.tensor_tensor(S8[0:CIN, 0:NT], S8[0:CIN, 0:NT], SQ[0:CIN, 8:NT + 8],
                                ALU.add).then_inc(window_sums.sem, 1)
                yield "a.split_fc1"
                g.wait_ge(ffw_loaded.sem, ffw_loaded.through(b))
                if later(b):
                    g.wait_ge(fc1_mm.sem, fc1_mm.before(b))
                gate(8)
                link(g.tensor_scalar(F1H[:, :], FW[:, 0:H0], 1.0, 0.0, ALU.mult, ALU.add))
                g.tensor_tensor(F1L[:, :], FW[:, 0:H0], F1H[:, :], ALU.subtract).then_inc(f1_split.sem, 1)
                link.end()

            def pool_b(b):
                for p in range(4):
                    yield f"b.qk{p}"
                    full, rounded = QKF[:, 2 * (p % 2):2 * (p % 2) + 2, :], QKR[:, 2 * (p % 2):2 * (p % 2) + 2, :]
                    g.wait_ge(qk_full.sem, qk_full.at(b, 2 * p + 2))
                    if p >= 2:
                        g.wait_ge(k_out.sem, k_out.at(b, p - 1))
                    elif later(b):
                        g.wait_ge(k_out.sem, k_out.before(b))
                    gate(2 * p)
                    g.tensor_scalar(rounded[:, 1, :], full[:, 1, :], 1.0, 0.0, ALU.mult,
                                    ALU.add).then_inc(qk_round.sem, 1)
                    g.tensor_scalar(rounded[:, 0, :], full[:, 0, :], 1.0, 0.0, ALU.mult,
                                    ALU.add).then_inc(qk_round.sem, 1)
                    g.wait_ge(qk_round.sem, qk_round.at(b, 2 * p + 2))
                    if later(b):
                        g.wait_ge(q2_out.sem, q2_out.before(b))
                    gate(2 * p + 1)
                    g.tensor_scalar(rounded[:, 0, :], rounded[:, 0, :], col("qneg"), 0.0, ALU.mult,
                                    ALU.add).then_inc(q_signed.sem, 1)
                    g.wait_ge(q_signed.sem, q_signed.at(b, p + 1))
                    g.tensor_tensor(Q[:, p, :], rounded[:, 0, :], full[:, 0, :], ALU.add).then_inc(q_out.sem, 1)

            g.memset(KZ[:, :, :].bitcast(F32), 0.0)
            g.memset(V[:, :, :, HD:32], 0.0)
            g.memset(M[:, :, :, :], 0.0)
            g.memset(CB[:, :, :], 0.0)
            g.memset(GATE[:, :], 0.0)
            g.memset(MAGIC[:, :], 0x5F3759DF).then_inc(zeros_set.sem, 1)
            g.wait_ge(zeros_set.sem, 1)
            g.memset(V[:, :, :, HD:HD + 1], 1.0).then_inc(zeros_set.sem, 1)
            g.wait_ge(first_loaded.sem, 48)
            run_streams(g, ORDER["gpsimd"], pool_a, pool_b, nothing)

        @block.tensor
        def _(pe):
            def mm3(o, wt, xt):
                pe.matmul(o, wt[0], xt[0], start=True, stop=False)
                pe.matmul(o, wt[0], xt[1], start=False, stop=False)
                return pe.matmul(o, wt[1], xt[0], start=False, stop=True)

            def keys(k):
                return TP if k < CH - 1 else TLAST

            def pe_a(b):
                yield "a.window"
                pe.wait_ge(window_sums.sem, window_sums.through(b))
                if later(b):
                    pe.wait_ge(next_in.sem, next_in.before(b))
                for c in range(CH):
                    mm = pe.matmul(tm(0, PA)[:, c, :], chunk(S8, c), w("ones"), start=True, stop=True)
                mm.then_inc(wsq_done.sem, 1)
                yield "a.conv"
                pe.wait_ge(x_loaded.sem, x_loaded.through(b))
                if later(b):
                    pe.wait_ge(gelu0.sem, gelu0.before(b))
                for c in range(CH):
                    if c > 0:
                        yield f"a.conv/{c}"
                    for j in range(NPAIR):
                        mm = pe.matmul(tm(1, PA)[:, c, :], XX[:, c * TP + 2 * j:c * TP + 2 * j + TP], w("conv", j),
                                       start=(j == 0), stop=(j == NPAIR - 1))
                mm.then_inc(conv_done.sem, 1)
                yield "a.turn1"
                pe.wait_ge(n1_ready.sem, n1_ready.through(b))
                if later(b):
                    pe.wait_ge(y0_out.sem, y0_out.before(b))
                for c in range(CH):
                    mm = pe.transpose(chunk(PA[:, 2, :], c), NA[:, c, :], identT)
                mm.then_inc(n1T_done.sem, 1)
                for j in range(4):
                    yield f"a.hid{j}"
                    if j == 0:
                        if not later(b):
                            pe.wait_ge(weights_split.sem, 2)
                            pe.wait_ge(loaded.sem, 16)
                        pe.wait_ge(xa_hi.sem, xa_hi.through(b))
                        pe.wait_ge(xa_lo.sem, xa_lo.through(b))
                        pe.wait_ge(tanh_done.sem, tanh_done.through(b))
                    if j >= 2:
                        pe.wait_ge(e1_out.sem, e1_out.at(b, j - 1))
                    mm3(PA[:, 2 * j % 3, 0:NT], ws("k1", j), (XHa[:, :], XLa[:, :])).then_inc(k1_mm.sem, 1)
                    yield f"a.hid{j}/e"
                    if j >= 1:
                        pe.wait_ge(k1_out.sem, k1_out.at(b, j))
                    mm3(PA[:, (2 * j + 1) % 3, 0:NT], ws("e1", j), (XHa[:, :], XLa[:, :])).then_inc(e1_mm.sem, 1)
                for i, name in ((1, "a.queries"), (0, "a.keys")):
                    yield name
                    pe.wait_ge(k1_out.sem, k1_out.through(b))
                    if i == 1:
                        pe.wait_ge(e1_out.sem, e1_out.at(b, 3))
                    for j in range(4):
                        if j > 0:
                            yield f"{name}/{j}"
                        mm = pe.matmul(PA[:, 2 * i, 0:NT], w("k2", 2 * j + i), K1[:, j, :],
                                       start=(j == 0), stop=(j == 3))
                    mm.then_inc(kq_mm.sem, 1)
                yield "a.emb"
                pe.wait_ge(e1_out.sem, e1_out.through(b))
                for c in range(CH):
                    if c > 0:
                        yield f"a.emb/{c}"
                    for j in range(4):
                        mm = pe.matmul(tm(1, PA)[:, c, :], chunk(E1t[:, j, :], c), w("e2", j),
                                       start=(j == 0), stop=(j == 3))
                mm.then_inc(emb_mm.sem, 1)
                yield "a.scores"
                pe.wait_ge(kq_hi.sem, kq_hi.through(b))
                pe.wait_ge(kq_lo.sem, kq_lo.through(b))
                for c in range(CH):
                    if c == 1:
                        pe.wait_ge(emb_out.sem, emb_out.through(b))
                    mm = mm3(PA[0:TP, c, 0:NT], (chunk(KQH[:, 1, :], c), chunk(KQL[:, 1, :], c)),
                             (KQH[:, 0, :], KQL[:, 0, :]))
                    mm.then_inc(s0_mm.sem, 1)
                yield "a.probsT"
                pe.wait_ge(exp0.sem, exp0.through(b))
                for k in range(CH):
                    for c in range(CH):
                        mm = pe.transpose(chunk(PA[0:keys(k), k, :], c), EX[:, c, k * TP:k * TP + keys(k)], identT)
                    mm.then_inc(exT_mm.sem, 1)
                yield "a.attend"
                pe.wait_ge(exT_out.sem, exT_out.through(b))
                pe.wait_ge(emb_out.sem, emb_out.through(b))
                for c in range(CH):
                    if c > 0:
                        yield f"a.attend/{c}"
                    for k in range(CH):
                        mm = pe.matmul(tm(0, PA)[:, c, :], chunk(EXT[0:keys(k), k, :], c), EMB[0:keys(k), k, :],
                                       start=(k == 0), stop=(k == CH - 1))
                mm.then_inc(av0_mm.sem, 1)
                yield "a.turn2"
                for i, t in enumerate((NA, NA2)):
                    pe.wait_ge(n2_ready.sem, n2_ready.at(b, i + 1))
                    for c in range(CH):
                        mm = pe.transpose(chunk(PA[:, 1 + i, :], c), t[:, c, :], identT)
                    mm.then_inc(n2T_done.sem, 1)
                yield "a.attn"
                pe.wait_ge(nt_out.sem, nt_out.through(b))
                pe.matmul(PA[:, 0, 0:NT], w("attn"), NTt[:, :], start=True, stop=True).then_inc(at_mm.sem, 1)
                for j in range(4):
                    yield f"a.fc1_{j}"
                    if j == 0:
                        pe.wait_ge(xa_out.sem, xa_out.through(b))
                        pe.wait_ge(f1_split.sem, f1_split.through(b))
                    if j == 3:
                        pe.wait_ge(gelu0.sem, gelu0.at(b, 1))
                    mm3(PA[:, (1 + j) % 3, 0:NT], (F1H[:, j * D:(j + 1) * D], F1L[:, j * D:(j + 1) * D]),
                        (XHa[:, :], XLa[:, :])).then_inc(fc1_mm.sem, 1)
                yield "a.fc2"
                for j in range(4):
                    if j > 0:
                        yield f"a.fc2/{j}"
                    pe.wait_ge(gelu0.sem, gelu0.at(b, max(j + 1, 2)))
                    mm = pe.matmul(PA[:, 2, 0:NT], FW[:, H0 + j * D:H0 + (j + 1) * D], G0[:, j, :],
                                   start=(j == 0), stop=(j == 3))
                mm.then_inc(fc2_mm.sem, 1)
                yield "a.last"
                pe.wait_ge(y0_out.sem, y0_out.through(b))
                for c in range(CH):
                    mm = pe.matmul(tm(0, PA)[:, c, :], chunk(Y0, c), w("next"), start=True, stop=True)
                mm.then_inc(next_mm.sem, 1)

            def pe_b(b):
                yield "b.turn1"
                pe.wait_ge(n3_ready.sem, n3_ready.at(b, 1))
                if later(b):
                    pe.wait_ge(cnT_out.sem, cnT_out.before(b))
                for c in range(CH):
                    mm = pe.transpose(chunk(PB[:, 0, :], c), NBt[:, c, :], identT)
                mm.then_inc(n3T_mm.sem, 1)
                for p in range(4):
                    yield f"b.qk{p}"
                    if p == 0:
                        pe.wait_ge(xb_hi.sem, xb_hi.through(b))
                        pe.wait_ge(xb_lo.sem, xb_lo.through(b))
                        if later(b):
                            pe.wait_ge(hb_ready.sem, hb_ready.before(b))
                    for i in (2 * p, 2 * p + 1):
                        if i % 2 == 1:
                            yield f"b.qk{p}/k"
                        if i >= 3:
                            pe.wait_ge(qk_full.sem, qk_full.at(b, i - 2))
                        mm3(PB[:, (1 + i) % 3, 0:NT], ws("qk", i), (XHb[:, :], XLb[:, :])).then_inc(qk_mm.sem, 1)
                yield "b.values"
                pe.wait_ge(qk_full.sem, qk_full.at(b, 6))
                for c in range(CH):
                    mm = pe.matmul(tm(0, PB)[:, c, :], chunk(XFb, c), w("v"), start=True, stop=True)
                mm.then_inc(v_mm.sem, 1)
                for s in range(12):
                    yield f"b.s{s}"
                    for u in (2 * s, 2 * s + 1):
                        if u % 2 == 1:
                            yield f"b.s{s}/1"
                        h, c = divmod(u, CH)
                        if u == 0:
                            pe.wait_ge(qk_full.sem, qk_full.through(b))
                        if u == 2:
                            pe.wait_ge(v_out.sem, v_out.through(b))
                        if u >= 3:
                            pe.wait_ge(s1_max.sem, s1_max.at(b, u - 2))
                        if c == 0 and h % 2 == 0:
                            pe.wait_ge(q_out.sem, q_out.at(b, h // 2 + 1))
                            pe.wait_ge(k_out.sem, k_out.at(b, h // 2 + 1))
                        pe.matmul(PB[0:TP, (1 + u) % 3, 0:NT], chunk(Q[:, h // 2, :], c), KZ[:, h, :],
                                  start=True, stop=True).then_inc(s1_mm.sem, 1)
                yield "b.maxT"
                pe.wait_ge(m_ready.sem, m_ready.through(b))
                for p in range(4):
                    if p == 3:
                        pe.wait_ge(q2_out.sem, q2_out.at(b, 1))
                    for c in range(CH):
                        mm = pe.transpose(chunk(PB[:, (1 + p) % 3, :], c),
                                          M[:, c, 2 * p:2 * p + 2, :].rearrange("p h d -> p (h d)"), identT)
                    mm.then_inc(mT_mm.sem, 1)

                def scores_t(h):
                    for k in range(CH):
                        if k > 0:
                            yield f"b.st{h}/{k}"
                        if h == 0:
                            pe.wait_ge(q2_out.sem, q2_out.at(b, k + 2))
                        elif h < 6:
                            pe.wait_ge(exp1.sem, exp1.at(b, CH * (h - 1) + k + 1))
                        elif h == 6 and k == 2:
                            pe.wait_ge(ct_out.sem, ct_out.at(b, 1))
                        elif h == 6:
                            pe.wait_ge(exp1.sem, exp1.at(b, CH * (h - 1) + k + 2))
                        else:
                            pe.wait_ge(exp1.sem, exp1.at(b, CH * (h - 1) + k + 1))
                        pe.matmul(PB[0:keys(k), ((2 if h < 6 else 0) + k) % 3, 0:NT], chunk(KZ[:, h, :], k, keys(k)),
                                  Q2[:, h // 2, :], start=True, stop=True).then_inc(st_mm.sem, 1)

                def attend(q):
                    if q == 0:
                        pe.wait_ge(exp1.sem, exp1.at(b, 16))
                    else:
                        pe.wait_ge(exp1.sem, exp1.through(b))
                    for k in range(CH):
                        if k > 0:
                            yield f"b.av{q}/{k}"
                        for j in range(4):
                            mm = pe.matmul(PB[32 * j:32 * j + 32, AV_BANK[q], 0:NT], V[0:keys(k), k, 4 * q + j, :],
                                           ET[0:keys(k), (4 * q + j) % ET_HEADS, k, :],
                                           start=(k == 0), stop=(k == CH - 1), skip_group_check=True)
                    mm.then_inc(av1_mm.sem, 1)

                for h in range(NH):
                    yield f"b.st{h}"
                    yield from scores_t(h)
                    if h == 5:
                        yield "b.av0"
                        yield from attend(0)
                yield "b.av1"
                yield from attend(1)
                yield "b.ctx"
                for q in range(2):
                    pe.wait_ge(ct_out.sem, ct_out.at(b, q + 1))
                    for c in range(CH):
                        mm = pe.transpose(tm(1 + q, PB)[:, c, :], chunk(CT[:, q, :], c), ident)
                    mm.then_inc(ctT_mm.sem, 1)
                yield "b.ctxT"
                pe.wait_ge(cn_ready.sem, cn_ready.through(b))
                for c in range(CH):
                    mm = pe.transpose(chunk(PB[:, 0, :], c), CN[:, c, :], identT)
                mm.then_inc(cnT_mm.sem, 1)
                yield "b.proj"
                pe.wait_ge(cnT_out.sem, cnT_out.through(b))
                for c in range(CH):
                    mm = pe.matmul(tm(1, PB)[:, c, :], chunk(CNT, c), w("out"), start=True, stop=True)
                mm.then_inc(out_mm.sem, 1)

            def pe_c(b):
                yield "c.turn2"
                pe.wait_ge(n3_ready.sem, n3_ready.at(b, 2))
                if later(b):
                    pe.wait_ge(w2_out.sem, w2_out.before(b))
                for c in range(CH):
                    mm = pe.transpose(chunk(PC[:, 0, :], c), NBt[:, c, :], identT)
                mm.then_inc(n3T_mm.sem, 1)
                yield "c.router"
                pe.wait_ge(xc_full.sem, xc_full.through(b))
                for c in range(CH):
                    mm = pe.matmul(tm(1, PC)[:, c, :], chunk(XFc, c), w("router"), start=True, stop=True)
                mm.then_inc(rt_mm.sem, 1)

                def w1(t, bank):
                    mm3(PC[:, bank, 0:NT], ws("w1", t), (XHc[:, :], XLc[:, :])).then_inc(w1_mm.sem, 1)

                yield "c.first"
                pe.wait_ge(xc_hi.sem, xc_hi.through(b))
                pe.wait_ge(xc_lo.sem, xc_lo.through(b))
                w1(0, 0)
                pe.wait_ge(rt_in.sem, rt_in.through(b))
                w1(1, 1)
                yield "c.combT"
                pe.wait_ge(cb_ready.sem, cb_ready.through(b))
                pe.wait_ge(gelu1.sem, gelu1.at(b, 1))
                for c in range(CH):
                    mm = pe.transpose(chunk(PC[:, 0, :], c), CB[:, c, :], identT)
                mm.then_inc(cbT_mm.sem, 1)
                yield "c.bias"
                pe.wait_ge(cbT_out.sem, cbT_out.through(b))
                pe.wait_ge(gelu1.sem, gelu1.at(b, 2))
                for c in range(CH):
                    mm = pe.matmul(tm(1, PC)[:, c, :], chunk(CBT, c), w("b2"), start=True, stop=True)
                mm.then_inc(b2_mm.sem, 1)
                for e in range(E1):
                    if e + 1 < E1:
                        yield f"c.p{e}"
                        if e > 0:
                            pe.wait_ge(w2_out.sem, w2_out.at(b, e + 1))
                        w1(2 * e + 2, e % 2)
                    yield f"c.e{e}"
                    pe.wait_ge(gelu1.sem, gelu1.at(b, 2 * e + 2))
                    if e == 0:
                        pe.wait_ge(w2_out.sem, w2_out.at(b, 1))
                    for c in range(CH):
                        if c > 0:
                            yield f"c.e{e}/{c}"
                        for j in range(2):
                            mm = pe.matmul(tm((e + 1) % 2, PC)[:, c, :], chunk(G1[:, (2 * e + j) % 4, :], c),
                                           w("w2", 2 * e + j), start=(j == 0), stop=(j == 1))
                    mm.then_inc(w2_mm.sem, 1)
                    if e + 1 < E1:
                        yield f"c.q{e}"
                        pe.wait_ge(gelu1.sem, gelu1.at(b, 2 * e + 3))
                        w1(2 * e + 3, e % 2)

            pe.wait_ge(first_loaded.sem, 48)
            run_streams(pe, ORDER["tensor"], pe_a, pe_b, pe_c)

        @block.scalar
        def _(s):
            def act_a(b):
                yield "a.tanh"
                s.wait_ge(conv_done.sem, conv_done.through(b))
                s.wait_ge(tok_scale.sem, tok_scale.through(b))
                if later(b):
                    s.wait_ge(n1_ready.sem, n1_ready.before(b))
                for c in range(CH):
                    a = s.activation(TOK[:, c, :], tm(1, PA)[:, c, :], ACT.Tanh, scale=smA[:, 4, c:c + 1])
                a.then_inc(tanh_done.sem, 1)
                yield "a.turn1"
                s.wait_ge(n1T_done.sem, n1T_done.through(b))
                s.activation(XHa[:, :], PA[:, 2, 0:NT], ACT.Copy).then_inc(xa_hi.sem, 1)
                for j in range(4):
                    yield f"a.hid{j}"
                    s.wait_ge(k1_mm.sem, k1_mm.at(b, j + 1))
                    s.activation(K1[:, j, :], PA[:, 2 * j % 3, 0:NT], ACT.Relu,
                                 bias=col("bk1", j)).then_inc(k1_out.sem, 1)
                    yield f"a.hid{j}/e"
                    s.wait_ge(e1_mm.sem, e1_mm.at(b, j + 1))
                    if j == 0:
                        s.wait_ge(wsq_done.sem, wsq_done.through(b))
                    s.activation(E1t[:, j, :], PA[:, (2 * j + 1) % 3, 0:NT], ACT.Relu,
                                 bias=col("be1", j)).then_inc(e1_out.sem, 1)
                for n, (i, name) in enumerate(((1, "a.queries"), (0, "a.keys"))):
                    yield name
                    s.wait_ge(kq_mm.sem, kq_mm.at(b, n + 1))
                    s.activation(KQH[:, i, :], PA[:, 2 * i, 0:NT], ACT.Identity,
                                 bias=col("bk2", i)).then_inc(kq_hi.sem, 1)
                yield "a.exp"
                s.wait_ge(max0.sem, max0.through(b))
                for c in range(CH):
                    s.activation(EX[:, c, 0:L], PA[0:TP, c, 0:L], ACT.Exp, bias=smA[:, 5, c:c + 1],
                                 accum_out=smA[:, 6 + c, 0:1]).then_inc(exp0.sem, 1)
                yield "a.probsT"
                s.wait_ge(exT_mm.sem, exT_mm.at(b, 1))
                s.activation(EXT[:, 0, :], PA[0:TP, 0, 0:NT], ACT.Copy).then_inc(exT_out.sem, 1)
                yield "a.probsT/2"
                s.wait_ge(exT_mm.sem, exT_mm.at(b, 3))
                s.activation(EXT[0:TLAST, 2, :], PA[0:TLAST, 2, 0:NT], ACT.Copy).then_inc(exT_out.sem, 1)
                yield "a.turn2"
                s.wait_ge(n2T_done.sem, n2T_done.at(b, 1))
                s.activation(XF[:, :], PA[:, 1, 0:NT], ACT.Copy).then_inc(xf_out.sem, 1)
                yield "a.turn2/1"
                s.wait_ge(n2T_done.sem, n2T_done.at(b, 2))
                s.activation(NTt[:, :], PA[:, 2, 0:NT], ACT.Identity, bias=col("ln_b"), scale=col("ln_g"))\
                    .then_inc(nt_out.sem, 1)
                for j in range(4):
                    yield f"a.fc1_{j}"
                    s.wait_ge(fc1_mm.sem, fc1_mm.at(b, j + 1))
                    s.activation(G0[:, j, :], PA[:, (1 + j) % 3, 0:NT], ACT.Gelu,
                                 bias=FW[:, 2 * H0 + j:2 * H0 + j + 1]).then_inc(gelu0.sem, 1)
                yield "a.gelu"
                s.wait_ge(next_in.sem, next_in.through(b))
                s.activation(NG[:, :, :], NX[:, :, :], ACT.Gelu).then_inc(gelu_n.sem, 1)

            def act_b(b):
                yield "b.turn1"
                s.wait_ge(n3T_mm.sem, n3T_mm.at(b, 1))
                s.activation(XHb[:, :], PB[:, 0, 0:NT], ACT.Copy).then_inc(xb_hi.sem, 1)
                s.activation(XFb[:, :], PB[:, 0, 0:NT], ACT.Copy).then_inc(xb_full.sem, 1)
                for p in range(4):
                    yield f"b.qk{p}"
                    if p >= 2:
                        s.wait_ge(q_out.sem, q_out.at(b, p - 1))
                        s.wait_ge(k_out.sem, k_out.at(b, p - 1))
                    elif later(b):
                        s.wait_ge(q_out.sem, q_out.before(b))
                        s.wait_ge(k_out.sem, k_out.before(b))
                    for i in (2 * p, 2 * p + 1):
                        if i % 2 == 1:
                            yield f"b.qk{p}/k"
                        s.wait_ge(qk_mm.sem, qk_mm.at(b, i + 1))
                        s.activation(QKF[:, i % 4, :], PB[:, (1 + i) % 3, 0:NT], ACT.Identity,
                                     bias=col("qkb", i)).then_inc(qk_full.sem, 1)

                def exps(h):
                    if h == ET_HEADS:
                        s.wait_ge(av1_mm.sem, av1_mm.at(b, 1))
                    elif h == 0 and later(b):
                        s.wait_ge(av1_mm.sem, av1_mm.before(b))
                    for k in range(CH):
                        if k > 0:
                            yield f"b.st{h}/{k}"
                        n = TP if k < CH - 1 else TLAST
                        s.wait_ge(st_mm.sem, st_mm.at(b, CH * h + k + 1))
                        s.activation(ET[0:n, h % ET_HEADS, k, :], PB[0:n, ((2 if h < 6 else 0) + k) % 3, 0:NT],
                                     ACT.Exp, scale=FACTOR).then_inc(exp1.sem, 1)

                def context(q):
                    s.wait_ge(av1_mm.sem, av1_mm.at(b, q + 1))
                    s.activation(CT[:, q, :], PB[:, AV_BANK[q], 0:NT], ACT.Copy).then_inc(ct_out.sem, 1)

                for h in range(NH):
                    yield f"b.st{h}"
                    yield from exps(h)
                    if h == 5:
                        yield "b.av0"
                        context(0)
                yield "b.av1"
                context(1)
                yield "b.ctxT"
                s.wait_ge(cnT_mm.sem, cnT_mm.through(b))
                s.activation(CNT, PB[:, 0, 0:NT], ACT.Copy).then_inc(cnT_out.sem, 1)

            def act_c(b):
                yield "c.turn2"
                s.wait_ge(n3T_mm.sem, n3T_mm.at(b, 2))
                s.activation(XFc[:, :], PC[:, 0, 0:NT], ACT.Copy).then_inc(xc_full.sem, 1)
                s.activation(XHc[:, :], PC[:, 0, 0:NT], ACT.Copy).then_inc(xc_hi.sem, 1)
                yield "c.top2"
                s.wait_ge(rt_in.sem, rt_in.through(b))
                s.activation(PRB[:, :, :], LG[:, :, :], ACT.Exp).then_inc(rt_exp.sem, 1)

                def gelu(t, bank):
                    s.wait_ge(w1_mm.sem, w1_mm.at(b, t + 1))
                    if t >= 4:
                        s.wait_ge(w2_mm.sem, w2_mm.at(b, t // 2 - 1))
                    s.activation(G1[:, t % 4, :], PC[:, bank, 0:NT], ACT.Gelu, bias=col("b1", t))\
                        .then_inc(gelu1.sem, 1)

                yield "c.first"
                gelu(0, 0)
                gelu(1, 1)
                for e in range(E1 - 1):
                    yield f"c.p{e}"
                    gelu(2 * e + 2, e % 2)
                    yield f"c.q{e}"
                    gelu(2 * e + 3, e % 2)

            s.wait_ge(first_loaded.sem, 48)
            run_streams(s, ORDER["scalar"], act_a, act_b, act_c)

        @block.vector
        def _(v):
            def pair(small, i):
                return small[:, i:i + 2, :].rearrange("p a c -> p (a c)")

            def rsqrt(y, x, small, at, link, step):
                yield step
                link.wait()
                n = x.shape[1]
                scratch = small[:, at:at + 4, :].rearrange("p a c -> p (a c)")
                half, t = scratch[:, 0:n], scratch[:, n:2 * n]
                v.tensor_scalar(half, x, -0.5, None, ALU.mult)
                link(v.tensor_scalar(t.bitcast(I32), x.bitcast(I32), 1, None, ALU.logical_shift_right))
                link.mark(v.tensor_tensor(y.bitcast(I32), MAGIC[0:TP, 0:n], t.bitcast(I32), ALU.subtract))
                for k in range(3):
                    yield f"{step}.{k}"
                    link.wait()
                    link(v.tensor_tensor(t, y, y, ALU.mult))
                    link(v.tensor_tensor(t, t, half, ALU.mult))
                    link.mark(v.scalar_tensor_tensor(out=y, in0=t, scalar=1.5, in1=y, op0=ALU.add, op1=ALU.mult))

            def norm_stats(h, st, mv, small, link):
                for c in range(CH):
                    last = v.bn_stats(st[:, c, :], h[:, c, :])
                link(last)
                v.tensor_tensor(small[:, 15, 0:1], small[:, 15, 2:3], small[:, 15, 2:3], ALU.add)
                for c in range(CH):
                    last = v.bn_aggr(mv[:, c, :], st[:, c, :])
                link(last)
                link.mark(v.tensor_scalar(small[:, 1, :], mv[:, :, 1], EPS_LN, None, ALU.add))

            def dve_a(b):
                link = Chain(v, dveA, b)
                yield "a.window"
                v.wait_ge(wsq_done.sem, wsq_done.through(b))
                if later(b):
                    v.wait_ge(tanh_done.sem, tanh_done.before(b))
                link.mark(v.tensor_scalar(smA[:, 1, :], tm(0, PA)[:, :, 0], 1e-30, None, ALU.max))
                yield from rsqrt(smA[:, 0, :], smA[:, 1, :], smA, 2, link, "a.root")
                yield "a.clamp"
                link.wait()
                link(v.tensor_tensor(smA[:, 0, :], smA[:, 0, :], smA[:, 1, :], ALU.mult))
                link(v.tensor_scalar(smA[:, 0, :], smA[:, 0, :], EPS_TOK, 1.0, ALU.add, ALU.max))
                link(v.reciprocal(smA[:, 1, :], smA[:, 0, :]))
                v.tensor_scalar(smA[:, 4, :], smA[:, 1, :], LAM_HALF, None, ALU.mult).then_inc(tok_scale.sem, 1)
                yield "a.norm1"
                v.wait_ge(tanh_done.sem, tanh_done.through(b))
                link(v.tensor_tensor(TOK[:, :, :], TOK[:, :, :], row3("tok_b"), ALU.add))
                link(v.tensor_scalar(HA[:, :, :], TOK[:, :, :], 0.0, None, ALU.max))
                norm_stats(HA, stA, mvA, smA, link)
                yield from rsqrt(smA[:, 0, :], smA[:, 1, :], smA, 2, link, "a.rstd1")
                yield "a.scale1"
                link.wait()
                for c in range(CH):
                    last = v.tensor_scalar(NA[:, c, :], HA[:, c, :], mvA[:, c, 0:1], smA[:, 0, c:c + 1],
                                           ALU.subtract, ALU.mult)
                last.then_inc(n1_ready.sem, 1)
                yield "a.turn1"
                if not later(b):
                    v.wait_ge(split_loaded.sem, 16)
                    v.tensor_copy(WH[:, :], WS).then_inc(weights_split.sem, 1)
                    v.wait_ge(weights_split.sem, 1)
                    v.tensor_tensor(WL[:, :], WS, WH[:, :], ALU.subtract).then_inc(weights_split.sem, 1)
                v.wait_ge(n1T_done.sem, n1T_done.through(b))
                v.wait_ge(xa_hi.sem, xa_hi.through(b))
                v.tensor_tensor(XLa[:, :], PA[:, 2, 0:NT], XHa[:, :], ALU.subtract).then_inc(xa_lo.sem, 1)
                for n, (i, name) in enumerate(((1, "a.queries"), (0, "a.keys"))):
                    yield name
                    v.wait_ge(kq_hi.sem, kq_hi.at(b, n + 1))
                    v.scalar_tensor_tensor(out=KQL[:, i, :], in0=PA[:, 2 * i, 0:NT], scalar=col("bk2", i),
                                           in1=KQH[:, i, :], op0=ALU.add, op1=ALU.subtract).then_inc(kq_lo.sem, 1)
                yield "a.emb"
                v.wait_ge(emb_mm.sem, emb_mm.through(b))
                v.tensor_tensor(EMB[:, :, :], tm(1, PA), row3("be2"), ALU.add).then_inc(emb_out.sem, 1)
                yield "a.scores"
                for c in range(CH):
                    if c > 0:
                        yield f"a.scores/{c}"
                    v.wait_ge(s0_mm.sem, s0_mm.at(b, c + 1))
                    last = v.tensor_reduce(smA[:, 1, c:c + 1], PA[0:TP, c, 0:L], AX.X, ALU.max)
                link(last)
                v.tensor_scalar(smA[:, 5, :], smA[:, 1, :], -1.0, None, ALU.mult).then_inc(max0.sem, 1)
                yield "a.probsT"
                v.wait_ge(exT_mm.sem, exT_mm.at(b, 2))
                v.tensor_copy(EXT[:, 1, :], PA[0:TP, 1, 0:NT]).then_inc(exT_out.sem, 1)
                yield "a.recip"
                v.wait_ge(exp0.sem, exp0.through(b))
                link.mark(v.reciprocal(smA[:, 9, :], smA[:, 6:9, 0:1].rearrange("p c o -> p (c o)")))
                yield "a.attend"
                v.wait_ge(av0_mm.sem, av0_mm.through(b))
                link.wait()
                for c in range(CH):
                    last = v.scalar_tensor_tensor(out=HA[:, c, :], in0=tm(0, PA)[:, c, :], scalar=smA[:, 9, c:c + 1],
                                                  in1=HA[:, c, :], op0=ALU.mult, op1=ALU.add)
                link.mark(last)
                yield "a.moments2"
                link.wait()
                norm_stats(HA, stA, mvA, smA, link)
                link.wait()
                link.mark(v.scalar_tensor_tensor(out=smA[:, 2, :], in0=smA[:, 1, :], scalar=EPS_LN, in1=mvA[:, :, 1],
                                            op0=ALU.mult, op1=ALU.add))
                yield from rsqrt(pair(smA, 10), pair(smA, 1), smA, 16, link, "a.rstd2")
                yield "a.scale2"
                link.wait()
                for c in range(CH):
                    last = v.tensor_scalar(NA[:, c, :], HA[:, c, :], mvA[:, c, 0:1], smA[:, 10, c:c + 1],
                                           ALU.subtract, ALU.mult)
                last.then_inc(n2_ready.sem, 1)
                yield "a.scale3"
                for c in range(CH):
                    last = v.tensor_scalar(NA2[:, c, :], HA[:, c, :], mvA[:, c, 0:1], smA[:, 11, c:c + 1],
                                           ALU.subtract, ALU.mult)
                last.then_inc(n2_ready.sem, 1)
                yield "a.attn"
                v.wait_ge(at_mm.sem, at_mm.through(b))
                v.wait_ge(xf_out.sem, xf_out.through(b))
                link(v.scalar_tensor_tensor(out=XA[:, :], in0=PA[:, 0, 0:NT], scalar=col("attn_b"), in1=XF[:, :],
                                            op0=ALU.add, op1=ALU.add))
                v.tensor_copy(XHa[:, :], XA[:, :]).then_inc(xa_out.sem, 1)
                v.wait_ge(xa_out.sem, xa_out.at(b, 1))
                v.tensor_tensor(XLa[:, :], XA[:, :], XHa[:, :], ALU.subtract).then_inc(xa_out.sem, 1)
                yield "a.fc2"
                v.wait_ge(fc2_mm.sem, fc2_mm.through(b))
                v.tensor_scalar(Y0[:, :], PA[:, 2, 0:NT], FW[:, 2 * H0 + 4:2 * H0 + 5], None, ALU.add)\
                    .then_inc(y0_out.sem, 1)
                yield "a.last"
                v.wait_ge(next_mm.sem, next_mm.through(b))
                v.tensor_tensor(NX[:, :, :], tm(0, PA), row3("next_b"), ALU.add).then_inc(next_in.sem, 1)
                yield "a.result"
                v.wait_ge(gelu_n.sem, gelu_n.through(b))
                if later(b):
                    v.wait_ge(hm_ready.sem, hm_ready.before(b))
                v.tensor_tensor(HN[:, :, :], HA[:, :, :], NG[:, :, :], ALU.add).then_inc(hn_ready.sem, 1)
                link.end()

            def dve_b(b):
                link = Chain(v, dveB, b)

                def normalise(h, n):
                    norm_stats(h, stB, mvB, smB, link)
                    yield from rsqrt(smB[:, 0, :], smB[:, 1, :], smB, 2, link, f"b.rstd{n}")
                    yield f"b.scale{n}"
                    link.wait()
                    for c in range(CH):
                        last = v.tensor_scalar(NBt[:, c, :], h[:, c, :], mvB[:, c, 0:1], smB[:, 0, c:c + 1],
                                               ALU.subtract, ALU.mult)
                    last.then_inc(n3_ready.sem, 1)

                yield "b.norm1"
                v.wait_ge(hn_ready.sem, hn_ready.through(b))
                if later(b):
                    v.wait_ge(n3T_mm.sem, n3T_mm.before(b))
                yield from normalise(HN, 1)
                yield "b.bias"
                v.tensor_tensor(HM[:, :, :], HN[:, :, :], row3("out_b"), ALU.add).then_inc(hm_ready.sem, 1)
                yield "b.turn1"
                v.wait_ge(xb_full.sem, xb_full.through(b))
                v.wait_ge(xb_hi.sem, xb_hi.through(b))
                v.tensor_tensor(XLb[:, :], PB[:, 0, 0:NT], XHb[:, :], ALU.subtract).then_inc(xb_lo.sem, 1)
                for p in range(4):
                    yield f"b.qk{p}"
                    v.wait_ge(qk_round.sem, qk_round.at(b, 2 * p + 1))
                    for i in range(2):
                        r = slice(64 * i, 64 * i + 64)
                        last = v.scalar_tensor_tensor(out=KZ[r, 2 * p + i, :], in0=QKR[r, 2 * (p % 2) + 1, :],
                                                      scalar=col("kneg")[r, :], in1=QKF[r, 2 * (p % 2) + 1, :],
                                                      op0=ALU.mult, op1=ALU.add)
                    last.then_inc(k_out.sem, 1)
                yield "b.values"
                v.wait_ge(v_mm.sem, v_mm.through(b))
                v.tensor_tensor(V[:, :, :, 0:HD], tm(0, PB).rearrange("p c (h d) -> p c h d", h=NH),
                                row3("vb").rearrange("p c (h d) -> p c h d", h=NH), ALU.add).then_inc(v_out.sem, 1)
                for step in range(12):
                    yield f"b.s{step}"
                    for u in (2 * step, 2 * step + 1):
                        if u % 2 == 1:
                            yield f"b.s{step}/1"
                        v.wait_ge(s1_mm.sem, s1_mm.at(b, u + 1))
                        v.tensor_reduce(MX[:, u // CH, u % CH:u % CH + 1], PB[0:TP, (1 + u) % 3, 0:L], AX.X, ALU.max)\
                            .then_inc(s1_max.sem, 1)
                yield "b.maxT"
                v.wait_ge(s1_max.sem, s1_max.through(b))
                v.tensor_scalar(M[:, :, :, 0], MX[:, :, :].rearrange("p h c -> p c h"), -1.0, None, ALU.mult)\
                    .then_inc(m_ready.sem, 1)
                for p in range(4):
                    yield f"b.maxT/{p}"
                    v.wait_ge(mT_mm.sem, mT_mm.at(b, p + 1))
                    v.tensor_tensor(Q2[:, p, :], PB[:, (1 + p) % 3, 0:NT], Q[:, p, :], ALU.add).then_inc(q2_out.sem, 1)
                yield "b.ctx"
                v.wait_ge(ctT_mm.sem, ctT_mm.through(b))
                ct = [tm(1 + q, PB).rearrange("p c (h d) -> p c h d", h=4) for q in range(2)]
                for q in range(2):
                    last = v.reciprocal(RD[:, :, 4 * q:4 * q + 4], ct[q][:, :, :, HD])
                link(last)
                for q in range(2):
                    last = v.tensor_tensor(
                        CN[:, :, 64 * q:64 * q + 64].rearrange("p c (h d) -> p c h d", h=4), ct[q][:, :, :, 0:HD],
                        RD[:, :, 4 * q:4 * q + 4].unsqueeze(3).to_broadcast([TP, CH, 4, HD]), ALU.mult)
                last.then_inc(cn_ready.sem, 1)
                yield "b.proj"
                v.wait_ge(out_mm.sem, out_mm.through(b))
                v.wait_ge(hm_ready.sem, hm_ready.through(b))
                v.tensor_tensor(HB[:, :, :], tm(1, PB), HM[:, :, :], ALU.add).then_inc(hb_ready.sem, 1)
                yield "b.norm2"
                v.wait_ge(hb_ready.sem, hb_ready.through(b))
                yield from normalise(HB, 2)
                link.end()

            def dve_c(b):
                link = Chain(v, dveC, b)
                yield "c.router"
                v.wait_ge(rt_mm.sem, rt_mm.through(b))
                link(v.tensor_tensor(LG[:, :, :], tm(1, PC)[:, :, 0:E1], row3("br"), ALU.add))
                link(v.tensor_reduce(smB[:, 5, :], LG[:, :, :], AX.X, ALU.max))
                v.tensor_tensor(LG[:, :, :], LG[:, :, :], smB[:, 5, :].unsqueeze(2).to_broadcast([TP, CH, E1]),
                                ALU.subtract).then_inc(rt_in.sem, 1)
                yield "c.x_low"
                v.wait_ge(xc_full.sem, xc_full.through(b))
                v.wait_ge(xc_hi.sem, xc_hi.through(b))
                v.tensor_tensor(XLc[:, :], PC[:, 0, 0:NT], XHc[:, :], ALU.subtract).then_inc(xc_lo.sem, 1)
                yield "c.top2"
                v.wait_ge(rt_exp.sem, rt_exp.through(b))
                link(v.tensor_reduce(smB[:, 6, :], PRB[:, :, :], AX.X, ALU.add))
                link(v.reciprocal(smB[:, 7, :], smB[:, 6, :]))
                link.mark(v.tensor_tensor(PRB[:, :, :], PRB[:, :, :],
                                     smB[:, 7, :].unsqueeze(2).to_broadcast([TP, CH, E1]), ALU.mult))
                mine = PRB[:, :, :].unsqueeze(3).to_broadcast([TP, CH, E1, E1])
                theirs = PRB[:, :, :].unsqueeze(2).to_broadcast([TP, CH, E1, E1])
                before = row("before").rearrange("p (e j) -> p e j", e=E1).unsqueeze(1)\
                    .to_broadcast([TP, CH, E1, E1])
                yield "c.rank"
                link.wait()
                v.tensor_tensor(BEAT[:, :, :, :], theirs, mine, ALU.is_gt)
                link(v.tensor_tensor(TIE[:, :, :, :], theirs, mine, ALU.is_equal))
                link(v.tensor_tensor(TIE[:, :, :, :], TIE[:, :, :, :], before, ALU.mult))
                link(v.tensor_tensor(BEAT[:, :, :, :], BEAT[:, :, :, :], TIE[:, :, :, :], ALU.add))
                link(v.tensor_reduce(CNTB[:, :, :], BEAT[:, :, :, :], AX.X, ALU.add))
                v.scalar_tensor_tensor(out=CB[:, :, 0:E1], in0=CNTB[:, :, :], scalar=1.5, in1=PRB[:, :, :],
                                       op0=ALU.is_lt, op1=ALU.mult).then_inc(cb_ready.sem, 1)
                yield "c.combT"
                v.wait_ge(cbT_mm.sem, cbT_mm.through(b))
                v.tensor_copy(CBT, PC[:, 0, 0:NT]).then_inc(cbT_out.sem, 1)
                yield "c.bias"
                v.wait_ge(b2_mm.sem, b2_mm.through(b))
                if later(b):
                    v.wait_ge(stored.sem, stored.before(b))
                v.tensor_tensor(HC[:, :, :], tm(1, PC), HB[:, :, :], ALU.add).then_inc(w2_out.sem, 1)
                for e in range(E1):
                    yield f"c.e{e}"
                    v.wait_ge(w2_mm.sem, w2_mm.at(b, e + 1))
                    v.wait_ge(w2_out.sem, w2_out.at(b, e + 1))
                    for c in range(CH):
                        last = v.scalar_tensor_tensor(out=HC[:, c, :], in0=tm((e + 1) % 2, PC)[:, c, :],
                                                      scalar=CB[:, c, e:e + 1], in1=HC[:, c, :],
                                                      op0=ALU.mult, op1=ALU.add)
                    last.then_inc(w2_out.sem, 1)
                link.end()

            v.wait_ge(first_loaded.sem, 48)
            v.wait_ge(zeros_set.sem, 2)
            v.memset(smA[:, 15, :], 0.0)
            v.memset(smB[:, 15, :], 0.0)
            run_streams(v, ORDER["vector"], dve_a, dve_b, dve_c)


_INS = ["x", "weights", "split_w", "cols", "rows", "ffw"]


def lay_out(i):
    f = np.float32
    a = {k: np.asarray(v) for k, v in i.items()}

    def blocks(m):
        n = m.shape[0] // 128
        return m.reshape(n, 128, -1).transpose(1, 0, 2).reshape(128, -1)

    def wide(m):
        o = np.zeros((m.shape[0], 128), f)
        o[:, :m.shape[1]] = m
        return o

    x = np.zeros((NB, CIN, XPAD), f)
    x[:, :, :L_IN] = a["x"].transpose(0, 2, 1)
    conv = np.zeros((TAPS + 1, CIN, D), f)
    conv[:TAPS] = a["L0_tok_kernel"]
    b2 = np.zeros((128, D), f)
    b2[:E1] = a["L1_ffn_b2"]
    qkv = a["L1_attn_qkv_w"].reshape(NH, 3, HD, D)
    qkv_b = a["L1_attn_qkv_b"].reshape(NH, 3, HD)
    parts = {
        "conv": blocks(conv.reshape(-1, D)),
        "k2": blocks(a["L0_attn_Wk2"].T), "e2": blocks(a["L0_attn_We2"].T),
        "attn": a["L0_ffn_attn_w"].T, "next": a["L0_ffn_next_w"].T,
        "v": qkv[:, 2].reshape(NH * HD, D).T, "out": a["L1_attn_out_w"].T,
        "router": wide(a["L1_ffn_Wr"].T), "b2": b2,
        "w2": blocks(a["L1_ffn_W2"].reshape(E1 * H1, D)),
        "ident": np.eye(128, dtype=f), "ones": np.ones((128, 128), f),
    }
    qk = np.zeros((D, 4, 2, 2, 4, HD), f)
    qkb = np.zeros((4, 2, 2, 4, HD), f)
    for h in range(NH):
        for s in range(2):
            for blk in range(1, 4):
                qk[:, h // 2, s, h % 2, blk] = qkv[h, s].T
                qkb[h // 2, s, h % 2, blk] = qkv_b[h, s]
    qkb[:, 1, :, 0, 0] = 1.0
    neg = np.zeros((2, 2, 4, HD), f)
    neg[0, :, 3], neg[1, :, 2] = -1.0, -1.0
    split = {"k1": a["L0_attn_Wk1"].T, "e1": a["L0_attn_We1"].T, "qk": qk.reshape(D, -1),
             "w1": a["L1_ffn_W1"].transpose(1, 0, 2).reshape(D, -1)}
    cols = {"bk1": a["L0_attn_bk1"].reshape(4, 128).T, "be1": a["L0_attn_be1"].reshape(4, 128).T,
            "bk2": a["L0_attn_bk2"].reshape(2, 128).T, "ln_g": a["L0_ffn_ln_g"][:, None],
            "ln_b": a["L0_ffn_ln_b"][:, None], "attn_b": a["L0_ffn_attn_b"][:, None],
            "qkb": qkb.reshape(8, 128).T, "b1": a["L1_ffn_b1"].reshape(16, 128).T,
            "qneg": neg[0].reshape(128, 1), "kneg": neg[1].reshape(128, 1)}
    before = np.tril(np.ones((E1, E1), f), -1)
    rows = {"tok_b": a["L0_tok_bias"], "be2": a["L0_attn_be2"], "next_b": a["L0_ffn_next_b"],
            "vb": qkv_b[:, 2].reshape(-1), "out_b": a["L1_attn_out_b"], "br": a["L1_ffn_br"],
            "before": before.reshape(-1)}
    ffw = np.zeros((E0, 128, FFW), f)
    ffw[:, :, 0:H0] = a["L0_ffn_fc1_w"].transpose(0, 2, 1)
    ffw[:, :, H0:2 * H0] = a["L0_ffn_fc2_w"].transpose(0, 2, 1).reshape(E0, 4, 128, D).transpose(0, 2, 1, 3)\
        .reshape(E0, 128, 4 * D)
    ffw[:, :, 2 * H0:2 * H0 + 4] = a["L0_ffn_fc1_b"].reshape(E0, 4, 128).transpose(0, 2, 1)
    ffw[:, :, 2 * H0 + 4] = a["L0_ffn_fc2_b"]
    row = np.concatenate([rows[n] for n, _ in ROWS])
    return {
        "x": x, "ffw": ffw,
        "weights": np.concatenate([parts[n] for n, _ in WEIGHTS], 1),
        "split_w": np.concatenate([split[n] for n, _ in SPLIT], 1),
        "cols": np.concatenate([cols[n] for n, _ in COLS], 1),
        "rows": np.ascontiguousarray(np.broadcast_to(row, (128, R_N))),
    }


def kernel(**inputs):
    import concourse.bacc as bacc
    from concourse.bass_utils import run_bass_kernel_spmd

    nc = bacc.Bacc("TRN2", target_bir_lowering=False, num_devices=1)
    arrays, args = {}, []
    for name, value in lay_out(inputs).items():
        value = np.ascontiguousarray(value)
        arrays[f"in_{name}"] = value
    for name in _INS:
        value = arrays[f"in_{name}"]
        args.append(nc.dram_tensor(f"in_{name}", value.shape, mybir.dt.from_np(value.dtype), kind="ExternalInput").ap())
    out = nc.dram_tensor("out_0", (NB, L, D), F32, kind="ExternalOutput").ap()
    tower_kernel(nc, *args, out)
    r = run_bass_kernel_spmd(nc, [arrays], core_ids=[0])
    return r.results[0]["out_0"]
```
